# Optimizing a Trainium2 kernel written in Bass

```python
import numpy as np
import jax
import jax.numpy as jnp

def _softmax(x, axis=-1):
    return jax.nn.softmax(x, axis=axis)

def _gelu(x):
    return jax.nn.gelu(x, approximate=True)

def _silu(x):
    return jax.nn.silu(x)

def _sigmoid(x):
    return jax.nn.sigmoid(x)

def _layernorm(x, axis=-1, eps=1e-05):
    m = jnp.mean(x, axis=axis, keepdims=True)
    v = jnp.var(x, axis=axis, keepdims=True)
    return (x - m) / jnp.sqrt(v + eps)

def _scatter_add(tgt, idx, src, axis=0):
    return tgt.at[idx].add(src)

def _segment_sum(src, seg, n):
    return jax.ops.segment_sum(src, seg, n)
kernel_name = 'mk_seq_preln_d1_jaxref_r8_6539bb'

def setup_inputs(seed: int=0):
    np.random.seed(seed)
    _w = jnp.asarray

    def _L0_attn_setup():
        import jax, jax.numpy as jnp
        import numpy as np
        D_MODEL = 128
        H = 32
        P = 64
        N = 64
        G = 8
        K = 4
        D_INNER = H * P
        CONV_DIM = D_INNER + 2 * G * N
        D_PROJ = 2 * D_INNER + 2 * G * N + H
        GROUP_SIZE = D_INNER // G
        EPS = 1e-05

        def _rmsnorm(x, w):
            var = jnp.mean(jnp.square(x), axis=-1, keepdims=True)
            return x * jax.lax.rsqrt(var + EPS) * w

        def _silu(x):
            return x * jax.nn.sigmoid(x)

        def _mamba_layer(hidden_states, norm_w, in_proj_w, conv_w, conv_b, dt_bias, A_log, D, gate_norm_w, out_proj_w):
            B_, S, _ = hidden_states.shape
            residual = hidden_states
            x = _rmsnorm(hidden_states, norm_w)
            proj = jnp.einsum('bsd,de->bse', x, in_proj_w)
            z = proj[..., :D_INNER]
            xBC = proj[..., D_INNER:D_INNER + CONV_DIM]
            dt_raw = proj[..., D_INNER + CONV_DIM:]
            xc = jnp.swapaxes(xBC, 1, 2)
            xc = jnp.pad(xc, ((0, 0), (0, 0), (K - 1, 0)))
            xc = jax.lax.conv_general_dilated(xc, conv_w[:, None, :], window_strides=(1,), padding='VALID', dimension_numbers=('NCH', 'OIH', 'NCH'), feature_group_count=CONV_DIM)
            xc = xc + conv_b[None, :, None]
            xBC = _silu(jnp.swapaxes(xc, 1, 2))
            xs = xBC[..., :D_INNER].reshape(B_, S, H, P)
            Bg = xBC[..., D_INNER:D_INNER + G * N].reshape(B_, S, G, N)
            Cg = xBC[..., D_INNER + G * N:].reshape(B_, S, G, N)
            Bh = jnp.repeat(Bg, H // G, axis=2)
            Ch = jnp.repeat(Cg, H // G, axis=2)
            dt = jax.nn.softplus(dt_raw + dt_bias)
            A = -jnp.exp(A_log)
            dA = jnp.exp(dt * A)

            def step(h, inp):
                x_t, B_t, C_t, dA_t, dt_t = inp
                h = dA_t[..., None, None] * h + (dt_t[..., None] * x_t)[..., None] * B_t[:, :, None, :]
                y_t = jnp.einsum('bhpn,bhn->bhp', h, C_t)
                return (h, y_t)
            h0 = jnp.zeros((B_, H, P, N), hidden_states.dtype)
            tm = lambda a: jnp.swapaxes(a, 0, 1)
            _, y = jax.lax.scan(step, h0, (tm(xs), tm(Bh), tm(Ch), tm(dA), tm(dt)))
            y = jnp.swapaxes(y, 0, 1)
            y = y + D[None, None, :, None] * xs
            y = y.reshape(B_, S, D_INNER)
            g = y * _silu(z)
            gg = g.reshape(B_, S, G, GROUP_SIZE)
            var = jnp.mean(jnp.square(gg), axis=-1, keepdims=True)
            g = (gg * jax.lax.rsqrt(var + EPS)).reshape(B_, S, D_INNER) * gate_norm_w
            out = jnp.einsum('bsd,de->bse', g, out_proj_w)
            return residual + out
        key = jax.random.key(seed)
        ks = jax.random.split(key, 6)
        B_, S = (1, 256)
        sc = lambda k, shape, s=0.02: jax.random.normal(k, shape, jnp.float32) * s
        return {'hidden_states': jax.random.normal(ks[0], (B_, S, D_MODEL), jnp.float32), 'norm_w': jnp.ones((D_MODEL,), jnp.float32), 'in_proj_w': sc(ks[1], (D_MODEL, D_PROJ)), 'conv_w': sc(ks[2], (CONV_DIM, K), 0.1), 'conv_b': jnp.zeros((CONV_DIM,), jnp.float32), 'dt_bias': sc(ks[3], (H,), 0.5), 'A_log': jnp.log(jnp.arange(1, H + 1, dtype=jnp.float32)), 'D': jnp.ones((H,), jnp.float32), 'gate_norm_w': jnp.ones((D_INNER,), jnp.float32), 'out_proj_w': sc(ks[4], (D_INNER, D_MODEL))}
    _L0_attn_in = _L0_attn_setup()

    def _L0_ffn_setup():
        import jax, jax.numpy as jnp
        import numpy as np
        LN_EPS = 1e-05

        def layer_norm(x, g, b):
            mu = jnp.mean(x, axis=-1, keepdims=True)
            var = jnp.mean(jnp.square(x - mu), axis=-1, keepdims=True)
            return (x - mu) * jax.lax.rsqrt(var + LN_EPS) * g + b

        def ternary_quant(w):
            scale = 1.0 / jnp.clip(jnp.mean(jnp.abs(w)), 1e-05)
            wq = jnp.clip(jnp.round(w * scale), -1.0, 1.0) / scale
            return w + jax.lax.stop_gradient(wq - w)
        key = jax.random.key(seed)
        ks = jax.random.split(key, 3)
        dim, hidden = (128, 512)
        B, S = (8, 128)
        x = jax.random.normal(ks[0], (B, S, dim), dtype=jnp.float32)
        w1 = jax.random.normal(ks[1], (hidden, dim), dtype=jnp.float32) * 0.02
        w2 = jax.random.normal(ks[2], (dim, hidden), dtype=jnp.float32) * 0.02
        return {'x': x, 'ln1_g': jnp.ones((dim,), jnp.float32), 'ln1_b': jnp.zeros((dim,), jnp.float32), 'w1': w1, 'b1': jnp.zeros((hidden,), jnp.float32), 'ln2_g': jnp.ones((hidden,), jnp.float32), 'ln2_b': jnp.zeros((hidden,), jnp.float32), 'w2': w2, 'b2': jnp.zeros((dim,), jnp.float32)}
    _L0_ffn_in = _L0_ffn_setup()
    _d = {'L0_attn_hidden_states': _L0_attn_in['hidden_states'], 'L0_attn_norm_w': _L0_attn_in['norm_w'], 'L0_attn_in_proj_w': _L0_attn_in['in_proj_w'], 'L0_attn_conv_w': _L0_attn_in['conv_w'], 'L0_attn_conv_b': _L0_attn_in['conv_b'], 'L0_attn_dt_bias': _L0_attn_in['dt_bias'], 'L0_attn_A_log': _L0_attn_in['A_log'], 'L0_attn_D': _L0_attn_in['D'], 'L0_attn_gate_norm_w': _L0_attn_in['gate_norm_w'], 'L0_attn_out_proj_w': _L0_attn_in['out_proj_w'], 'L0_ffn_ln1_g': _L0_ffn_in['ln1_g'], 'L0_ffn_ln1_b': _L0_ffn_in['ln1_b'], 'L0_ffn_w1': _L0_ffn_in['w1'], 'L0_ffn_b1': _L0_ffn_in['b1'], 'L0_ffn_ln2_g': _L0_ffn_in['ln2_g'], 'L0_ffn_ln2_b': _L0_ffn_in['ln2_b'], 'L0_ffn_w2': _L0_ffn_in['w2'], 'L0_ffn_b2': _L0_ffn_in['b2']}
    _x0 = _d['L0_attn_hidden_states']
    _d['L0_attn_hidden_states'] = jax.random.normal(jax.random.fold_in(jax.random.key(seed), 1), (8, 512, 128), dtype=_x0.dtype)
    del _x0
    return _d

def reference(L0_attn_hidden_states, L0_attn_norm_w, L0_attn_in_proj_w, L0_attn_conv_w, L0_attn_conv_b, L0_attn_dt_bias, L0_attn_A_log, L0_attn_D, L0_attn_gate_norm_w, L0_attn_out_proj_w, L0_ffn_ln1_g, L0_ffn_ln1_b, L0_ffn_w1, L0_ffn_b1, L0_ffn_ln2_g, L0_ffn_ln2_b, L0_ffn_w2, L0_ffn_b2):

    def _L0_attn_ref(hidden_states, norm_w, in_proj_w, conv_w, conv_b, dt_bias, A_log, D, gate_norm_w, out_proj_w):
        import jax, jax.numpy as jnp
        import numpy as np
        D_MODEL = 128
        H = 32
        P = 64
        N = 64
        G = 8
        K = 4
        D_INNER = H * P
        CONV_DIM = D_INNER + 2 * G * N
        D_PROJ = 2 * D_INNER + 2 * G * N + H
        GROUP_SIZE = D_INNER // G
        EPS = 1e-05

        def _rmsnorm(x, w):
            var = jnp.mean(jnp.square(x), axis=-1, keepdims=True)
            return x * jax.lax.rsqrt(var + EPS) * w

        def _silu(x):
            return x * jax.nn.sigmoid(x)

        def _mamba_layer(hidden_states, norm_w, in_proj_w, conv_w, conv_b, dt_bias, A_log, D, gate_norm_w, out_proj_w):
            B_, S, _ = hidden_states.shape
            residual = hidden_states
            x = _rmsnorm(hidden_states, norm_w)
            proj = jnp.einsum('bsd,de->bse', x, in_proj_w)
            z = proj[..., :D_INNER]
            xBC = proj[..., D_INNER:D_INNER + CONV_DIM]
            dt_raw = proj[..., D_INNER + CONV_DIM:]
            xc = jnp.swapaxes(xBC, 1, 2)
            xc = jnp.pad(xc, ((0, 0), (0, 0), (K - 1, 0)))
            xc = jax.lax.conv_general_dilated(xc, conv_w[:, None, :], window_strides=(1,), padding='VALID', dimension_numbers=('NCH', 'OIH', 'NCH'), feature_group_count=CONV_DIM)
            xc = xc + conv_b[None, :, None]
            xBC = _silu(jnp.swapaxes(xc, 1, 2))
            xs = xBC[..., :D_INNER].reshape(B_, S, H, P)
            Bg = xBC[..., D_INNER:D_INNER + G * N].reshape(B_, S, G, N)
            Cg = xBC[..., D_INNER + G * N:].reshape(B_, S, G, N)
            Bh = jnp.repeat(Bg, H // G, axis=2)
            Ch = jnp.repeat(Cg, H // G, axis=2)
            dt = jax.nn.softplus(dt_raw + dt_bias)
            A = -jnp.exp(A_log)
            dA = jnp.exp(dt * A)

            def step(h, inp):
                x_t, B_t, C_t, dA_t, dt_t = inp
                h = dA_t[..., None, None] * h + (dt_t[..., None] * x_t)[..., None] * B_t[:, :, None, :]
                y_t = jnp.einsum('bhpn,bhn->bhp', h, C_t)
                return (h, y_t)
            h0 = jnp.zeros((B_, H, P, N), hidden_states.dtype)
            tm = lambda a: jnp.swapaxes(a, 0, 1)
            _, y = jax.lax.scan(step, h0, (tm(xs), tm(Bh), tm(Ch), tm(dA), tm(dt)))
            y = jnp.swapaxes(y, 0, 1)
            y = y + D[None, None, :, None] * xs
            y = y.reshape(B_, S, D_INNER)
            g = y * _silu(z)
            gg = g.reshape(B_, S, G, GROUP_SIZE)
            var = jnp.mean(jnp.square(gg), axis=-1, keepdims=True)
            g = (gg * jax.lax.rsqrt(var + EPS)).reshape(B_, S, D_INNER) * gate_norm_w
            out = jnp.einsum('bsd,de->bse', g, out_proj_w)
            return residual + out
        return _mamba_layer(hidden_states, norm_w, in_proj_w, conv_w, conv_b, dt_bias, A_log, D, gate_norm_w, out_proj_w)

    def _L0_ffn_ref(x, ln1_g, ln1_b, w1, b1, ln2_g, ln2_b, w2, b2):
        import jax, jax.numpy as jnp
        import numpy as np
        LN_EPS = 1e-05

        def layer_norm(x, g, b):
            mu = jnp.mean(x, axis=-1, keepdims=True)
            var = jnp.mean(jnp.square(x - mu), axis=-1, keepdims=True)
            return (x - mu) * jax.lax.rsqrt(var + LN_EPS) * g + b

        def ternary_quant(w):
            scale = 1.0 / jnp.clip(jnp.mean(jnp.abs(w)), 1e-05)
            wq = jnp.clip(jnp.round(w * scale), -1.0, 1.0) / scale
            return w + jax.lax.stop_gradient(wq - w)
        h = layer_norm(x, ln1_g, ln1_b)
        h = jnp.einsum('bsd,hd->bsh', h, ternary_quant(w1)) + b1
        h = jax.nn.gelu(h, approximate=False)
        h = layer_norm(h, ln2_g, ln2_b)
        out = jnp.einsum('bsh,dh->bsd', h, ternary_quant(w2)) + b2
        return out
    x = L0_attn_hidden_states
    x = x + _L0_attn_ref(_layernorm(x, axis=-1), L0_attn_norm_w, L0_attn_in_proj_w, L0_attn_conv_w, L0_attn_conv_b, L0_attn_dt_bias, L0_attn_A_log, L0_attn_D, L0_attn_gate_norm_w, L0_attn_out_proj_w)
    x = x + _L0_ffn_ref(_layernorm(x, axis=-1), L0_ffn_ln1_g, L0_ffn_ln1_b, L0_ffn_w1, L0_ffn_b1, L0_ffn_ln2_g, L0_ffn_ln2_b, L0_ffn_w2, L0_ffn_b2)
    return x

_drawn_inputs = setup_inputs


def setup_inputs(seed=0):
    import zlib

    import numpy as np

    out = dict(_drawn_inputs(seed))
    spreads = {'L0_attn_norm_w': (1.0, 0.2),
     'L0_attn_conv_b': (0.0, 0.1),
     'L0_attn_D': (1.0, 0.2),
     'L0_attn_gate_norm_w': (1.0, 0.2),
     'L0_ffn_ln1_g': (1.0, 0.6),
     'L0_ffn_ln1_b': (0.0, 0.647),
     'L0_ffn_b1': (0.0, 0.1),
     'L0_ffn_ln2_g': (1.0, 0.563),
     'L0_ffn_ln2_b': (0.0, 0.606),
     'L0_ffn_b2': (0.0, 0.1)}
    factors = {'L0_attn_dt_bias': 28.228, 'L0_attn_A_log': 64.0}
    for name, (base, spread) in spreads.items():
        noise = np.random.default_rng([zlib.crc32(name.encode()), seed]).standard_normal(out[name].shape)
        drawn = base * np.exp(spread * noise) if base else spread * noise
        out[name] = jnp.asarray(drawn.astype(out[name].dtype))
    for name, factor in factors.items():
        out[name] = (out[name] * factor).astype(out[name].dtype)
    return out
```

```python
from contextlib import ExitStack

import concourse.bass as bass
from concourse import mybir

F32 = mybir.dt.float32
F32R = mybir.dt.float32r
BF16 = mybir.dt.bfloat16
ALU = mybir.AluOpType
ACT = mybir.ActivationFunctionType
AX_X = mybir.AxisListType.X

P = 128
NB, S, DM = 8, 512, 128
H, HP, G, NS, KW = 32, 64, 8, 64, 4
DI = H * HP
CH = S // P
NCH = NB * CH
UNITS, R = G // 2, 4
SLOTS = UNITS * R
TILES = 10
CONVS = 6
HID = 512
HT = HID // P
EPS = 1e-5
Z0, X0, B0, C0, DT0 = 0, DI, 2 * DI, 2 * DI + G * NS, 2 * DI + 2 * G * NS
DPROJ = DT0 + H

PLAN = [[2, 3], [0, 1], [4], [5]]
CONV_ORDER = [(q, t) for q in range(UNITS) for r in range(R) for t in PLAN[r]]
NCONV = len(CONV_ORDER)


def tap_numbers():
    found, n = {}, 0
    for q in range(UNITS):
        for r in range(R):
            for shift in range(1, KW):
                for t in PLAN[r]:
                    found[q, t, shift] = n
                    n += 1
    return found


TAP = tap_numbers()
NTAP = len(TAP)

LAG_SSD, LAG_M, LAG_STATE, LAG_Y, LAG_SUM, LAG_VAR, LAG_FACTOR, LAG_NORM, LAG_OUT = 4, 5, 6, 7, 8, 12, 13, 14, 15
XN_SLOT = 8
XO_SLOT = LAG_OUT


def back(b, n, lag):
    m = n - lag
    while m < 0:
        b, m = b - 1, m + SLOTS
    if isinstance(b, int) and not 0 <= b < NB:
        return None
    return b, m


def following(b):
    return None if isinstance(b, int) and b + 1 >= NB else b + 1


def misc_plan():
    plan = []
    for q in range(UNITS):
        for r in range(R):
            n = 4 * q + r
            plan.append((n, "xt", LAG_SSD, 0))
            plan.append((n, "s", LAG_STATE, 0))
            if r == 0:
                plan.append((n, "var", LAG_VAR, 0))
            if r == 1:
                plan.append((n, "bt", LAG_M, 0))
                plan += [(n, "cb", LAG_M, 0), (n, "cb", LAG_M, 1)]
                plan.append((n, "rbc", LAG_FACTOR, 0))
            if n == XO_SLOT:
                plan.append((n, "xo", SLOTS, 0))
            if n == XN_SLOT:
                plan.append((n, "xn", 0, 0))
    return plan


MISC = misc_plan()
PROJ = [(4 * q + r, t) for q in range(UNITS) for r in range(R) for t in PLAN[r] + ["z"]]
assert len(PROJ) % 2 == 0


def proj_position(n, t):
    return PROJ.index((n, t))
assert len(MISC) % 2 == 0


def build(nc, hid_in, norm_w, in_w, conv_w, conv_b, dt_bias, a_log, d_skip, gnorm_w, out_w,
          ln1_g, ln1_b, w1, b1, ln2_g, ln2_b, w2, b2, out):
    ctx = ExitStack()
    with ctx:
        def sb(name, shape, dt=F32):
            return ctx.enter_context(nc.sbuf_tensor(name, shape, dt))

        def pb(name, shape, dt=F32):
            return ctx.enter_context(nc.psum_tensor(name, shape, dt))

        def sem(name):
            return ctx.enter_context(nc.semaphore(name))

        ident4 = sb("ident4", [P, S])
        ident = ident4[:, 0:P]
        ident_b = sb("ident_b", [P, P], BF16)
        sel = sb("sel", [96, SLOTS, 2 * P], BF16)
        blockones = sb("blockones", [P, 2])
        neghalf = sb("neghalf", [P, 8])
        inv_dm = sb("inv_dm", [P, 8])
        eps_c = sb("eps_c", [P, 8])
        one_c = sb("one_c", [P, 1])
        w_hi = sb("w_hi", [P, UNITS, TILES, P], F32R)
        w_lo = sb("w_lo", [P, UNITS, TILES, P], F32R)
        wdt_hi = sb("wdt_hi", [P, H], F32R)
        wdt_lo = sb("wdt_lo", [P, H], F32R)
        w_out = sb("w_out", [P, SLOTS, DM])
        nw = sb("nw", [P, 1])
        cw = sb("cw", [P, UNITS, CONVS, KW])
        cb_bias = sb("cb_bias", [P, UNITS, CONVS])
        dskip = sb("dskip", [P, SLOTS])
        gnw = sb("gnw", [P, SLOTS])
        dtb = sb("dtb", [P, H])
        alog = sb("alog", [P, H])
        aexp = sb("aexp", [P, 2, H])
        fg1 = sb("fg1", [P, 1])
        fb1 = sb("fb1", [P, 1])
        fg2 = sb("fg2", [P, HT])
        fb2 = sb("fb2", [P, HT])
        dt_all = sb("dt_all", [P, NCH, H])
        da_parts = sb("da_parts", [96, NB * S], BF16)
        pr_parts = sb("pr_parts", [96, NB * S], BF16)
        xn_dram = nc.dram_tensor("xn_scratch", (P, NCH, DM), F32, kind="Internal").ap()
        res_dram = nc.dram_tensor("residual_scratch", (P, NCH, DM), F32, kind="Internal").ap()
        x1_dram = nc.dram_tensor("x1_scratch", (P, NCH, DM), F32, kind="Internal").ap()
        xn_hi = sb("xn_hi", [P, 2, S], F32R)
        xn_lo = sb("xn_lo", [P, 2, S], F32R)
        xn_stage = sb("xn_stage", [P, CH, DM])
        r_stage = sb("r_stage", [P, CH, DM])
        conv = sb("conv", [P, 4, S])
        bt = sb("bt", [P, CH, P])
        chan = sb("chan", [P, 2 * CONVS - 1, S])
        gate = sb("gate", [P, R, S])
        cbs = sb("cbs", [P, 2, S])
        lm = sb("lm", [P, 4, 2, S])
        xdt = sb("xdt", [P, 4, S])
        cdec = sb("cdec", [P, 4, S])
        pend = sb("pend", [P, 4, CH])
        xw = sb("xw", [P, 2, CH - 1, P])
        hpk = sb("hpk", [P, 2, CH - 1, NS])
        hbd = sb("hbd", [P, 2, CH - 1, P])
        gated = sb("gated", [P, 2, R, S])
        sq = sb("sq", [P, S])
        ssum = sb("ssum", [P, 2, S])
        rbs = sb("rbs", [P, S])
        vtok = sb("vtok", [P, 2 * CH])
        rtok = sb("rtok", [P, 2 * CH])
        rexp = sb("rexp", [P, 2 * CH, HP])
        ocm = rexp[:, :, :].rearrange("p c d -> p (c d)")

        def xn_of(ring, b):
            return ring[:, bass.ds(b % 2, 1), :].rearrange("p a s -> p (a s)")

        def chan_of(q, t):
            return 0 if t == 0 else 1 + (CONVS - 1) * (q % 2) + t - 1

        bank = [pb(f"bank{i}", [P, S]) for i in range(8)]
        proj_bank, bc_bank, misc_bank, y_bank, out_bank = bank[0:2], bank[2:4], bank[4:6], bank[6], bank[7]

        raw_w = lm[:, :, :, :].rearrange("p a b s -> p (a b s)")
        raw_w2 = gated[:, :, :, :].rearrange("p a b s -> p (a b s)")[:, 2048:2048 + DPROJ - 4096]
        work = chan[:, :, :].rearrange("p a s -> p (a s)")
        flat = [t.rearrange("p a s -> p (a s)") for t in (gate[:, :, :], cdec[:, :, :], conv[:, :, :])]
        gflat = gated[:, :, :, :].rearrange("p a b s -> p (a b s)")
        halves = [t[:, at:at + 1024] for t, at in ((gflat, 0), (gflat, 1024), (work, 4096), (flat[2], 1024),
                                                   (flat[0], 0), (flat[0], 1024), (flat[1], 0), (flat[1], 1024))]
        by_chunk = [t.rearrange("p (c d) -> p c d", d=DM) for t in halves]
        xg, xc = by_chunk[0:4], by_chunk[4:8]
        wk = [work[:, 1024 * i:1024 * i + 1024] for i in range(4)] + [halves[7], raw_w[:, 0:1024]]
        stat = conv[:, :, :].rearrange("p a s -> p (a s)")
        da_split = xdt[:, :, :].rearrange("p a s -> p (a s)").bitcast(BF16)[:, 0:3072]
        prod = raw_w[0:H, :]
        zeros = bt[0:H, 0, :]
        ones = cdec[:, 0, 0:P]

        w_loaded = sem("w_loaded")
        wo_loaded = sem("wo_loaded")
        small_loaded = sem("small_loaded")
        x_loaded = sem("x_loaded")
        consts = sem("consts")
        mean_sum = sem("mean_sum")
        cent = sem("cent")
        sqd = sem("sqd")
        sq_sum = sem("sq_sum")
        rr_pool = sem("rr_pool")
        t_done = sem("t_done")
        xn_done = sem("xn_done")
        xn_t = sem("xn_t")
        xnhi = sem("xnhi")
        xnlo = sem("xnlo")
        resid = sem("resid")
        w_norm = sem("w_norm")
        whi = sem("whi")
        wlo = sem("wlo")
        w_split_dt = sem("w_split_dt")
        dt_mm = sem("dt_mm")
        dt_raw = sem("dt_raw")
        dtstep_v = sem("dtstep_v")
        dtstep_a = sem("dtstep_a")
        da_split_done = sem("da_split_done")
        da_t = sem("da_t")
        da_copied = sem("da_copied")
        pr_t = sem("pr_t")
        pr_split = sem("pr_split")
        wo_scaled = sem("wo_scaled")
        proj_ready = sem("proj_ready")
        z_ready = sem("z_ready")
        xnt_ready = sem("xnt_ready")
        staged = sem("staged")
        res_stored = sem("res_stored")
        xn_stored = sem("xn_stored")
        res_loaded = sem("res_loaded")
        x1_stored = sem("x1_stored")
        x1_loaded = sem("x1_loaded")
        hi_done = sem("hi_done")
        lo_done = sem("lo_done")
        acc_init = sem("acc_init")
        tap = sem("tap")
        silu_done = sem("silu_done")
        gate_done = sem("gate_done")
        cb_ready = sem("cb_ready")
        cb_copied = sem("cb_copied")
        bt_ready = sem("bt_ready")
        bt_copied = sem("bt_copied")
        xt_ready = sem("xt_ready")
        xdt_done = sem("xdt_done")
        xw_done = sem("xw_done")
        bc_ready = sem("bc_ready")
        scanned = sem("scanned")
        cdec_done = sem("cdec_done")
        pend_done = sem("pend_done")
        m_done = sem("m_done")
        s_ready = sem("s_ready")
        hstep = sem("hstep")
        hbd_done = sem("hbd_done")
        y_ready = sem("y_ready")
        skipped = sem("skipped")
        gated_done = sem("gated_done")
        sq_done = sem("sq_done")
        ssum_step = sem("ssum_step")
        var_ready = sem("var_ready")
        var_copied = sem("var_copied")
        rstd_done = sem("rstd_done")
        rexp_done = sem("rexp_done")
        rbc_ready = sem("rbc_ready")
        rbc_copied = sem("rbc_copied")
        normed = sem("normed")
        out_copied = sem("out_copied")
        xo_ready = sem("xo_ready")
        x1_done = sem("x1_done")
        pr_scan = sem("pr_scan")
        dt_aux = sem("dt_aux")
        out_step = sem("out_step")
        f_msum = sem("f_msum")
        f_cent = sem("f_cent")
        f_sq = sem("f_sq")
        f_sqsum = sem("f_sqsum")
        f_rr = sem("f_rr")
        f_xn = sem("f_xn")
        f_t = sem("f_t")
        f_tcopy = sem("f_tcopy")
        f_mm1 = sem("f_mm1")
        f_h = sem("f_h")
        f_gelu = sem("f_gelu")
        f_stats = sem("f_stats")
        f_aggr = sem("f_aggr")
        f_r2 = sem("f_r2")
        f_nrm = sem("f_nrm")
        f_nt = sem("f_nt")
        f_ntcopy = sem("f_ntcopy")
        f_mm2 = sem("f_mm2")
        f_o1 = sem("f_o1")
        f_o2 = sem("f_o2")
        f_stored = sem("f_stored")
        q_load = sem("q_load")
        q_ones = sem("q_ones")
        q_abs = sem("q_abs")
        q_tot = sem("q_tot")
        q_step = sem("q_step")
        q_t = sem("q_t")
        q_copied = sem("q_copied")

        def after(eng, s, per, b, i):
            if isinstance(b, int) and b * per + i + 1 <= 0:
                return
            eng.wait_ge(s, b * per + (i + 1))

        def raw_t(i):
            return work[:, 1024 * i:1024 * i + 1024].rearrange("p (c d) -> p c d", d=DM)

        fst = conv[:, 0, :]
        fmv = conv[:, 1, 0:2 * CH].rearrange("p (c k) -> p c k", k=2)
        fr2 = conv[:, 1, 64:64 + CH]
        fbn = conv[:, 1, 128:128 + 6 * CH].rearrange("p (c k) -> p c k", k=6)
        w1t = gate[:, 0, :]
        w2t = gate[:, 1, :]
        fd = gate[:, 2, :].rearrange("p (c d) -> p c d", d=DM)
        fsq = gate[:, 3, :].rearrange("p (c d) -> p c d", d=DM)
        fxn = xdt[:, 0, :].rearrange("p (c d) -> p c d", d=DM)
        fxt = xdt[:, 1, :]
        bias1 = xdt[:, 2, :]
        bias2 = xdt[:, 3, 0:DM]
        fh = lm[:, 0:2, :, :].rearrange("p a b s -> p (a b) s")
        fge = lm[:, 2:4, :, :].rearrange("p a b s -> p (a b) s")
        x1_all = gflat.rearrange("p (c d) -> p c d", d=DM)
        fnt = work[:, 3072:5120].rearrange("p (t s) -> p t s", s=S)
        fo = cdec[:, 1, :].rearrange("p (c d) -> p c d", d=DM)
        qs = ssum[:, 0, :]
        wq = work[:, 1024:2048]
        wq2 = work[:, 2048:3072]

        def tile_sources(q):
            found = []
            bsrc = raw_w2[:, P * q:P * q + P]
            csrc = raw_w2[:, G * NS + P * q:G * NS + P * q + P]
            found.append((0, (bsrc, lambda w: w[:, q, 0, :])))
            found.append((1, (csrc, lambda w: w[:, q, 1, :])))
            for t0, at in ((2, X0), (CONVS, Z0)):
                src = raw_w[:, at + 512 * q:at + 512 * q + 512].rearrange("p (a r d) -> p r a d", a=2, r=R)
                found.append((t0, (src, lambda w, t0=t0: w[:, q, t0:t0 + R, :].rearrange("p r (a d) -> p r a d", a=2))))
            return found

        NSMALL = 3 + 2 * UNITS * 4 + 4 + 4

        def misc_position(kind, n, k=0):
            return [j for j, x in enumerate(MISC) if x[0] == n and x[1] == kind][k]

        def misc_of(kind, n, k=0):
            return misc_bank[misc_position(kind, n, k) % 2][:, :]

        block = ctx.enter_context(nc.Block())

        @block.sync
        def _(sp):
            x_v = hid_in.rearrange("b (c p) d -> p (b c) d", p=P)
            for i in range(4):
                sp.dma_start(xg[i], x_v[:, 8 * i:8 * i + 8, :]).then_inc(x_loaded, 16)
            sp.dma_start(raw_w, in_w[:, 0:4096]).then_inc(w_loaded, 16)
            sp.dma_start(raw_w2, in_w[:, 4096:DPROJ]).then_inc(w_loaded, 16)
            with nc.allow_non_contiguous_dma(reason="small parameters"):
                sp.dma_start(nw[:, :], norm_w.rearrange("(p o) -> p o", o=1)).then_inc(small_loaded, 16)
                sp.dma_start(dtb[:, :], dt_bias.rearrange("(o h) -> o h", o=1).broadcast_to([P, H])).then_inc(small_loaded, 16)
                sp.dma_start(alog[:, :], a_log.rearrange("(o h) -> o h", o=1).broadcast_to([P, H])).then_inc(small_loaded, 16)
                for a in range(2):
                    half = slice(HP * a, HP * a + HP)
                    for q in range(UNITS):
                        sp.dma_start(cw[half, q, 2:CONVS, :],
                                     conv_w[0:DI].rearrange("(q a r p) k -> q a p r k", q=UNITS, a=2, r=R)[q, a]).then_inc(small_loaded, 16)
                        sp.dma_start(cb_bias[half, q, 2:CONVS],
                                     conv_b[0:DI].rearrange("(q a r p) -> q a p r", q=UNITS, a=2, r=R)[q, a]).then_inc(small_loaded, 16)
                        sp.dma_start(gnw[half, R * q:R * q + R],
                                     gnorm_w.rearrange("(q a r p) -> q a p r", q=UNITS, a=2, r=R)[q, a]).then_inc(small_loaded, 16)
                        sp.dma_start(dskip[half, R * q:R * q + R],
                                     d_skip.rearrange("(q a r) -> q a r", q=UNITS, a=2)[q, a:a + 1].broadcast_to([HP, R])).then_inc(small_loaded, 16)
                for t, at in ((0, DI), (1, DI + G * NS)):
                    sp.dma_start(cw[:, :, t, :], conv_w[at:at + G * NS].rearrange("(q p) k -> p q k", p=P)).then_inc(small_loaded, 16)
                    sp.dma_start(cb_bias[:, :, t], conv_b[at:at + G * NS].rearrange("(q p) -> p q", p=P)).then_inc(small_loaded, 16)
                sp.dma_start(fg1[:, :], ln1_g.rearrange("(p o) -> p o", o=1)).then_inc(small_loaded, 16)
                sp.dma_start(fb1[:, :], ln1_b.rearrange("(p o) -> p o", o=1)).then_inc(small_loaded, 16)
                sp.dma_start(fg2[:, :], ln2_g.rearrange("(t p) -> p t", p=P)).then_inc(small_loaded, 16)
                sp.dma_start(fb2[:, :], ln2_b.rearrange("(t p) -> p t", p=P)).then_inc(small_loaded, 16)
            for a in range(2):
                src = out_w.rearrange("(q a r p) d -> a p q r d", q=UNITS, a=2, r=R)[a]
                for q in range(UNITS):
                    sp.dma_start(w_out[HP * a:HP * a + HP, R * q:R * q + R, :], src[:, q]).then_inc(wo_loaded, 16)
            for i in range(4):
                sp.wait_ge(resid, i + 1)
                sp.dma_start(res_dram[:, 8 * i:8 * i + 8, :], xg[i]).then_inc(res_stored, 16)
                sp.wait_ge(xn_done, i + 1)
                sp.dma_start(xn_dram[:, 8 * i:8 * i + 8, :], xc[i]).then_inc(xn_stored, 16)
            sp.wait_ge(res_stored, 64)
            sp.wait_ge(xn_stored, 64)

            def batch(b):
                if following(b) is not None:
                    sp.wait_ge(xnt_ready, b + 1)
                    sp.dma_start(xn_stage[:, :, :], xn_dram[:, bass.ds((b + 1) * CH, CH), :]).then_inc(staged, 16)
                if not (isinstance(b, int) and b == 0):
                    sp.wait_ge(x1_done, b)
                    sp.dma_start(x1_dram[:, bass.ds((b - 1) * CH, CH), :], r_stage[:, :, :]).then_inc(x1_stored, 16)
                    sp.wait_ge(x1_stored, b * 16)
                if not (isinstance(b, int) and b == NB):
                    sp.dma_start(r_stage[:, :, :], res_dram[:, bass.ds(b * CH, CH), :]).then_inc(res_loaded, 16)

            batch(0)
            with sp.Fori(1, NB - 1) as b:
                batch(b)
            batch(NB - 1)
            batch(NB)
            sp.dma_start(x1_all, x1_dram).then_inc(x1_loaded, 16)
            sp.dma_start(work[:, 0:HID].rearrange("p (t d) -> p t d", d=DM), w1.rearrange("(t p) d -> p t d", p=P)).then_inc(q_load, 16)
            sp.dma_start(work[:, HID:2 * HID], w2).then_inc(q_load, 16)
            sp.dma_start(bias1[:, :], b1.rearrange("(o h) -> o h", o=1).broadcast_to([P, HID])).then_inc(q_load, 16)
            sp.dma_start(bias2[:, :], b2.rearrange("(o h) -> o h", o=1).broadcast_to([P, DM])).then_inc(q_load, 16)
            out_v = out.rearrange("b (c p) d -> b p c d", p=P)
            with sp.Fori(0, NB) as b:
                sp.wait_ge(f_o2, b + 1)
                sp.dma_start(out_v[bass.ds(b, 1)].rearrange("b p c d -> p (b c) d"),
                             x1_all[:, bass.ds(b * CH, CH), :]).then_inc(f_stored, 16)
            sp.wait_ge(f_stored, 16 * NB)

        @block.gpsimd
        def _(gp):
            gp.memset(ident4[:, :], 0.0).then_inc(consts, 1)
            gp.memset(ident_b[:, :], 0.0).then_inc(consts, 1)
            gp.memset(sel[:, :, :], 0.0).then_inc(consts, 1)
            gp.memset(neghalf[:, :], -0.5).then_inc(consts, 1)
            gp.memset(inv_dm[:, :], 1.0 / DM).then_inc(consts, 1)
            gp.memset(eps_c[:, :], EPS).then_inc(consts, 1)
            gp.memset(one_c[:, :], 1.0).then_inc(consts, 1)
            gp.memset(zeros, 0.0).then_inc(consts, 1)
            gp.memset(blockones[:, :], 0.0).then_inc(consts, 1)
            gp.memset(hbd[:, :, :, :], 0.0).then_inc(consts, 1)
            gp.wait_ge(consts, 10)
            gp.affine_select(out=ident_b[:, :], in_=ident_b[:, :], compare_op=ALU.not_equal, fill=1.0, base=0,
                             pattern=[[-1, P]], channel_multiplier=1).then_inc(consts, 1)
            i4 = ident4[:, :].rearrange("p (c i) -> p c i", c=CH)
            gp.affine_select(out=i4, in_=i4, compare_op=ALU.not_equal, fill=1.0, base=0,
                             pattern=[[0, CH], [-1, P]], channel_multiplier=1).then_inc(consts, 1)
            for k in range(3):
                gp.wait_ge(consts, 12 + UNITS * k)
                part = sel[32 * k:32 * k + 32, :, :]
                part = part.rearrange("k (q r) (a c) -> k q r a c", r=R, a=2)
                for q in range(UNITS):
                    gp.affine_select(out=part[:, q], in_=part[:, q], compare_op=ALU.not_equal, fill=1.0, base=-8 * q,
                                     pattern=[[-1, R], [-4, 2], [0, P]], channel_multiplier=1).then_inc(consts, 1)
            for a in range(2):
                gp.wait_ge(consts, 12 + 3 * UNITS + a)
                gp.memset(blockones[HP * a:HP * a + HP, a:a + 1], 1.0).then_inc(consts, 1)
            gp.wait_ge(consts, 26)

            def rsqrt_chain(s, n0, vsum, r1, r2, rr, width):
                inv, eps, exponent = inv_dm[:, 0:width], eps_c[:, 0:width], neghalf[:, 0:width]
                gp.tensor_tensor(r2, vsum, inv, ALU.mult).then_inc(s, 1)
                gp.wait_ge(s, n0 + 1)
                gp.tensor_tensor(r1, r2, eps, ALU.add).then_inc(s, 1)
                gp.wait_ge(s, n0 + 2)
                gp.tensor_tensor(r1, r1, exponent, ALU.pow).then_inc(s, 1)
                gp.wait_ge(s, n0 + 3)
                gp.tensor_tensor(rr, r1, r1, ALU.mult).then_inc(s, 1)
                gp.wait_ge(s, n0 + 4)
                gp.tensor_tensor(r2, rr, r2, ALU.mult).then_inc(s, 1)
                gp.wait_ge(s, n0 + 5)
                gp.tensor_tensor(r2, r2, eps, ALU.add).then_inc(s, 1)
                gp.wait_ge(s, n0 + 6)
                gp.tensor_tensor(r2, r2, exponent, ALU.pow).then_inc(s, 1)
                gp.wait_ge(s, n0 + 7)
                gp.tensor_tensor(rr, r1, r2, ALU.mult).then_inc(s, 1)

            for i in range(4):
                gp.wait_ge(sq_sum, i + 1)
                rsqrt_chain(rr_pool, 8 * i, stat[:, 64 + 8 * i:72 + 8 * i],
                            stat[:, 192 + 8 * i:200 + 8 * i], stat[:, 256 + 8 * i:264 + 8 * i],
                            stat[:, 320 + 8 * i:328 + 8 * i], 8)
            for i in range(4):
                gp.wait_ge(t_done, i + 1)
                gp.tensor_tensor(xg[i], xg[i], raw_t(i), ALU.add).then_inc(resid, 1)
            gp.wait_ge(pr_split, 5)
            gp.wait_ge(xnlo, NB)

            def slot(b, n):
                q, r = divmod(n, R)
                if back(b, n, LAG_NORM) is not None:
                    bb, m = back(b, n, LAG_NORM)
                    v = m // R
                    after(gp, rbc_copied, UNITS, bb, v)
                    after(gp, sq_done, SLOTS, bb, m)
                    gp.tensor_tensor(gated[:, v % 2, m % R, :], gated[:, v % 2, m % R, :], rbs[:, :], ALU.mult).then_inc(normed, 1)
                ssd = back(b, n, LAG_M)
                if ssd is not None:
                    bb, m = ssd
                    mq, mr = divmod(m, R)
                    after(gp, xdt_done, SLOTS, bb, m)
                    after(gp, scanned, 2 * SLOTS, bb, 2 * m + 1)
                    after(gp, s_ready, SLOTS, bb, m - 2)
                    for a in range(2):
                        ldec = (lm[:, mr, a, :].rearrange("p (c i) -> p c i", c=CH)[:, 0:CH - 1, P - 1:P]
                                .broadcast_to([P, CH - 1, HP]))
                        gp.tensor_tensor(xw[:, mr % 2, :, HP * a:HP * a + HP],
                                         xdt[:, mr, :].rearrange("p (c d) -> p c d", c=CH)[:, 0:CH - 1, HP * a:HP * a + HP],
                                         ldec, ALU.mult).then_inc(xw_done, 1)
                    after(gp, cb_copied, 2 * UNITS, bb, 2 * mq + 1)
                    after(gp, xw_done, 2 * SLOTS, bb, 2 * m + 1)
                    gp.tensor_tensor(lm[:, mr, :, :], lm[:, mr, :, :], cbs[:, :, :], ALU.mult).then_inc(m_done, 1)
                yy = back(b, n, LAG_SUM)
                if yy is not None and yy[1] % R > 0:
                    bb, m = yy
                    after(gp, sq_done, SLOTS, bb, m)
                    after(gp, ssum_step, 3 * UNITS, bb, 3 * (m // R) + m % R - 2)
                    gp.tensor_tensor(ssum[:, m // R % 2, :], ssum[:, m // R % 2, :], sq[:, :], ALU.add).then_inc(ssum_step, 1)
                if r == 0 and back(b, n, LAG_VAR) is not None:
                    bb, m = back(b, n, LAG_VAR)
                    v = m // R
                    after(gp, var_copied, UNITS, bb, v)
                    after(gp, rexp_done, UNITS, bb, v - 1)
                    gp.tensor_tensor(rtok[:, :], vtok[:, :], neghalf[:, 0:2 * CH], ALU.pow).then_inc(rstd_done, 1)

            for n in range(SLOTS):
                slot(0, n)
            with gp.Fori(1, NB - 1) as b:
                for n in range(SLOTS):
                    slot(b, n)
            for b in (NB - 1, NB):
                for n in range(SLOTS):
                    slot(b, n)

            with gp.Fori(0, NB) as b:
                gp.wait_ge(f_sqsum, b + 1)
                rsqrt_chain(f_rr, b * 8, fst[:, 4:8], fst[:, 12:16], fst[:, 16:20], fst[:, 20:24], 4)
                gp.wait_ge(f_aggr, b * 2 + 2)
                gp.tensor_tensor(fr2[:, :], fmv[:, :, 1], neghalf[:, 0:CH], ALU.pow).then_inc(f_r2, 1)

        @block.scalar
        def _(act):
            for i in range(4):
                act.wait_ge(cent, i + 1)
                act.activation(raw_t(i), xc[i], ACT.Square).then_inc(sqd, 1)
            act.wait_ge(w_norm, 1)
            act.activation(wdt_hi[:, :], raw_w2[:, DT0 - 4096:DT0 - 4096 + H], ACT.Copy).then_inc(w_split_dt, 1)
            act.wait_ge(w_norm, 2)
            for q in range(UNITS):
                for t0, src in tile_sources(q):
                    act.activation(src[1](w_hi), src[0], ACT.Copy).then_inc(whi, 1)
            for b in range(NB):
                act.wait_ge(xn_t, b + 1)
                if b >= 2:
                    act.wait_ge(dt_mm, b - 1)
                act.activation(xn_hi[:, b % 2, :], bank[b % 2][:, :], ACT.Copy).then_inc(xnhi, 1)
            act.wait_ge(dtstep_v, 2)
            act.activation(aexp[:, :, :], aexp[:, :, :], ACT.Exp).then_inc(dtstep_a, 1)
            act.wait_ge(dtstep_v, 4)
            act.activation(wk[1], wk[1], ACT.Exp, scale=-1.0).then_inc(dtstep_a, 1)
            act.wait_ge(dtstep_v, 20)
            act.activation(wk[4], wk[4], ACT.Exp, scale=-1.0).then_inc(dtstep_a, 1)
            for i in range(NB):
                act.wait_ge(da_t, i + 1)
                act.activation(da_parts[:, S * i:S * i + S], bank[i % 2][0:96, 0:S // 2].bitcast(BF16), ACT.Copy).then_inc(da_copied, 1)
            act.wait_ge(wo_loaded, 16 * 2 * UNITS)
            act.wait_ge(small_loaded, NSMALL * 16)
            for k in range(SLOTS):
                act.activation(w_out[:, k, :], w_out[:, k, :], ACT.Copy, scale=gnw[:, k:k + 1]).then_inc(wo_scaled, 1)
            act.wait_ge(pr_split, 5)
            act.wait_ge(res_stored, 64)
            act.wait_ge(xnt_ready, 1)
            act.activation(xn_hi[:, 0, :], bank[6][:, :], ACT.Copy).then_inc(hi_done, 1)

            def slot(b, n):
                q, r = divmod(n, R)
                real = not (isinstance(b, int) and b == NB)
                if real:
                    for t in PLAN[r]:
                        ci = CONV_ORDER.index((q, t))
                        after(act, proj_ready, NCONV, b, ci)
                        after(act, silu_done, NCONV, b, ci - 4)
                        act.activation(conv[:, ci % 4, :], proj_bank[proj_position(n, t) % 2][:, :], ACT.Identity,
                                       scale=cw[:, q, t, KW - 1:KW], bias=cb_bias[:, q, t:t + 1]).then_inc(acc_init, 1)
                prev = back(b, n, 1)
                if prev is not None:
                    bb, m = prev
                    pq, prr = divmod(m, R)
                    for t in PLAN[prr]:
                        i = CONV_ORDER.index((pq, t))
                        after(act, tap, NTAP, bb, TAP[pq, t, KW - 1])
                        if t == 0:
                            after(act, bt_ready, UNITS, bb, pq - 1)
                            after(act, cb_ready, 2 * UNITS, bb, 2 * (pq - 1) + 1)
                        elif t == 1:
                            after(act, cdec_done, SLOTS, bb, 4 * (pq - 2) + 3)
                        else:
                            after(act, skipped, SLOTS, bb, 4 * (pq - 2) + t - 2)
                        act.activation(chan[:, chan_of(pq, t), :], conv[:, i % 4, :], ACT.Silu).then_inc(silu_done, 1)
                st = back(b, n, LAG_STATE + 1)
                if st is not None:
                    bb, m = st
                    after(act, hstep, 3 * SLOTS, bb, 3 * m + 2)
                    after(act, y_ready, SLOTS, bb, m - 2)
                    for a in range(2):
                        half = slice(HP * a, HP * a + HP)
                        act.activation(hbd[half, m % 2, :, half], hpk[half, m % 2, :, :], ACT.Copy).then_inc(hbd_done, 1)
                yy = back(b, n, LAG_SUM)
                if yy is not None:
                    bb, m = yy
                    after(act, gated_done, SLOTS, bb, m)
                    v = m // R
                    if m % R == 0:
                        after(act, var_ready, UNITS, bb, v - 2)
                        after(act, ssum_step, 3 * UNITS, bb, 3 * v - 1)
                        dst = ssum[:, v % 2, :]
                    else:
                        after(act, ssum_step, 3 * UNITS, bb, 3 * v + m % R - 2)
                        dst = sq[:, :]
                    act.activation(dst, gated[:, v % 2, m % R, :], ACT.Square).then_inc(sq_done, 1)
                if r == 1 and back(b, n, LAG_FACTOR) is not None:
                    bb, m = back(b, n, LAG_FACTOR)
                    v = m // R
                    after(act, rstd_done, UNITS, bb, v)
                    after(act, rbc_ready, UNITS, bb, v - 1)
                    act.activation(rexp[:, :, :], rtok[:, :].unsqueeze(2).broadcast_to([P, 2 * CH, HP]), ACT.Copy).then_inc(rexp_done, 1)
                ssd = back(b, n, LAG_SSD)
                if n == XN_SLOT and following(b) is not None:
                    after(act, xnt_ready, 1, b, 1)
                    act.activation(xn_of(xn_hi, following(b)), misc_of("xn", n), ACT.Copy).then_inc(hi_done, 1)
                if n == XO_SLOT - 1 and back(b, n, SLOTS) is not None:
                    bb, _ = back(b, n, SLOTS)
                    after(act, out_step, SLOTS, bb, SLOTS - 1)
                    after(act, xo_ready, 1, bb, -1)
                    act.activation(ocm[:, :], out_bank[:, :], ACT.Copy).then_inc(out_copied, 1)
                if r == 0 and back(b, n, LAG_VAR) is not None:
                    bb, m = back(b, n, LAG_VAR)
                    v = m // R
                    after(act, var_ready, UNITS, bb, v)
                    after(act, rstd_done, UNITS, bb, v - 1)
                    act.activation(vtok[:, :], misc_of("var", n)[:, 0:2 * CH], ACT.Identity, scale=1.0 / (DI // G),
                                   bias=eps_c[:, 0:1]).then_inc(var_copied, 1)
                if r == 1 and back(b, n, LAG_M) is not None:
                    bb, m = back(b, n, LAG_M)
                    v = m // R
                    after(act, bt_ready, UNITS, bb, v)
                    after(act, s_ready, SLOTS, bb, m - 1)
                    act.activation(bt[:, :, :], misc_of("bt", n).rearrange("p (c d) -> p c d", c=CH), ACT.Copy).then_inc(bt_copied, 1)
                    for a in range(2):
                        after(act, cb_ready, 2 * UNITS, bb, 2 * v + a)
                        after(act, m_done, SLOTS, bb, m - 1)
                        act.activation(cbs[:, a, :], misc_of("cb", n, a), ACT.Copy).then_inc(cb_copied, 1)
                if ssd is not None:
                    bb, m = ssd
                    after(act, z_ready, SLOTS, bb, m)
                    after(act, gated_done, SLOTS, bb, m - 4)
                    act.activation(gate[:, m % R, :], proj_bank[proj_position(n, "z") % 2][:, :], ACT.Silu).then_inc(gate_done, 1)
                if r == 1 and back(b, n, LAG_FACTOR) is not None:
                    bb, m = back(b, n, LAG_FACTOR)
                    v = m // R
                    after(act, rbc_ready, UNITS, bb, v)
                    after(act, normed, SLOTS, bb, 4 * v - 1)
                    act.activation(rbs[:, :], misc_of("rbc", n), ACT.Copy).then_inc(rbc_copied, 1)

            for n in range(SLOTS):
                slot(0, n)
            with act.Fori(1, NB - 1) as b:
                for n in range(SLOTS):
                    slot(b, n)
            for b in (NB - 1, NB):
                for n in range(SLOTS):
                    slot(b, n)

            act.wait_ge(q_load, 64)
            for k in range(2):
                act.activation(wq[:, HID * k:HID * k + HID], work[:, HID * k:HID * k + HID], ACT.Abs,
                               accum_out=qs[:, k:k + 1]).then_inc(q_abs, 1)
            for k in range(2):
                act.wait_ge(q_t, k + 1)
                act.activation((w1t, w2t)[k], bank[1 + k][:, :], ACT.Copy).then_inc(q_copied, 1)
            with act.Fori(0, NB) as b:
                act.wait_ge(f_cent, b + 1)
                act.activation(fsq, fd, ACT.Square).then_inc(f_sq, 1)
                act.wait_ge(f_t, b + 1)
                act.activation(fxt, bank[0][:, :], ACT.Identity, scale=fg1[:, :], bias=fb1[:, :]).then_inc(f_tcopy, 1)
                for c in range(CH):
                    act.wait_ge(f_h, b * CH + (c + 1))
                    act.activation(fge[:, c, :], fh[:, c, :], ACT.Gelu).then_inc(f_gelu, 1)
                for t in range(HT):
                    act.wait_ge(f_nt, b * HT + (t + 1))
                    act.activation(fnt[:, t, :], bank[3 + t % 2][:, :], ACT.Identity, scale=fg2[:, t:t + 1],
                                   bias=fb2[:, t:t + 1]).then_inc(f_ntcopy, 1)

        @block.vector
        def _(dve):
            V = nc.vector
            dve.wait_ge(x_loaded, 64)
            for i in range(4):
                V.tensor_reduce(stat[:, 8 * i:8 * i + 8], xg[i], AX_X, ALU.add).then_inc(mean_sum, 1)
            dve.wait_ge(mean_sum, 4)
            V.tensor_scalar(stat[:, 32:64], stat[:, 0:32], 1.0 / DM, None, ALU.mult).then_inc(mean_sum, 1)
            dve.wait_ge(mean_sum, 5)

            for i in range(4):
                V.tensor_tensor(xc[i], xg[i],
                                stat[:, 32 + 8 * i:40 + 8 * i].unsqueeze(2).broadcast_to([P, 8, DM]),
                                ALU.subtract).then_inc(cent, 1)
            for i in range(4):
                dve.wait_ge(sqd, i + 1)
                V.tensor_reduce(stat[:, 64 + 8 * i:72 + 8 * i], raw_t(i), AX_X, ALU.add).then_inc(sq_sum, 1)
            dve.wait_ge(w_loaded, 32)
            dve.wait_ge(small_loaded, NSMALL * 16)
            V.tensor_scalar(raw_w2, raw_w2, nw[:, :], None, ALU.mult).then_inc(w_norm, 1)
            V.tensor_scalar(raw_w, raw_w, nw[:, :], None, ALU.mult).then_inc(w_norm, 1)
            for i in range(4):
                dve.wait_ge(rr_pool, 8 * i + 8)
                V.tensor_tensor(raw_t(i), xc[i],
                                stat[:, 192 + 8 * i:200 + 8 * i].unsqueeze(2).broadcast_to([P, 8, DM]),
                                ALU.mult).then_inc(t_done, 1)
            for i in range(4):
                V.tensor_tensor(xc[i], xc[i],
                                stat[:, 320 + 8 * i:328 + 8 * i].unsqueeze(2).broadcast_to([P, 8, DM]),
                                ALU.mult).then_inc(xn_done, 1)
            dve.wait_ge(w_split_dt, 1)
            V.tensor_tensor(wdt_lo[:, :], raw_w2[:, DT0 - 4096:DT0 - 4096 + H], wdt_hi[:, :].bitcast(F32), ALU.subtract).then_inc(w_split_dt, 1)
            n_hi = 0
            for q in range(UNITS):
                for t0, src in tile_sources(q):
                    n_hi += 1
                    dve.wait_ge(whi, n_hi)
                    V.tensor_tensor(src[1](w_lo), src[0], src[1](w_hi).bitcast(F32), ALU.subtract).then_inc(wlo, 1)
            for b in range(NB):
                dve.wait_ge(xnhi, b + 1)
                V.tensor_tensor(xn_lo[:, b % 2, :], bank[b % 2][:, :], xn_hi[:, b % 2, :].bitcast(F32),
                                ALU.subtract).then_inc(xnlo, 1)
            step = 0

            def chain(ins):
                nonlocal step
                step += 1
                ins.then_inc(dtstep_v, 1)
                dve.wait_ge(dtstep_v, step)

            chain(V.tensor_scalar(aexp[:, 0, :], alog[:, :], 80.0, None, ALU.min))
            V.tensor_scalar(aexp[:, 1, :], alog[:, :], 80.0, 0.0, ALU.subtract, ALU.max).then_inc(dt_aux, 1)
            dve.wait_ge(dt_aux, 1)
            chain(V.tensor_scalar(aexp[:, 1, :], aexp[:, 1, :], 80.0, None, ALU.min))
            dve.wait_ge(resid, 4)
            dve.wait_ge(xn_stored, 64)
            dve.wait_ge(res_stored, 64)
            dve.wait_ge(dt_mm, NB)
            raw3 = wk[0].rearrange("p (c h) -> p c h", h=H)
            for k in range(2):
                V.tensor_tensor(raw3[:, 16 * k:16 * k + 16, :], bank[2 + k][:, :].rearrange("p (c h) -> p c h", h=H),
                                dtb[:, :].unsqueeze(1).broadcast_to([P, 16, H]), ALU.add).then_inc(dt_raw, 1)
            dve.wait_ge(dt_raw, 2)
            chain(V.tensor_scalar(wk[1], wk[0], -1.0, None, ALU.mult))
            chain(V.tensor_tensor(wk[1], wk[0], wk[1], ALU.max))
            dve.wait_ge(dtstep_a, 2)
            chain(V.tensor_scalar(wk[2], wk[1], 2.0, None, ALU.add))
            chain(V.reciprocal(wk[3], wk[2]))
            chain(V.tensor_tensor(wk[1], wk[1], wk[3], ALU.mult))
            chain(V.tensor_tensor(wk[2], wk[1], wk[1], ALU.mult))
            chain(V.tensor_scalar(wk[3], wk[2], 1.0 / 17, None, ALU.mult))
            for k in (15, 13, 11, 9, 7, 5, 3):
                chain(V.scalar_tensor_tensor(out=wk[3], in0=wk[3], scalar=1.0 / k, in1=wk[2], op0=ALU.add, op1=ALU.mult))
            chain(V.scalar_tensor_tensor(out=wk[3], in0=wk[3], scalar=1.0, in1=wk[1], op0=ALU.add, op1=ALU.mult))
            chain(V.tensor_scalar(wk[0], wk[0], 0.0, None, ALU.max))
            dt_flat = dt_all[:, :, :].rearrange("p c h -> p (c h)")
            chain(V.scalar_tensor_tensor(out=dt_flat, in0=wk[3], scalar=2.0, in1=wk[0], op0=ALU.mult, op1=ALU.add))
            assert step == 19, step
            dve.wait_ge(dtstep_a, 1)
            w4 = wk[4].rearrange("p (c h) -> p c h", h=H)
            V.tensor_tensor(w4, dt_all[:, :, :], aexp[:, 0:1, :].broadcast_to([P, NCH, H]), ALU.mult).then_inc(dt_aux, 1)
            dve.wait_ge(dt_aux, 2)
            V.tensor_scalar(wk[4], wk[4], 200.0, None, ALU.min).then_inc(dt_aux, 1)
            dve.wait_ge(dt_aux, 3)
            chain(V.tensor_tensor(w4, w4, aexp[:, 1:2, :].broadcast_to([P, NCH, H]), ALU.mult))
            dve.wait_ge(dtstep_a, 3)
            parts = da_split.rearrange("p (c k h) -> p c k h", k=3, h=H)
            w3, w5 = wk[3].rearrange("p (c h) -> p c h", h=H), wk[5].rearrange("p (c h) -> p c h", h=H)
            chain(V.tensor_copy(parts[:, :, 0, :], w4))
            chain(V.tensor_tensor(w5, w4, parts[:, :, 0, :], ALU.subtract))
            chain(V.tensor_copy(parts[:, :, 1, :], w5))
            chain(V.tensor_tensor(w3, w5, parts[:, :, 1, :], ALU.subtract))
            V.tensor_copy(parts[:, :, 2, :], w3).then_inc(da_split_done, 1)
            for i in range(NB):
                dve.wait_ge(pr_t, i + 1)
                for c in range(CH):
                    at = S * i + P * c
                    V.tensor_tensor_scan(prod[:, at:at + P], bank[2 + i % 2][0:H, P * c:P * c + P], zeros[:, :], 1.0,
                                         ALU.mult, ALU.add).then_inc(pr_scan, 1)
            dve.wait_ge(pr_scan, NCH)
            res = work[0:H, 0:4096]
            V.tensor_copy(pr_parts[0:H, :], prod).then_inc(pr_split, 1)
            dve.wait_ge(pr_split, 1)
            V.tensor_tensor(res, prod, pr_parts[0:H, :], ALU.subtract).then_inc(pr_split, 1)
            dve.wait_ge(pr_split, 2)
            V.tensor_copy(pr_parts[H:2 * H, :], res).then_inc(pr_split, 1)
            dve.wait_ge(pr_split, 3)
            V.tensor_copy(prod, pr_parts[H:2 * H, :]).then_inc(pr_split, 1)
            dve.wait_ge(pr_split, 4)
            V.tensor_tensor(pr_parts[2 * H:3 * H, :], res, prod, ALU.subtract).then_inc(pr_split, 1)
            dve.wait_ge(da_copied, NB)
            V.memset(da_parts[:, :].rearrange("p (c i) -> p c i", i=P)[:, :, 0:1], 0.0).then_inc(da_copied, 1)
            dve.wait_ge(hi_done, 1)
            V.tensor_tensor(xn_lo[:, 0, :], bank[6][:, :], xn_hi[:, 0, :].bitcast(F32), ALU.subtract).then_inc(lo_done, 1)

            def slot(b, n):
                q, r = divmod(n, R)
                real = not (isinstance(b, int) and b == NB)
                ssd = back(b, n, LAG_SSD)
                if ssd is not None:
                    bb, m = ssd
                    mq, mr = divmod(m, R)
                    after(dve, y_ready, SLOTS, bb, m - 4)
                    for a in range(2):
                        after(dve, bc_ready, 3 * SLOTS, bb, 3 * m + a)
                        V.tensor_tensor_scan(lm[:, mr, a, :], bc_bank[(3 * m + a) % 2][:, :], ident4[:, :], 0.0,
                                             ALU.mult, ALU.add).then_inc(scanned, 1)
                if ssd is not None:
                    bb, m = ssd
                    mr = m % R
                    after(dve, xt_ready, SLOTS, bb, m)
                    dt_b = (dt_all[:, bass.ds(bb * CH, CH), 8 * mq + mr:8 * mq + mr + 5:4]
                            .unsqueeze(3).broadcast_to([P, CH, 2, HP]))
                    V.tensor_tensor(xdt[:, mr, :].rearrange("p (c a d) -> p c a d", c=CH, a=2),
                                    misc_of("xt", n).rearrange("p (c a d) -> p c a d", c=CH, a=2),
                                    dt_b, ALU.mult).then_inc(xdt_done, 1)
                if real:
                    for shift in range(1, KW):
                        for t in PLAN[r]:
                            ci, i = CONV_ORDER.index((q, t)), proj_position(n, t)
                            if shift == 1:
                                after(dve, acc_init, NCONV, b, ci)
                            else:
                                after(dve, tap, NTAP, b, TAP[q, t, shift - 1])
                            V.scalar_tensor_tensor(out=conv[:, ci % 4, shift:S], in0=proj_bank[i % 2][:, 0:S - shift],
                                                   scalar=cw[:, q, t, KW - 1 - shift:KW - shift],
                                                   in1=conv[:, ci % 4, shift:S], op0=ALU.mult, op1=ALU.add).then_inc(tap, 1)
                st = back(b, n, LAG_STATE)
                if st is not None:
                    bb, m = st
                    after(dve, s_ready, SLOTS, bb, m)
                    after(dve, hbd_done, 2 * SLOTS, bb, 2 * (m - 2) + 1)
                    sbank = misc_of("s", n)
                    V.tensor_copy(hpk[:, m % 2, 0, :], sbank[:, 0:NS]).then_inc(hstep, 1)
                    after(dve, pend_done, SLOTS, bb, m)
                    for c in range(1, CH - 1):
                        after(dve, hstep, 3 * SLOTS, bb, 3 * m + c - 1)
                        V.scalar_tensor_tensor(out=hpk[:, m % 2, c, :], in0=hpk[:, m % 2, c - 1, :],
                                               scalar=pend[:, m % R, c:c + 1], in1=sbank[:, NS * c:NS * c + NS],
                                               op0=ALU.mult, op1=ALU.add).then_inc(hstep, 1)
                if ssd is not None:
                    bb, m = ssd
                    mr = m % R
                    after(dve, bc_ready, 3 * SLOTS, bb, 3 * m + 2)
                    pbank = bc_bank[(3 * m + 2) % 2]
                    V.tensor_copy(pend[:, mr, :].unsqueeze(2),
                                  pbank[:, :].rearrange("p (c i) -> p c i", c=CH)[:, :, P - 1:P]).then_inc(pend_done, 1)
                    V.tensor_tensor(cdec[:, mr, :], pbank[:, :], chan[:, chan_of(mq, 1), :], ALU.mult).then_inc(cdec_done, 1)
                yy = back(b, n, LAG_Y)
                if yy is not None:
                    bb, m = yy
                    v, mr = divmod(m, R)
                    after(dve, y_ready, SLOTS, bb, m)
                    after(dve, out_step, SLOTS, bb, m - 8)
                    V.scalar_tensor_tensor(out=gated[:, v % 2, mr, :], in0=chan[:, chan_of(v, 2 + mr), :],
                                           scalar=dskip[:, m:m + 1], in1=y_bank[:, :],
                                           op0=ALU.mult, op1=ALU.add).then_inc(skipped, 1)
                    after(dve, gate_done, SLOTS, bb, m)
                    after(dve, skipped, SLOTS, bb, m)
                    V.tensor_tensor(gated[:, v % 2, mr, :], gated[:, v % 2, mr, :], gate[:, mr, :],
                                    ALU.mult).then_inc(gated_done, 1)
                if n == XN_SLOT and following(b) is not None:
                    after(dve, hi_done, 1, b, 1)
                    V.tensor_tensor(xn_of(xn_lo, following(b)), misc_of("xn", n), xn_of(xn_hi, following(b)).bitcast(F32),
                                    ALU.subtract).then_inc(lo_done, 1)
                if n == XO_SLOT and back(b, n, SLOTS) is not None:
                    bb, _ = back(b, n, SLOTS)
                    after(dve, xo_ready, 1, bb, 0)
                    dve.wait_ge(res_loaded, bb * 16 + 16)
                    xs = r_stage[:, :, :]
                    V.tensor_tensor(xs, misc_of("xo", n).rearrange("p (c d) -> p c d", d=DM), xs, ALU.add).then_inc(x1_done, 1)

            for n in range(SLOTS):
                slot(0, n)
            with dve.Fori(1, NB - 1) as b:
                for n in range(SLOTS):
                    slot(b, n)
            for b in (NB - 1, NB):
                for n in range(SLOTS):
                    slot(b, n)

            dve.wait_ge(x1_loaded, 16)
            qn = 0

            def qchain(ins):
                nonlocal qn
                qn += 1
                ins.then_inc(q_step, 1)
                dve.wait_ge(q_step, qn)

            V.memset(ones, 1.0).then_inc(q_ones, 1)
            dve.wait_ge(q_tot, 1)
            mean, scale, inv = qs[:, 4:6], qs[:, 8:10], qs[:, 12:14]
            qchain(V.tensor_scalar(mean, bank[0][:, 0:2], 1.0 / (HID * DM), EPS, ALU.mult, ALU.max))
            qchain(V.reciprocal(scale, mean))
            qchain(V.reciprocal(inv, scale))
            MAGIC = 1.5 * 2.0 ** 23
            for k in range(2):
                w, t = work[:, HID * k:HID * k + HID], wq[:, HID * k:HID * k + HID]
                qchain(V.tensor_scalar(t, w, scale[:, k:k + 1], 2.0, ALU.mult, ALU.min))
                qchain(V.tensor_scalar(t, t, -2.0, MAGIC, ALU.max, ALU.add))
                qchain(V.tensor_scalar(t, t, MAGIC, None, ALU.subtract))
                qchain(V.tensor_scalar(t, t, 1.0, -1.0, ALU.min, ALU.max))
                qchain(V.scalar_tensor_tensor(out=t, in0=t, scalar=inv[:, k:k + 1], in1=w, op0=ALU.mult, op1=ALU.subtract))
                qchain(V.tensor_tensor(wq2[:, HID * k:HID * k + HID], w, t, ALU.add))
            with dve.Fori(0, NB) as b:
                xs = x1_all[:, bass.ds(b * CH, CH), :]
                V.tensor_reduce(fst[:, 0:4], xs, AX_X, ALU.add).then_inc(f_msum, 1)
                dve.wait_ge(f_msum, 2 * b + 1)
                V.tensor_scalar(fst[:, 24:28], fst[:, 0:4], 1.0 / DM, None, ALU.mult).then_inc(f_msum, 1)
                dve.wait_ge(f_msum, 2 * b + 2)
                V.tensor_tensor(fd, xs, fst[:, 24:28].unsqueeze(2).broadcast_to([P, CH, DM]), ALU.subtract).then_inc(f_cent, 1)
                dve.wait_ge(f_sq, b + 1)
                V.tensor_reduce(fst[:, 4:8], fsq, AX_X, ALU.add).then_inc(f_sqsum, 1)
                dve.wait_ge(f_rr, b * 8 + 8)
                V.tensor_tensor(fxn, fd, fst[:, 20:24].unsqueeze(2).broadcast_to([P, CH, DM]), ALU.mult).then_inc(f_xn, 1)
                for c in range(CH):
                    dve.wait_ge(f_mm1, b * CH + (c + 1))
                    V.tensor_tensor(fh[:, c, :], bank[1 + c % 2][:, :], bias1[:, :], ALU.add).then_inc(f_h, 1)
                for c in range(CH):
                    dve.wait_ge(f_gelu, b * CH + (c + 1))
                    if c > 0:
                        dve.wait_ge(f_stats, b * (2 * CH) + max(1, 2 * c - 2))
                    V.bn_stats(fbn[:, c, :], fge[:, c, :]).then_inc(f_stats, 1)
                    if c > 0:
                        V.bn_aggr(fmv[:, c - 1, :], fbn[:, c - 1, :]).then_inc(f_stats, 1)
                dve.wait_ge(f_stats, b * (2 * CH) + 2 * CH - 1)
                V.tensor_scalar(fmv[:, 0:CH - 1, 1:2], fmv[:, 0:CH - 1, 1:2], EPS, None, ALU.add).then_inc(f_aggr, 1)
                V.bn_aggr(fmv[:, CH - 1, :], fbn[:, CH - 1, :]).then_inc(f_stats, 1)
                dve.wait_ge(f_stats, b * (2 * CH) + 2 * CH)
                V.tensor_scalar(fmv[:, CH - 1:CH, 1:2], fmv[:, CH - 1:CH, 1:2], EPS, None, ALU.add).then_inc(f_aggr, 1)
                dve.wait_ge(f_r2, b + 1)
                for c in range(CH):
                    V.tensor_scalar(fge[:, c, :], fge[:, c, :], fmv[:, c, 0:1], fr2[:, c:c + 1],
                                    ALU.subtract, ALU.mult).then_inc(f_nrm, 1)
                dve.wait_ge(f_mm2, b + 1)
                V.tensor_tensor(fo, bank[5][:, :].rearrange("p (c d) -> p c d", d=DM),
                                bias2[:, :].unsqueeze(1).broadcast_to([P, CH, DM]), ALU.add).then_inc(f_o1, 1)
                dve.wait_ge(f_o1, b + 1)
                V.tensor_tensor(xs, fo, xs, ALU.add).then_inc(f_o2, 1)

        @block.tensor
        def _(pe):
            MM, TR = nc.tensor.matmul, nc.tensor.transpose
            pe.wait_ge(consts, 26)
            pe.wait_ge(w_split_dt, 2)

            def dt_products(b):
                pe.wait_ge(xnlo, b + 1)
                for c in range(CH):
                    dst = bank[2 + b // 4][:, H * (CH * (b % 4) + c):H * (CH * (b % 4) + c + 1)]
                    tok = slice(P * c, P * c + P)
                    MM(dst, xn_hi[:, b % 2, tok], wdt_hi[:, :], start=True, stop=False)
                    MM(dst, xn_lo[:, b % 2, tok], wdt_hi[:, :], start=False, stop=False)
                    last = MM(dst, xn_hi[:, b % 2, tok], wdt_lo[:, :], start=False, stop=True)
                last.then_inc(dt_mm, 1)

            for b in range(NB):
                pe.wait_ge(xn_done, b // 2 + 1)
                if b >= 2:
                    pe.wait_ge(xnlo, b - 1)
                for c in range(CH):
                    last = TR(bank[b % 2][:, P * c:P * c + P], xc[b // 2][:, CH * (b % 2) + c, :], ident)
                last.then_inc(xn_t, 1)
                if b >= 1:
                    dt_products(b - 1)
            dt_products(NB - 1)
            pe.wait_ge(dtstep_a, 3)
            pe.wait_ge(dt_raw, 2)
            for i in range(NB):
                if i >= 2:
                    pe.wait_ge(pr_scan, CH * (i - 1))
                for c in range(CH):
                    at = (CH * i + c) * H
                    last = TR(bank[2 + i % 2][0:H, P * c:P * c + P], wk[4][:, at:at + H], ident)
                last.then_inc(pr_t, 1)
            pe.wait_ge(da_split_done, 1)
            for i in range(NB):
                if i >= 2:
                    pe.wait_ge(da_copied, i - 1)
                for c in range(CH):
                    at = (CH * i + c) * 3 * H
                    last = TR(bank[i % 2][0:96, 0:S // 2].bitcast(BF16)[:, P * c:P * c + P], da_split[:, at:at + 3 * H], ident_b[:, :])
                last.then_inc(da_t, 1)
            pe.wait_ge(da_copied, NB + 1)
            pe.wait_ge(pr_split, 5)
            pe.wait_ge(wlo, 4 * UNITS)
            pe.wait_ge(wo_scaled, SLOTS)

            def misc_free(b, n, kind, k=0):
                at = misc_position(kind, n, k)
                bb = b
                while True:
                    at -= 2
                    if at < 0:
                        at, bb = at + len(MISC), bb - 1
                        if isinstance(bb, int) and bb < 0:
                            return
                    pn, pkind, lag, pk = MISC[at]
                    who = back(bb, pn, lag) if pkind != "xn" else following(bb)
                    if who is not None:
                        break
                if pkind == "xn":
                    after(pe, lo_done, 1, who, 0)
                    return
                wb, wm = who
                if pkind == "cb":
                    after(pe, cb_copied, 2 * UNITS, wb, 2 * (wm // R) + pk)
                elif pkind == "bt":
                    after(pe, bt_copied, UNITS, wb, wm // R)
                elif pkind == "xt":
                    after(pe, xdt_done, SLOTS, wb, wm)
                elif pkind == "s":
                    after(pe, hstep, 3 * SLOTS, wb, 3 * wm + 2)
                elif pkind == "var":
                    after(pe, var_copied, UNITS, wb, wm // R)
                elif pkind == "rbc":
                    after(pe, rbc_copied, UNITS, wb, wm // R)
                elif pkind == "xo":
                    after(pe, x1_done, 1, wb, 0)

            def proj_free(b, i):
                bb = b
                while True:
                    i -= 2
                    if i < 0:
                        i, bb = i + len(PROJ), bb - 1
                        if isinstance(bb, int) and bb < 0:
                            return
                    pn, pt = PROJ[i]
                    who = back(bb, pn, LAG_SSD if pt == "z" else 0)
                    if who is not None:
                        break
                if pt == "z":
                    after(pe, gate_done, SLOTS, *who)
                else:
                    after(pe, tap, NTAP, bb, TAP[pn // R, pt, KW - 1])

            def transpose_xn(src, dst):
                for c in range(CH):
                    last = TR(dst[:, P * c:P * c + P], src[:, c, :], ident)
                last.then_inc(xnt_ready, 1)

            transpose_xn(xc[0], bank[6])

            def project(b, n, t, who):
                q = n // R
                i = proj_position(n, t)
                proj_free(b, i)
                bb, m = who
                out_b = proj_bank[i % 2][:, :]
                tile = (m // R, CONVS + m % R) if t == "z" else (q, t)
                wh, wl = w_hi[:, tile[0], tile[1], :], w_lo[:, tile[0], tile[1], :]
                if (q, t) == CONV_ORDER[0]:
                    after(pe, lo_done, 1, b, 0)
                hi, lo = xn_of(xn_hi, bb), xn_of(xn_lo, bb)
                MM(out_b, wh, hi, start=True, stop=False)
                MM(out_b, wh, lo, start=False, stop=False)
                MM(out_b, wl, hi, start=False, stop=True).then_inc(z_ready if t == "z" else proj_ready, 1)

            def spread(bb, m, k):
                i = 3 * m + k
                pm, pk = divmod(i - 2, 3)
                if pk < 2:
                    after(pe, scanned, 2 * SLOTS, bb, 2 * pm + pk)
                else:
                    after(pe, cdec_done, SLOTS, bb, pm)
                first = (0, P, HP)[k]
                MM(bc_bank[i % 2][:, :], sel[:, m, first:first + P], (pr_parts if k == 2 else da_parts)[:, bass.ds(bb * S, S)],
                   start=True, stop=True).then_inc(bc_ready, 1)

            def slot(b, n):
                q, r = divmod(n, R)
                real = not (isinstance(b, int) and b == NB)
                ssd = back(b, n, LAG_SSD)
                if ssd is not None:
                    bb, m = ssd
                    mq, mr = divmod(m, R)
                    after(pe, silu_done, NCONV, bb, CONV_ORDER.index((mq, 2 + mr)))
                    misc_free(b, n, "xt")
                    for c in range(CH):
                        last = TR(misc_of("xt", n)[:, P * c:P * c + P], chan[:, chan_of(mq, 2 + mr), P * c:P * c + P], ident)
                    last.then_inc(xt_ready, 1)
                if real:
                    for t in PLAN[r]:
                        project(b, n, t, (b, n))
                st = back(b, n, LAG_STATE)
                if st is not None:
                    bb, m = st
                    after(pe, xw_done, 2 * SLOTS, bb, 2 * m + 1)
                    after(pe, bt_copied, UNITS, bb, m // R)
                    misc_free(b, n, "s")
                    for a in range(2):
                        half = slice(HP * a, HP * a + HP)
                        for c in range(CH - 1):
                            last = MM(misc_of("s", n)[half, NS * c:NS * c + NS], bt[:, c, half], xw[:, m % 2, c, half],
                                      start=True, stop=True)
                    last.then_inc(s_ready, 1)
                if ssd is not None:
                    spread(*ssd, 2)
                if back(b, n, LAG_OUT) is not None:
                    bb, m = back(b, n, LAG_OUT)
                    after(pe, normed, SLOTS, bb, m)
                    if m == 0:
                        after(pe, out_copied, 1, bb, -1)
                    last = MM(out_bank[:, :], w_out[:, m, :], gated[:, (m // R) % 2, m % R, :], start=(m == 0), stop=(m == SLOTS - 1))
                    last.then_inc(out_step, 1)
                yy = back(b, n, LAG_Y)
                if yy is not None:
                    bb, m = yy
                    mr = m % R
                    after(pe, m_done, SLOTS, bb, m)
                    after(pe, hbd_done, 2 * SLOTS, bb, 2 * m + 1)
                    after(pe, cdec_done, SLOTS, bb, m)
                    after(pe, skipped, SLOTS, bb, m - 1)
                    for c in range(CH):
                        tok = slice(P * c, P * c + P)
                        if c > 0:
                            MM(y_bank[:, tok], hbd[:, m % 2, c - 1, :], cdec[:, mr, tok], start=True, stop=False)
                        for a in range(2):
                            half = slice(HP * a, HP * a + HP)
                            last = MM(y_bank[half, tok], xdt[:, mr, P * c + HP * a:P * c + HP * a + HP], lm[:, mr, a, tok],
                                      start=(c == 0), stop=True)
                    last.then_inc(y_ready, 1)
                if r == 0 and back(b, n, LAG_VAR) is not None:
                    bb, m = back(b, n, LAG_VAR)
                    v = m // R
                    after(pe, ssum_step, 3 * UNITS, bb, 3 * v + 2)
                    misc_free(b, n, "var")
                    for c in range(CH):
                        last = MM(misc_of("var", n)[:, 2 * c:2 * c + 2], ssum[:, v % 2, P * c:P * c + P], blockones[:, :], start=True, stop=True)
                    last.then_inc(var_ready, 1)
                if r == 1 and back(b, n, LAG_M) is not None:
                    bb, m = back(b, n, LAG_M)
                    v = m // R
                    misc_free(b, n, "bt")
                    for c in range(CH):
                        last = TR(misc_of("bt", n)[:, P * c:P * c + P], chan[:, 0, P * c:P * c + P], ident)
                    last.then_inc(bt_ready, 1)
                if r == 1 and back(b, n, LAG_M) is not None:
                    bb, m = back(b, n, LAG_M)
                    v = m // R
                    after(pe, silu_done, NCONV, bb, CONV_ORDER.index((v, 1)))
                    for a in range(2):
                        half = slice(HP * a, HP * a + HP)
                        misc_free(b, n, "cb", a)
                        for c in range(CH):
                            tok = slice(P * c, P * c + P)
                            last = MM(misc_of("cb", n, a)[:, tok], chan[half, 0, tok], chan[half, chan_of(v, 1), tok],
                                      start=True, stop=True)
                        last.then_inc(cb_ready, 1)
                if ssd is not None:
                    project(b, n, "z", ssd)
                if r == 1 and back(b, n, LAG_FACTOR) is not None:
                    bb, m = back(b, n, LAG_FACTOR)
                    v = m // R
                    after(pe, rexp_done, UNITS, bb, v)
                    misc_free(b, n, "rbc")
                    for c in range(CH):
                        last = TR(misc_of("rbc", n)[:, P * c:P * c + P], rexp[:, 2 * c:2 * c + 2, :].rearrange("p a d -> p (a d)"), ident)
                    last.then_inc(rbc_ready, 1)
                if n == XN_SLOT and following(b) is not None:
                    pe.wait_ge(staged, b * 16 + 16)
                    misc_free(b, n, "xn")
                    transpose_xn(xn_stage, misc_of("xn", n))
                if n == XO_SLOT and back(b, n, SLOTS) is not None:
                    bb, _ = back(b, n, SLOTS)
                    after(pe, out_copied, 1, bb, 0)
                    misc_free(b, n, "xo")
                    for c in range(CH):
                        last = TR(misc_of("xo", n)[:, P * c:P * c + P], ocm[:, P * c:P * c + P], ident)
                    last.then_inc(xo_ready, 1)
                if back(b, n + 1, LAG_SSD) is not None:
                    for k in range(2):
                        spread(*back(b, n + 1, LAG_SSD), k)

            for n in range(SLOTS):
                slot(0, n)
            with pe.Fori(1, NB - 1) as b:
                for n in range(SLOTS):
                    slot(b, n)
            for b in (NB - 1, NB):
                for n in range(SLOTS):
                    slot(b, n)

            pe.wait_ge(q_abs, 2)
            pe.wait_ge(q_ones, 1)
            MM(bank[0][:, 0:2], ones, qs[:, 0:2], start=True, stop=True).then_inc(q_tot, 1)
            for k in range(2):
                pe.wait_ge(q_step, 9 + 6 * k)
                for t in range(HT):
                    last = TR(bank[1 + k][:, P * t:P * t + P], wq2[:, HID * k + P * t:HID * k + P * t + P], ident)
                last.then_inc(q_t, 1)
            pe.wait_ge(q_copied, 2)
            with pe.Fori(0, NB) as b:
                pe.wait_ge(f_xn, b + 1)
                for c in range(CH):
                    last = TR(bank[0][:, P * c:P * c + P], fxn[:, c, :], ident)
                last.then_inc(f_t, 1)
                pe.wait_ge(f_tcopy, b + 1)
                for c in range(CH):
                    if c >= 2:
                        pe.wait_ge(f_h, b * CH + (c - 1))
                    MM(bank[1 + c % 2][:, :], fxt[:, P * c:P * c + P], w1t, start=True, stop=True).then_inc(f_mm1, 1)
                pe.wait_ge(f_nrm, b * CH + CH)
                for t in range(HT):
                    if t >= 2:
                        pe.wait_ge(f_ntcopy, b * HT + (t - 1))
                    for c in range(CH):
                        last = TR(bank[3 + t % 2][:, P * c:P * c + P], fge[:, c, P * t:P * t + P], ident)
                    last.then_inc(f_nt, 1)
                pe.wait_ge(f_ntcopy, b * HT + HT)
                for c in range(CH):
                    for t in range(HT):
                        last = MM(bank[5][:, P * c:P * c + P], fnt[:, t, P * c:P * c + P], w2t[:, P * t:P * t + P],
                                  start=(t == 0), stop=(t == HT - 1))
                last.then_inc(f_mm2, 1)


_INS = ["L0_attn_hidden_states", "L0_attn_norm_w", "L0_attn_in_proj_w", "L0_attn_conv_w", "L0_attn_conv_b",
        "L0_attn_dt_bias", "L0_attn_A_log", "L0_attn_D", "L0_attn_gate_norm_w", "L0_attn_out_proj_w",
        "L0_ffn_ln1_g", "L0_ffn_ln1_b", "L0_ffn_w1", "L0_ffn_b1", "L0_ffn_ln2_g", "L0_ffn_ln2_b", "L0_ffn_w2",
        "L0_ffn_b2"]


def kernel(**inputs):
    import numpy as _np
    import concourse.bacc as _bacc
    from concourse.bass_utils import run_bass_kernel_spmd as _run

    nc = _bacc.Bacc("TRN2", target_bir_lowering=False, num_devices=1)
    arrays, args = {}, []
    for name in _INS:
        a = _np.ascontiguousarray(inputs[name])
        arrays[f"in_{name}"] = a
        args.append(nc.dram_tensor(f"in_{name}", a.shape, mybir.dt.from_np(a.dtype), kind="ExternalInput").ap())
    out = nc.dram_tensor("out_tokens", (NB, S, DM), F32, kind="ExternalOutput").ap()
    build(nc, *args, out)
    r = _run(nc, [arrays], core_ids=[0])
    return r.results[0]["out_tokens"]
```

```python
from contextlib import ExitStack

import concourse.bass as bass
from concourse import mybir

F32 = mybir.dt.float32
F32R = mybir.dt.float32r
BF16 = mybir.dt.bfloat16
ALU = mybir.AluOpType
ACT = mybir.ActivationFunctionType
AX_X = mybir.AxisListType.X

P = 128
NB, S, DM = 8, 512, 128
H, HP, G, NS, KW = 32, 64, 8, 64, 4
DI = H * HP
CH = S // P
NCH = NB * CH
UNITS, R = G // 2, 4
SLOTS = UNITS * R
TILES = 10
CONVS = 6
HID = 512
HT = HID // P
EPS = 1e-5
MAGIC = 1.5 * 2.0 ** 23
Z0, X0, B0, C0, DT0 = 0, DI, 2 * DI, 2 * DI + G * NS, 2 * DI + 2 * G * NS
DPROJ = DT0 + H

PLAN = [[2], [3, 4], [0, 1], [5]]
CONV_ORDER = [(q, t) for q in range(UNITS) for r in range(R) for t in PLAN[r]]
NCONV = len(CONV_ORDER)


def tap_numbers():
    found, n = {}, 0
    for q in range(UNITS):
        for r in range(R):
            for shift in range(1, KW):
                for t in PLAN[r]:
                    found[q, t, shift] = n
                    n += 1
    return found


TAP = tap_numbers()
NTAP = len(TAP)

LAG_SSD, LAG_M, LAG_STATE, LAG_Y, LAG_SUM, LAG_VAR, LAG_FACTOR, LAG_NORM, LAG_OUT = 4, 5, 6, 7, 8, 12, 13, 14, 15
QUANT_SLOT = 7
XN_SLOT = 7
XO_SLOT = LAG_OUT


def back(b, n, lag):
    m = n - lag
    while m < 0:
        b, m = b - 1, m + SLOTS
    if isinstance(b, int) and not 0 <= b < NB:
        return None
    return b, m


def following(b):
    return None if isinstance(b, int) and b + 1 >= NB else b + 1


def misc_plan():
    plan = []
    for q in range(UNITS):
        for r in range(R):
            n = 4 * q + r
            plan.append((n, "xt", LAG_SSD, 0))
            plan.append((n, "s", LAG_STATE, 0))
            if r == 0:
                plan.append((n, "var", LAG_VAR, 0))
                plan += [(n, "cb", LAG_SSD, 0), (n, "cb", LAG_SSD, 1)]
            if r == 1:
                plan.append((n, "bt", LAG_M, 0))
                plan.append((n, "rbc", LAG_FACTOR, 0))
            if n == XO_SLOT:
                plan.append((n, "xo", SLOTS, 0))
            if n == XN_SLOT:
                plan.append((n, "xn", 0, 0))
    return plan


MISC = misc_plan()
PROJ = [(4 * q + r, t) for q in range(UNITS) for r in range(R) for t in PLAN[r] + ["z"]]
assert len(PROJ) % 2 == 0


def proj_position(n, t):
    return PROJ.index((n, t))
assert len(MISC) % 2 == 0


def build(nc, hid_in, norm_w, in_w, conv_w, conv_b, dt_bias, a_log, d_skip, gnorm_w, out_w,
          ln1_g, ln1_b, w1, b1, ln2_g, ln2_b, w2, b2, out):
    ctx = ExitStack()
    with ctx:
        def sb(name, shape, dt=F32):
            return ctx.enter_context(nc.sbuf_tensor(name, shape, dt))

        def pb(name, shape, dt=F32):
            return ctx.enter_context(nc.psum_tensor(name, shape, dt))

        def sem(name):
            return ctx.enter_context(nc.semaphore(name))

        ident4 = sb("ident4", [P, S])
        ident = ident4[:, 0:P]
        ident_b = sb("ident_b", [P, P], BF16)
        sel = sb("sel", [96, SLOTS, 2 * P], BF16)
        blockones = sb("blockones", [P, 2])
        neghalf = sb("neghalf", [P, 8])
        inv_dm = sb("inv_dm", [P, 8])
        eps_c = sb("eps_c", [P, 8])
        one_c = sb("one_c", [P, 1])
        w_hi = sb("w_hi", [P, UNITS, TILES, P], F32R)
        w_lo = sb("w_lo", [P, UNITS, TILES, P], F32R)
        wdt_hi = sb("wdt_hi", [P, H], F32R)
        wdt_lo = sb("wdt_lo", [P, H], F32R)
        w_out = sb("w_out", [P, SLOTS, DM])
        nw = sb("nw", [P, 1])
        cw = sb("cw", [P, UNITS, CONVS, KW])
        cb_bias = sb("cb_bias", [P, UNITS, CONVS])
        dskip = sb("dskip", [P, SLOTS])
        gnw = sb("gnw", [P, SLOTS])
        dtb = sb("dtb", [P, H])
        alog = sb("alog", [P, H])
        aexp = sb("aexp", [P, 2, H])
        w1t = sb("w1t", [P, HID])
        w2t = sb("w2t", [P, HID])
        fg1 = sb("fg1", [P, 1])
        fb1 = sb("fb1", [P, 1])
        fg2 = sb("fg2", [P, HT])
        fb2 = sb("fb2", [P, HT])
        dt_all = sb("dt_all", [P, NCH, H])
        da_parts = sb("da_parts", [96, NB * S], BF16)
        pr_parts = sb("pr_parts", [96, NB * S], BF16)
        xn_dram = nc.dram_tensor("xn_scratch", (P, NCH, DM), F32, kind="Internal").ap()
        res_dram = nc.dram_tensor("residual_scratch", (P, NCH, DM), F32, kind="Internal").ap()
        x1_dram = nc.dram_tensor("x1_scratch", (P, NCH, DM), F32, kind="Internal").ap()
        xn_hi = sb("xn_hi", [P, 2, S], F32R)
        xn_lo = sb("xn_lo", [P, 2, S], F32R)
        xn_stage = sb("xn_stage", [P, CH, DM])
        r_stage = sb("r_stage", [P, CH, DM])
        conv = sb("conv", [P, 4, S])
        bt = sb("bt", [P, CH, P])
        chan = sb("chan", [P, 2 * CONVS - 1, S])
        gate = sb("gate", [P, R, S])
        cbs = sb("cbs", [P, 2, S])
        lm = sb("lm", [P, 4, 2, S])
        xdt = sb("xdt", [P, 4, S])
        cdec = sb("cdec", [P, 4, S])
        pend = sb("pend", [P, 4, CH])
        xw = sb("xw", [P, 2, CH - 1, P])
        hpk = sb("hpk", [P, 2, CH - 1, NS])
        hbd = sb("hbd", [P, 2, CH - 1, P])
        gated = sb("gated", [P, 2, R, S])
        sq = sb("sq", [P, S])
        ssum = sb("ssum", [P, 2, S])
        rbs = sb("rbs", [P, S])
        vtok = sb("vtok", [P, 2 * CH])
        rtok = sb("rtok", [P, 2 * CH])
        rexp = sb("rexp", [P, 2 * CH, HP])
        ocm = rexp[:, :, :].rearrange("p c d -> p (c d)")

        def xn_of(ring, b):
            return ring[:, bass.ds(b % 2, 1), :].rearrange("p a s -> p (a s)")

        def chan_of(q, t):
            return 0 if t == 0 else 1 + (CONVS - 1) * (q % 2) + t - 1

        bank = [pb(f"bank{i}", [P, S]) for i in range(8)]
        proj_bank, bc_bank, misc_bank, y_bank, out_bank = bank[0:2], bank[2:4], bank[4:6], bank[6], bank[7]

        raw_w = lm[:, :, :, :].rearrange("p a b s -> p (a b s)")
        raw_w2 = gated[:, :, :, :].rearrange("p a b s -> p (a b s)")[:, 2048:2048 + DPROJ - 4096]
        work = chan[:, :, :].rearrange("p a s -> p (a s)")
        flat = [t.rearrange("p a s -> p (a s)") for t in (gate[:, :, :], cdec[:, :, :], conv[:, :, :])]
        gflat = gated[:, :, :, :].rearrange("p a b s -> p (a b s)")
        halves = [t[:, at:at + 1024] for t, at in ((gflat, 0), (gflat, 1024), (work, 4096), (flat[2], 1024),
                                                   (flat[0], 0), (flat[0], 1024), (flat[1], 0), (flat[1], 1024))]
        by_chunk = [t.rearrange("p (c d) -> p c d", d=DM) for t in halves]
        xg, xc = by_chunk[0:4], by_chunk[4:8]
        wk = [work[:, 1024 * i:1024 * i + 1024] for i in range(4)] + [halves[7], raw_w[:, 0:1024]]
        stat = conv[:, :, :].rearrange("p a s -> p (a s)")
        da_split = xdt[:, :, :].rearrange("p a s -> p (a s)").bitcast(BF16)[:, 0:3072]
        prod = raw_w[0:H, :]
        zeros = bt[0:H, 0, :]
        ones = cdec[:, 0, 0:P]

        w_loaded = sem("w_loaded")
        wo_loaded = sem("wo_loaded")
        small_loaded = sem("small_loaded")
        x_loaded = sem("x_loaded")
        consts = sem("consts")
        mean_sum = sem("mean_sum")
        cent = sem("cent")
        sqd = sem("sqd")
        sq_sum = sem("sq_sum")
        rr_pool = sem("rr_pool")
        t_done = sem("t_done")
        xn_done = sem("xn_done")
        xn_t = sem("xn_t")
        xnhi = sem("xnhi")
        xnlo = sem("xnlo")
        resid = sem("resid")
        w_norm = sem("w_norm")
        whi = sem("whi")
        wlo = sem("wlo")
        w_split_dt = sem("w_split_dt")
        dt_mm = sem("dt_mm")
        dt_raw = sem("dt_raw")
        dtstep_v = sem("dtstep_v")
        dtstep_a = sem("dtstep_a")
        da_split_done = sem("da_split_done")
        da_t = sem("da_t")
        da_copied = sem("da_copied")
        pr_t = sem("pr_t")
        pr_split = sem("pr_split")
        wo_scaled = sem("wo_scaled")
        proj_ready = sem("proj_ready")
        z_ready = sem("z_ready")
        xnt_ready = sem("xnt_ready")
        staged = sem("staged")
        res_stored = sem("res_stored")
        xn_stored = sem("xn_stored")
        res_loaded = sem("res_loaded")
        x1_stored = sem("x1_stored")
        hi_done = sem("hi_done")
        lo_done = sem("lo_done")
        acc_init = sem("acc_init")
        tap = sem("tap")
        silu_done = sem("silu_done")
        gate_done = sem("gate_done")
        cb_ready = sem("cb_ready")
        cb_copied = sem("cb_copied")
        bt_ready = sem("bt_ready")
        bt_copied = sem("bt_copied")
        xt_ready = sem("xt_ready")
        xdt_done = sem("xdt_done")
        xw_done = sem("xw_done")
        bc_ready = sem("bc_ready")
        scanned = sem("scanned")
        cdec_done = sem("cdec_done")
        pend_done = sem("pend_done")
        m_done = sem("m_done")
        s_ready = sem("s_ready")
        hstep = sem("hstep")
        hbd_done = sem("hbd_done")
        y_ready = sem("y_ready")
        skipped = sem("skipped")
        gated_done = sem("gated_done")
        sq_done = sem("sq_done")
        ssum_step = sem("ssum_step")
        var_ready = sem("var_ready")
        var_copied = sem("var_copied")
        rstd_done = sem("rstd_done")
        rexp_done = sem("rexp_done")
        rbc_ready = sem("rbc_ready")
        rbc_copied = sem("rbc_copied")
        normed = sem("normed")
        out_copied = sem("out_copied")
        xo_ready = sem("xo_ready")
        x1_done = sem("x1_done")
        pr_scan = sem("pr_scan")
        dt_aux = sem("dt_aux")
        out_step = sem("out_step")
        f_loaded = [sem("f_loaded_even"), sem("f_loaded_odd")]
        f_xstats = sem("f_xstats")
        f_xaggr = sem("f_xaggr")
        f_xeps = sem("f_xeps")
        f_xr = sem("f_xr")
        f_xn = sem("f_xn")
        f_xb = sem("f_xb")
        f_t = sem("f_t")
        f_tcopy = sem("f_tcopy")
        f_mm1 = sem("f_mm1")
        f_h = sem("f_h")
        f_gelu = sem("f_gelu")
        f_hstats = sem("f_hstats")
        f_haggr = sem("f_haggr")
        f_heps = sem("f_heps")
        f_hr = sem("f_hr")
        f_nrm = sem("f_nrm")
        f_nt = sem("f_nt")
        f_ntcopy = sem("f_ntcopy")
        f_mm2 = sem("f_mm2")
        f_out = sem("f_out")
        f_stored = sem("f_stored")
        b_load = sem("b_load")
        q_load = sem("q_load")
        q_ones = sem("q_ones")
        q_abs = sem("q_abs")
        q_tot = sem("q_tot")
        q_step = sem("q_step")
        q_t = sem("q_t")
        q_copied = sem("q_copied")

        def after(eng, s, per, b, i):
            if isinstance(b, int) and b * per + i + 1 <= 0:
                return
            eng.wait_ge(s, b * per + (i + 1))

        def raw_t(i):
            return work[:, 1024 * i:1024 * i + 1024].rearrange("p (c d) -> p c d", d=DM)

        qw, qt = conv[:, 0:2, :], conv[:, 2:4, :]
        ones = xn_stage[:, 0, :]
        qs = xn_stage[:, 1, :]
        fx = cbs[:, :, :].rearrange("p a (c d) -> p a c d", d=DM)
        fres = gflat.rearrange("p (c d) -> p c d", d=DM)
        fxn = xdt[:, 0, :].rearrange("p (c d) -> p c d", d=DM)
        fxt = xdt[:, 1, :]
        bias1 = xdt[:, 2, :]
        bias2 = xdt[:, 3, 0:DM]
        fh = gate[:, :, :]
        fge = lm[:, :, :, :].rearrange("p (k a) b s -> p k (a b) s", k=2)
        fnt = cdec[:, :, :]
        fst = sq[:, :]
        bn_x = fst[:, 0:6 * CH].rearrange("p (c k) -> p c k", k=6)
        mv_x = fst[:, 32:32 + 2 * CH].rearrange("p (c k) -> p c k", k=2)
        ve_x, r_x = fst[:, 48:48 + CH], fst[:, 64:64 + CH]
        bn_h = fst[:, 128:128 + 6 * CH].rearrange("p (c k) -> p c k", k=6)
        mv_h = fst[:, 160:160 + 2 * CH].rearrange("p (c k) -> p c k", k=2)
        ve_h, r_h = fst[:, 176:176 + CH], fst[:, 192:192 + CH]
        h_bank = (bank[1], bank[2], bank[6], bank[7])

        def ffn_steps(step, loop):
            for i in range(-1, 2):
                step(i, i % 2, i // 2)
            with loop(1, NB // 2 - 1) as k:
                step(k * 2, 0, k)
                step(k * 2 + 1, 1, k)
            for i in range(NB - 2, NB + 2):
                step(i, i % 2, i // 2)

        def there(i, shift):
            return not isinstance(i, int) or 0 <= i + shift < NB

        def reach(eng, s, value, per, more=0):
            if isinstance(value, int) and value * per + more <= 0:
                return
            eng.wait_ge(s, value * per + more)

        def tile_sources(q):
            found = []
            bsrc = raw_w2[:, P * q:P * q + P]
            csrc = raw_w2[:, G * NS + P * q:G * NS + P * q + P]
            found.append((0, (bsrc, lambda w: w[:, q, 0, :])))
            found.append((1, (csrc, lambda w: w[:, q, 1, :])))
            for t0, at in ((2, X0), (CONVS, Z0)):
                src = raw_w[:, at + 512 * q:at + 512 * q + 512].rearrange("p (a r d) -> p r a d", a=2, r=R)
                found.append((t0, (src, lambda w, t0=t0: w[:, q, t0:t0 + R, :].rearrange("p r (a d) -> p r a d", a=2))))
            return found

        NSMALL = 3 + 2 * UNITS * 4 + 4 + 4

        def misc_position(kind, n, k=0):
            return [j for j, x in enumerate(MISC) if x[0] == n and x[1] == kind][k]

        def misc_of(kind, n, k=0):
            return misc_bank[misc_position(kind, n, k) % 2][:, :]

        block = ctx.enter_context(nc.Block())

        @block.sync
        def _(sp):
            x_v = hid_in.rearrange("b (c p) d -> p (b c) d", p=P)
            for i in range(4):
                sp.dma_start(xg[i], x_v[:, 8 * i:8 * i + 8, :]).then_inc(x_loaded, 16)
            sp.dma_start(raw_w, in_w[:, 0:4096]).then_inc(w_loaded, 16)
            sp.dma_start(raw_w2, in_w[:, 4096:DPROJ]).then_inc(w_loaded, 16)
            with nc.allow_non_contiguous_dma(reason="small parameters"):
                sp.dma_start(nw[:, :], norm_w.rearrange("(p o) -> p o", o=1)).then_inc(small_loaded, 16)
                sp.dma_start(dtb[:, :], dt_bias.rearrange("(o h) -> o h", o=1).broadcast_to([P, H])).then_inc(small_loaded, 16)
                sp.dma_start(alog[:, :], a_log.rearrange("(o h) -> o h", o=1).broadcast_to([P, H])).then_inc(small_loaded, 16)
                for a in range(2):
                    half = slice(HP * a, HP * a + HP)
                    for q in range(UNITS):
                        sp.dma_start(cw[half, q, 2:CONVS, :],
                                     conv_w[0:DI].rearrange("(q a r p) k -> q a p r k", q=UNITS, a=2, r=R)[q, a]).then_inc(small_loaded, 16)
                        sp.dma_start(cb_bias[half, q, 2:CONVS],
                                     conv_b[0:DI].rearrange("(q a r p) -> q a p r", q=UNITS, a=2, r=R)[q, a]).then_inc(small_loaded, 16)
                        sp.dma_start(gnw[half, R * q:R * q + R],
                                     gnorm_w.rearrange("(q a r p) -> q a p r", q=UNITS, a=2, r=R)[q, a]).then_inc(small_loaded, 16)
                        sp.dma_start(dskip[half, R * q:R * q + R],
                                     d_skip.rearrange("(q a r) -> q a r", q=UNITS, a=2)[q, a:a + 1].broadcast_to([HP, R])).then_inc(small_loaded, 16)
                for t, at in ((0, DI), (1, DI + G * NS)):
                    sp.dma_start(cw[:, :, t, :], conv_w[at:at + G * NS].rearrange("(q p) k -> p q k", p=P)).then_inc(small_loaded, 16)
                    sp.dma_start(cb_bias[:, :, t], conv_b[at:at + G * NS].rearrange("(q p) -> p q", p=P)).then_inc(small_loaded, 16)
                sp.dma_start(fg1[:, :], ln1_g.rearrange("(p o) -> p o", o=1)).then_inc(small_loaded, 16)
                sp.dma_start(fb1[:, :], ln1_b.rearrange("(p o) -> p o", o=1)).then_inc(small_loaded, 16)
                sp.dma_start(fg2[:, :], ln2_g.rearrange("(t p) -> p t", p=P)).then_inc(small_loaded, 16)
                sp.dma_start(fb2[:, :], ln2_b.rearrange("(t p) -> p t", p=P)).then_inc(small_loaded, 16)
            for a in range(2):
                src = out_w.rearrange("(q a r p) d -> a p q r d", q=UNITS, a=2, r=R)[a]
                for q in range(UNITS):
                    sp.dma_start(w_out[HP * a:HP * a + HP, R * q:R * q + R, :], src[:, q]).then_inc(wo_loaded, 16)
            for i in range(4):
                sp.wait_ge(resid, i + 1)
                sp.dma_start(res_dram[:, 8 * i:8 * i + 8, :], xg[i]).then_inc(res_stored, 16)
                sp.wait_ge(xn_done, i + 1)
                sp.dma_start(xn_dram[:, 8 * i:8 * i + 8, :], xc[i]).then_inc(xn_stored, 16)
            sp.wait_ge(res_stored, 64)
            sp.wait_ge(xn_stored, 64)

            def batch(b):
                if following(b) is not None:
                    sp.wait_ge(xnt_ready, b + 1)
                    sp.dma_start(xn_stage[:, :, :], xn_dram[:, bass.ds((b + 1) * CH, CH), :]).then_inc(staged, 16)
                if not (isinstance(b, int) and b == 0):
                    sp.wait_ge(x1_done, b)
                    sp.dma_start(x1_dram[:, bass.ds((b - 1) * CH, CH), :], r_stage[:, :, :]).then_inc(x1_stored, 16)
                    sp.wait_ge(x1_stored, b * 16)
                if not (isinstance(b, int) and b == NB):
                    sp.dma_start(r_stage[:, :, :], res_dram[:, bass.ds(b * CH, CH), :]).then_inc(res_loaded, 16)

            batch(0)
            with sp.Fori(1, NB - 1) as b:
                batch(b)
            batch(NB - 1)
            sp.wait_ge(silu_done, NB * NCONV)
            sp.dma_start(qw[:, 0, :].rearrange("p (t d) -> p t d", d=DM), w1.rearrange("(t p) d -> p t d", p=P)).then_inc(q_load, 16)
            sp.dma_start(qw[:, 1, :], w2).then_inc(q_load, 16)
            batch(NB)
            out_v = out.rearrange("b (c p) d -> b p c d", p=P)

            def store(j):
                sp.wait_ge(f_out, j + 1)
                sp.dma_start(out_v[bass.ds(j, 1)].rearrange("b p c d -> p (b c) d"), fres[:, bass.ds(j * CH, CH), :]).then_inc(f_stored, 16)

            def step(i, par, k):
                if there(i, 1):
                    reach(sp, f_xn, i, CH)
                    sp.dma_start(fx[:, 1 - par, :, :], x1_dram[:, bass.ds((i + 1) * CH, CH), :]).then_inc(f_loaded[1 - par], 16)
                if isinstance(i, int) and i == -1:
                    sp.dma_start(bias1[:, :], b1.rearrange("(o h) -> o h", o=1).broadcast_to([P, HID])).then_inc(b_load, 16)
                if isinstance(i, int) and i == 0:
                    sp.dma_start(bias2[:, :], b2.rearrange("(o h) -> o h", o=1).broadcast_to([P, DM])).then_inc(b_load, 16)
                    sp.dma_start(fres, x1_dram).then_inc(b_load, 16)
                if there(i, -2):
                    store(i - 2)

            ffn_steps(step, sp.Fori)
            sp.wait_ge(f_stored, 16 * NB)

        @block.gpsimd
        def _(gp):
            gp.memset(ident4[:, :], 0.0).then_inc(consts, 1)
            gp.memset(ident_b[:, :], 0.0).then_inc(consts, 1)
            gp.memset(sel[:, :, :], 0.0).then_inc(consts, 1)
            gp.memset(neghalf[:, :], -0.5).then_inc(consts, 1)
            gp.memset(inv_dm[:, :], 1.0 / DM).then_inc(consts, 1)
            gp.memset(eps_c[:, :], EPS).then_inc(consts, 1)
            gp.memset(one_c[:, :], 1.0).then_inc(consts, 1)
            gp.memset(zeros, 0.0).then_inc(consts, 1)
            gp.memset(blockones[:, :], 0.0).then_inc(consts, 1)
            gp.memset(hbd[:, :, :, :], 0.0).then_inc(consts, 1)
            gp.wait_ge(consts, 10)
            gp.affine_select(out=ident_b[:, :], in_=ident_b[:, :], compare_op=ALU.not_equal, fill=1.0, base=0,
                             pattern=[[-1, P]], channel_multiplier=1).then_inc(consts, 1)
            i4 = ident4[:, :].rearrange("p (c i) -> p c i", c=CH)
            gp.affine_select(out=i4, in_=i4, compare_op=ALU.not_equal, fill=1.0, base=0,
                             pattern=[[0, CH], [-1, P]], channel_multiplier=1).then_inc(consts, 1)
            for k in range(3):
                gp.wait_ge(consts, 12 + UNITS * k)
                part = sel[32 * k:32 * k + 32, :, :]
                part = part.rearrange("k (q r) (a c) -> k q r a c", r=R, a=2)
                for q in range(UNITS):
                    gp.affine_select(out=part[:, q], in_=part[:, q], compare_op=ALU.not_equal, fill=1.0, base=-8 * q,
                                     pattern=[[-1, R], [-4, 2], [0, P]], channel_multiplier=1).then_inc(consts, 1)
            for a in range(2):
                gp.wait_ge(consts, 12 + 3 * UNITS + a)
                gp.memset(blockones[HP * a:HP * a + HP, a:a + 1], 1.0).then_inc(consts, 1)
            gp.wait_ge(consts, 26)

            def rsqrt_chain(s, n0, vsum, r1, r2, rr, width):
                inv, eps, exponent = inv_dm[:, 0:width], eps_c[:, 0:width], neghalf[:, 0:width]
                gp.tensor_tensor(r2, vsum, inv, ALU.mult).then_inc(s, 1)
                gp.wait_ge(s, n0 + 1)
                gp.tensor_tensor(r1, r2, eps, ALU.add).then_inc(s, 1)
                gp.wait_ge(s, n0 + 2)
                gp.tensor_tensor(r1, r1, exponent, ALU.pow).then_inc(s, 1)
                gp.wait_ge(s, n0 + 3)
                gp.tensor_tensor(rr, r1, r1, ALU.mult).then_inc(s, 1)
                gp.wait_ge(s, n0 + 4)
                gp.tensor_tensor(r2, rr, r2, ALU.mult).then_inc(s, 1)
                gp.wait_ge(s, n0 + 5)
                gp.tensor_tensor(r2, r2, eps, ALU.add).then_inc(s, 1)
                gp.wait_ge(s, n0 + 6)
                gp.tensor_tensor(r2, r2, exponent, ALU.pow).then_inc(s, 1)
                gp.wait_ge(s, n0 + 7)
                gp.tensor_tensor(rr, r1, r2, ALU.mult).then_inc(s, 1)

            for i in range(4):
                gp.wait_ge(sq_sum, i + 1)
                rsqrt_chain(rr_pool, 8 * i, stat[:, 64 + 8 * i:72 + 8 * i],
                            stat[:, 192 + 8 * i:200 + 8 * i], stat[:, 256 + 8 * i:264 + 8 * i],
                            stat[:, 320 + 8 * i:328 + 8 * i], 8)
            for i in range(4):
                gp.wait_ge(t_done, i + 1)
                gp.tensor_tensor(xg[i], xg[i], raw_t(i), ALU.add).then_inc(resid, 1)
            gp.wait_ge(pr_split, 5)
            gp.wait_ge(xnlo, NB)

            def slot(b, n):
                q, r = divmod(n, R)
                if back(b, n, LAG_NORM) is not None:
                    bb, m = back(b, n, LAG_NORM)
                    v = m // R
                    after(gp, rbc_copied, UNITS, bb, v)
                    after(gp, sq_done, SLOTS, bb, m)
                    gp.tensor_tensor(gated[:, v % 2, m % R, :], gated[:, v % 2, m % R, :], rbs[:, :], ALU.mult).then_inc(normed, 1)
                ssd = back(b, n, LAG_M)
                if ssd is not None:
                    bb, m = ssd
                    mq, mr = divmod(m, R)
                    after(gp, xdt_done, SLOTS, bb, m)
                    after(gp, scanned, 2 * SLOTS, bb, 2 * m + 1)
                    after(gp, s_ready, SLOTS, bb, m - 2)
                    for a in range(2):
                        ldec = (lm[:, mr, a, :].rearrange("p (c i) -> p c i", c=CH)[:, 0:CH - 1, P - 1:P]
                                .broadcast_to([P, CH - 1, HP]))
                        gp.tensor_tensor(xw[:, mr % 2, :, HP * a:HP * a + HP],
                                         xdt[:, mr, :].rearrange("p (c d) -> p c d", c=CH)[:, 0:CH - 1, HP * a:HP * a + HP],
                                         ldec, ALU.mult).then_inc(xw_done, 1)
                    after(gp, cb_copied, 2 * UNITS, bb, 2 * mq + 1)
                    after(gp, xw_done, 2 * SLOTS, bb, 2 * m + 1)
                    gp.tensor_tensor(lm[:, mr, :, :], lm[:, mr, :, :], cbs[:, :, :], ALU.mult).then_inc(m_done, 1)
                yy = back(b, n, LAG_SUM)
                if yy is not None and yy[1] % R > 0:
                    bb, m = yy
                    after(gp, sq_done, SLOTS, bb, m)
                    after(gp, ssum_step, 3 * UNITS, bb, 3 * (m // R) + m % R - 2)
                    gp.tensor_tensor(ssum[:, m // R % 2, :], ssum[:, m // R % 2, :], sq[:, :], ALU.add).then_inc(ssum_step, 1)
                if r == 0 and back(b, n, LAG_VAR) is not None:
                    bb, m = back(b, n, LAG_VAR)
                    v = m // R
                    after(gp, var_copied, UNITS, bb, v)
                    after(gp, rexp_done, UNITS, bb, v - 1)
                    gp.tensor_tensor(rtok[:, :], vtok[:, :], neghalf[:, 0:2 * CH], ALU.pow).then_inc(rstd_done, 1)

            for n in range(SLOTS):
                slot(0, n)
            with gp.Fori(1, NB - 1) as b:
                for n in range(SLOTS):
                    slot(b, n)
            for b in (NB - 1, NB):
                for n in range(SLOTS):
                    slot(b, n)

            gp.wait_ge(xo_ready, NB)

            def step(i, par, k):
                if there(i, 1):
                    reach(gp, f_xaggr, i, CH, 2 * CH)
                    gp.tensor_tensor(ve_x, mv_x[:, :, 1], eps_c[:, 0:CH], ALU.add).then_inc(f_xeps, 1)
                    reach(gp, f_xeps, i, 1, 2)
                    reach(gp, f_xn, i, CH, CH)
                    gp.tensor_tensor(r_x, ve_x, neghalf[:, 0:CH], ALU.pow).then_inc(f_xr, 1)
                if there(i, -1):
                    reach(gp, f_haggr, i, CH)
                    gp.tensor_tensor(ve_h, mv_h[:, :, 1], eps_c[:, 0:CH], ALU.add).then_inc(f_heps, 1)
                    reach(gp, f_heps, i, 1)
                    reach(gp, f_nrm, i, CH, -CH)
                    gp.tensor_tensor(r_h, ve_h, neghalf[:, 0:CH], ALU.pow).then_inc(f_hr, 1)
                if isinstance(i, int) and i == 0:
                    gp.wait_ge(b_load, 48)
                    gp.tensor_tensor(fres, fres, bias2[:, :].unsqueeze(1).broadcast_to([P, NCH, DM]), ALU.add).then_inc(f_xb, 1)

            ffn_steps(step, gp.Fori)

        @block.scalar
        def _(act):
            for i in range(4):
                act.wait_ge(cent, i + 1)
                act.activation(raw_t(i), xc[i], ACT.Square).then_inc(sqd, 1)
            act.wait_ge(w_norm, 1)
            act.activation(wdt_hi[:, :], raw_w2[:, DT0 - 4096:DT0 - 4096 + H], ACT.Copy).then_inc(w_split_dt, 1)
            act.wait_ge(w_norm, 2)
            for q in range(UNITS):
                for t0, src in tile_sources(q):
                    act.activation(src[1](w_hi), src[0], ACT.Copy).then_inc(whi, 1)
            for b in range(NB):
                act.wait_ge(xn_t, b + 1)
                if b >= 2:
                    act.wait_ge(dt_mm, b - 1)
                act.activation(xn_hi[:, b % 2, :], bank[b % 2][:, :], ACT.Copy).then_inc(xnhi, 1)
            act.wait_ge(dtstep_v, 2)
            act.activation(aexp[:, :, :], aexp[:, :, :], ACT.Exp).then_inc(dtstep_a, 1)
            act.wait_ge(dtstep_v, 4)
            act.activation(wk[1], wk[1], ACT.Exp, scale=-1.0).then_inc(dtstep_a, 1)
            act.wait_ge(dtstep_v, 20)
            act.activation(wk[4], wk[4], ACT.Exp, scale=-1.0).then_inc(dtstep_a, 1)
            for i in range(NB):
                act.wait_ge(da_t, i + 1)
                act.activation(da_parts[:, S * i:S * i + S], bank[i % 2][0:96, 0:S // 2].bitcast(BF16), ACT.Copy).then_inc(da_copied, 1)
            act.wait_ge(wo_loaded, 16 * 2 * UNITS)
            act.wait_ge(small_loaded, NSMALL * 16)
            for k in range(SLOTS):
                act.activation(w_out[:, k, :], w_out[:, k, :], ACT.Copy, scale=gnw[:, k:k + 1]).then_inc(wo_scaled, 1)
            act.wait_ge(pr_split, 5)
            act.wait_ge(res_stored, 64)
            act.wait_ge(xnt_ready, 1)
            act.activation(xn_hi[:, 0, :], bank[6][:, :], ACT.Copy).then_inc(hi_done, 1)

            def slot(b, n):
                q, r = divmod(n, R)
                real = not (isinstance(b, int) and b == NB)
                st = back(b, n, LAG_STATE + 1)
                if st is not None:
                    bb, m = st
                    after(act, hstep, 3 * SLOTS, bb, 3 * m + 2)
                    after(act, y_ready, SLOTS, bb, m - 2)
                    for a in range(2):
                        half = slice(HP * a, HP * a + HP)
                        act.activation(hbd[half, m % 2, :, half], hpk[half, m % 2, :, :], ACT.Copy).then_inc(hbd_done, 1)
                if real:
                    for t in PLAN[r]:
                        ci = CONV_ORDER.index((q, t))
                        after(act, proj_ready, NCONV, b, ci)
                        after(act, silu_done, NCONV, b, ci - 4)
                        act.activation(conv[:, ci % 4, :], proj_bank[proj_position(n, t) % 2][:, :], ACT.Identity,
                                       scale=cw[:, q, t, KW - 1:KW], bias=cb_bias[:, q, t:t + 1]).then_inc(acc_init, 1)
                prev = back(b, n, 1)
                if prev is not None:
                    bb, m = prev
                    pq, prr = divmod(m, R)
                    for t in PLAN[prr]:
                        i = CONV_ORDER.index((pq, t))
                        after(act, tap, NTAP, bb, TAP[pq, t, KW - 1])
                        if t == 0:
                            after(act, bt_ready, UNITS, bb, pq - 1)
                            after(act, cb_ready, 2 * UNITS, bb, 2 * (pq - 1) + 1)
                        elif t == 1:
                            after(act, cdec_done, SLOTS, bb, 4 * (pq - 2) + 3)
                        else:
                            after(act, skipped, SLOTS, bb, 4 * (pq - 2) + t - 2)
                        act.activation(chan[:, chan_of(pq, t), :], conv[:, i % 4, :], ACT.Silu).then_inc(silu_done, 1)
                yy = back(b, n, LAG_SUM)
                if yy is not None:
                    bb, m = yy
                    after(act, gated_done, SLOTS, bb, m)
                    v = m // R
                    if m % R == 0:
                        after(act, var_ready, UNITS, bb, v - 2)
                        after(act, ssum_step, 3 * UNITS, bb, 3 * v - 1)
                        dst = ssum[:, v % 2, :]
                    else:
                        after(act, ssum_step, 3 * UNITS, bb, 3 * v + m % R - 2)
                        dst = sq[:, :]
                    act.activation(dst, gated[:, v % 2, m % R, :], ACT.Square).then_inc(sq_done, 1)
                if r == 1 and back(b, n, LAG_FACTOR) is not None:
                    bb, m = back(b, n, LAG_FACTOR)
                    v = m // R
                    after(act, rstd_done, UNITS, bb, v)
                    after(act, rbc_ready, UNITS, bb, v - 1)
                    act.activation(rexp[:, :, :], rtok[:, :].unsqueeze(2).broadcast_to([P, 2 * CH, HP]), ACT.Copy).then_inc(rexp_done, 1)
                ssd = back(b, n, LAG_SSD)
                if n == XN_SLOT and following(b) is not None:
                    after(act, xnt_ready, 1, b, 1)
                    act.activation(xn_of(xn_hi, following(b)), misc_of("xn", n), ACT.Copy).then_inc(hi_done, 1)
                if n == XO_SLOT - 1 and back(b, n, SLOTS) is not None:
                    bb, _ = back(b, n, SLOTS)
                    after(act, out_step, SLOTS, bb, SLOTS - 1)
                    after(act, xo_ready, 1, bb, -1)
                    act.activation(ocm[:, :], out_bank[:, :], ACT.Copy).then_inc(out_copied, 1)
                if r == 0 and back(b, n, LAG_VAR) is not None:
                    bb, m = back(b, n, LAG_VAR)
                    v = m // R
                    after(act, var_ready, UNITS, bb, v)
                    after(act, rstd_done, UNITS, bb, v - 1)
                    act.activation(vtok[:, :], misc_of("var", n)[:, 0:2 * CH], ACT.Identity, scale=1.0 / (DI // G),
                                   bias=eps_c[:, 0:1]).then_inc(var_copied, 1)
                if r == 1 and back(b, n, LAG_M) is not None:
                    bb, m = back(b, n, LAG_M)
                    v = m // R
                    after(act, bt_ready, UNITS, bb, v)
                    after(act, s_ready, SLOTS, bb, m - 1)
                    act.activation(bt[:, :, :], misc_of("bt", n).rearrange("p (c d) -> p c d", c=CH), ACT.Copy).then_inc(bt_copied, 1)
                if ssd is not None:
                    bb, m = ssd
                    after(act, z_ready, SLOTS, bb, m)
                    after(act, gated_done, SLOTS, bb, m - 4)
                    act.activation(gate[:, m % R, :], proj_bank[proj_position(n, "z") % 2][:, :], ACT.Silu).then_inc(gate_done, 1)
                if r == 0 and ssd is not None:
                    bb, m = ssd
                    v = m // R
                    for a in range(2):
                        after(act, cb_ready, 2 * UNITS, bb, 2 * v + a)
                        after(act, m_done, SLOTS, bb, m - 1)
                        act.activation(cbs[:, a, :], misc_of("cb", n, a), ACT.Copy).then_inc(cb_copied, 1)
                if r == 1 and back(b, n, LAG_FACTOR) is not None:
                    bb, m = back(b, n, LAG_FACTOR)
                    v = m // R
                    after(act, rbc_ready, UNITS, bb, v)
                    after(act, normed, SLOTS, bb, 4 * v - 1)
                    act.activation(rbs[:, :], misc_of("rbc", n), ACT.Copy).then_inc(rbc_copied, 1)

            for n in range(SLOTS):
                slot(0, n)
            with act.Fori(1, NB - 1) as b:
                for n in range(SLOTS):
                    slot(b, n)
            for b in (NB - 1, NB):
                for n in range(SLOTS):
                    slot(b, n)
                    if (b, n) == (NB, QUANT_SLOT):
                        act.wait_ge(q_load, 32)
                        for k in range(2):
                            act.activation(qt[:, k, :], qw[:, k, :], ACT.Abs, accum_out=qs[:, k:k + 1]).then_inc(q_abs, 1)

            for k in range(2):
                act.wait_ge(q_t, k + 1)
                act.activation((w1t, w2t)[k][:, :], bank[k][:, :], ACT.Copy).then_inc(q_copied, 1)

            def step(i, par, k):
                if there(i, 0):
                    for c in range(CH):
                        reach(act, f_h, i, CH, c + 1)
                        reach(act, f_nt, i, HT, -HT)
                        act.activation(fge[:, par, c, :], fh[:, c, :], ACT.Gelu).then_inc(f_gelu, 1)
                if there(i, 1):
                    reach(act, f_t, i, 1, 2)
                    reach(act, f_mm1, i, CH, CH)
                    act.activation(fxt, bank[0][:, :], ACT.Identity, scale=fg1[:, :], bias=fb1[:, :]).then_inc(f_tcopy, 1)
                if there(i, -1):
                    for t in range(HT):
                        reach(act, f_nt, i, HT, t + 1 - HT)
                        reach(act, f_mm2, i, 1, -1)
                        act.activation(fnt[:, t, :], bank[3 + t % 2][:, :], ACT.Identity, scale=fg2[:, t:t + 1],
                                       bias=fb2[:, t:t + 1]).then_inc(f_ntcopy, 1)

            act.wait_ge(xo_ready, NB)
            ffn_steps(step, act.Fori)

        @block.vector
        def _(dve):
            V = nc.vector
            dve.wait_ge(x_loaded, 64)
            for i in range(4):
                V.tensor_reduce(stat[:, 8 * i:8 * i + 8], xg[i], AX_X, ALU.add).then_inc(mean_sum, 1)
            dve.wait_ge(mean_sum, 4)
            V.tensor_scalar(stat[:, 32:64], stat[:, 0:32], 1.0 / DM, None, ALU.mult).then_inc(mean_sum, 1)
            dve.wait_ge(mean_sum, 5)

            for i in range(4):
                V.tensor_tensor(xc[i], xg[i],
                                stat[:, 32 + 8 * i:40 + 8 * i].unsqueeze(2).broadcast_to([P, 8, DM]),
                                ALU.subtract).then_inc(cent, 1)
            for i in range(4):
                dve.wait_ge(sqd, i + 1)
                V.tensor_reduce(stat[:, 64 + 8 * i:72 + 8 * i], raw_t(i), AX_X, ALU.add).then_inc(sq_sum, 1)
            dve.wait_ge(w_loaded, 32)
            dve.wait_ge(small_loaded, NSMALL * 16)
            V.tensor_scalar(raw_w2, raw_w2, nw[:, :], None, ALU.mult).then_inc(w_norm, 1)
            V.tensor_scalar(raw_w, raw_w, nw[:, :], None, ALU.mult).then_inc(w_norm, 1)
            for i in range(4):
                dve.wait_ge(rr_pool, 8 * i + 8)
                V.tensor_tensor(raw_t(i), xc[i],
                                stat[:, 192 + 8 * i:200 + 8 * i].unsqueeze(2).broadcast_to([P, 8, DM]),
                                ALU.mult).then_inc(t_done, 1)
            for i in range(4):
                V.tensor_tensor(xc[i], xc[i],
                                stat[:, 320 + 8 * i:328 + 8 * i].unsqueeze(2).broadcast_to([P, 8, DM]),
                                ALU.mult).then_inc(xn_done, 1)
            dve.wait_ge(w_split_dt, 1)
            V.tensor_tensor(wdt_lo[:, :], raw_w2[:, DT0 - 4096:DT0 - 4096 + H], wdt_hi[:, :].bitcast(F32), ALU.subtract).then_inc(w_split_dt, 1)
            n_hi = 0
            for q in range(UNITS):
                for t0, src in tile_sources(q):
                    n_hi += 1
                    dve.wait_ge(whi, n_hi)
                    V.tensor_tensor(src[1](w_lo), src[0], src[1](w_hi).bitcast(F32), ALU.subtract).then_inc(wlo, 1)
            for b in range(NB):
                dve.wait_ge(xnhi, b + 1)
                V.tensor_tensor(xn_lo[:, b % 2, :], bank[b % 2][:, :], xn_hi[:, b % 2, :].bitcast(F32),
                                ALU.subtract).then_inc(xnlo, 1)
            step = 0

            def chain(ins):
                nonlocal step
                step += 1
                ins.then_inc(dtstep_v, 1)
                dve.wait_ge(dtstep_v, step)

            chain(V.tensor_scalar(aexp[:, 0, :], alog[:, :], 80.0, None, ALU.min))
            V.tensor_scalar(aexp[:, 1, :], alog[:, :], 80.0, 0.0, ALU.subtract, ALU.max).then_inc(dt_aux, 1)
            dve.wait_ge(dt_aux, 1)
            chain(V.tensor_scalar(aexp[:, 1, :], aexp[:, 1, :], 80.0, None, ALU.min))
            dve.wait_ge(resid, 4)
            dve.wait_ge(xn_stored, 64)
            dve.wait_ge(res_stored, 64)
            dve.wait_ge(dt_mm, NB)
            raw3 = wk[0].rearrange("p (c h) -> p c h", h=H)
            for k in range(2):
                V.tensor_tensor(raw3[:, 16 * k:16 * k + 16, :], bank[2 + k][:, :].rearrange("p (c h) -> p c h", h=H),
                                dtb[:, :].unsqueeze(1).broadcast_to([P, 16, H]), ALU.add).then_inc(dt_raw, 1)
            dve.wait_ge(dt_raw, 2)
            chain(V.tensor_scalar(wk[1], wk[0], -1.0, None, ALU.mult))
            chain(V.tensor_tensor(wk[1], wk[0], wk[1], ALU.max))
            dve.wait_ge(dtstep_a, 2)
            chain(V.tensor_scalar(wk[2], wk[1], 2.0, None, ALU.add))
            chain(V.reciprocal(wk[3], wk[2]))
            chain(V.tensor_tensor(wk[1], wk[1], wk[3], ALU.mult))
            chain(V.tensor_tensor(wk[2], wk[1], wk[1], ALU.mult))
            chain(V.tensor_scalar(wk[3], wk[2], 1.0 / 17, None, ALU.mult))
            for k in (15, 13, 11, 9, 7, 5, 3):
                chain(V.scalar_tensor_tensor(out=wk[3], in0=wk[3], scalar=1.0 / k, in1=wk[2], op0=ALU.add, op1=ALU.mult))
            chain(V.scalar_tensor_tensor(out=wk[3], in0=wk[3], scalar=1.0, in1=wk[1], op0=ALU.add, op1=ALU.mult))
            chain(V.tensor_scalar(wk[0], wk[0], 0.0, None, ALU.max))
            dt_flat = dt_all[:, :, :].rearrange("p c h -> p (c h)")
            chain(V.scalar_tensor_tensor(out=dt_flat, in0=wk[3], scalar=2.0, in1=wk[0], op0=ALU.mult, op1=ALU.add))
            assert step == 19, step
            dve.wait_ge(dtstep_a, 1)
            w4 = wk[4].rearrange("p (c h) -> p c h", h=H)
            V.tensor_tensor(w4, dt_all[:, :, :], aexp[:, 0:1, :].broadcast_to([P, NCH, H]), ALU.mult).then_inc(dt_aux, 1)
            dve.wait_ge(dt_aux, 2)
            V.tensor_scalar(wk[4], wk[4], 200.0, None, ALU.min).then_inc(dt_aux, 1)
            dve.wait_ge(dt_aux, 3)
            chain(V.tensor_tensor(w4, w4, aexp[:, 1:2, :].broadcast_to([P, NCH, H]), ALU.mult))
            dve.wait_ge(dtstep_a, 3)
            parts = da_split.rearrange("p (c k h) -> p c k h", k=3, h=H)
            w3, w5 = wk[3].rearrange("p (c h) -> p c h", h=H), wk[5].rearrange("p (c h) -> p c h", h=H)
            chain(V.tensor_copy(parts[:, :, 0, :], w4))
            chain(V.tensor_tensor(w5, w4, parts[:, :, 0, :], ALU.subtract))
            chain(V.tensor_copy(parts[:, :, 1, :], w5))
            chain(V.tensor_tensor(w3, w5, parts[:, :, 1, :], ALU.subtract))
            V.tensor_copy(parts[:, :, 2, :], w3).then_inc(da_split_done, 1)
            for i in range(NB):
                dve.wait_ge(pr_t, i + 1)
                for c in range(CH):
                    at = S * i + P * c
                    V.tensor_tensor_scan(prod[:, at:at + P], bank[2 + i % 2][0:H, P * c:P * c + P], zeros[:, :], 1.0,
                                         ALU.mult, ALU.add).then_inc(pr_scan, 1)
            dve.wait_ge(pr_scan, NCH)
            res = work[0:H, 0:4096]
            V.tensor_copy(pr_parts[0:H, :], prod).then_inc(pr_split, 1)
            dve.wait_ge(pr_split, 1)
            V.tensor_tensor(res, prod, pr_parts[0:H, :], ALU.subtract).then_inc(pr_split, 1)
            dve.wait_ge(pr_split, 2)
            V.tensor_copy(pr_parts[H:2 * H, :], res).then_inc(pr_split, 1)
            dve.wait_ge(pr_split, 3)
            V.tensor_copy(prod, pr_parts[H:2 * H, :]).then_inc(pr_split, 1)
            dve.wait_ge(pr_split, 4)
            V.tensor_tensor(pr_parts[2 * H:3 * H, :], res, prod, ALU.subtract).then_inc(pr_split, 1)
            dve.wait_ge(da_copied, NB)
            V.memset(da_parts[:, :].rearrange("p (c i) -> p c i", i=P)[:, :, 0:1], 0.0).then_inc(da_copied, 1)
            dve.wait_ge(hi_done, 1)
            V.tensor_tensor(xn_lo[:, 0, :], bank[6][:, :], xn_hi[:, 0, :].bitcast(F32), ALU.subtract).then_inc(lo_done, 1)

            def slot(b, n):
                q, r = divmod(n, R)
                real = not (isinstance(b, int) and b == NB)
                ssd, state, yy = back(b, n, LAG_SSD), back(b, n, LAG_STATE), back(b, n, LAG_Y)

                def scans():
                    bb, m = ssd
                    after(dve, y_ready, SLOTS, bb, m - 4)
                    for a in range(2):
                        after(dve, bc_ready, 3 * SLOTS, bb, 3 * m + a)
                        V.tensor_tensor_scan(lm[:, m % R, a, :], bc_bank[(3 * m + a) % 2][:, :], ident4[:, :], 0.0,
                                             ALU.mult, ALU.add).then_inc(scanned, 1)

                def x_times_dt():
                    bb, m = ssd
                    mq, mr = divmod(m, R)
                    after(dve, xt_ready, SLOTS, bb, m)
                    dt_b = (dt_all[:, bass.ds(bb * CH, CH), 8 * mq + mr:8 * mq + mr + 5:4]
                            .unsqueeze(3).broadcast_to([P, CH, 2, HP]))
                    V.tensor_tensor(xdt[:, mr, :].rearrange("p (c a d) -> p c a d", c=CH, a=2),
                                    misc_of("xt", n).rearrange("p (c a d) -> p c a d", c=CH, a=2),
                                    dt_b, ALU.mult).then_inc(xdt_done, 1)

                def taps(shift):
                    for t in PLAN[r]:
                        ci, i = CONV_ORDER.index((q, t)), proj_position(n, t)
                        if shift == 1:
                            after(dve, acc_init, NCONV, b, ci)
                        else:
                            after(dve, tap, NTAP, b, TAP[q, t, shift - 1])
                        V.scalar_tensor_tensor(out=conv[:, ci % 4, shift:S], in0=proj_bank[i % 2][:, 0:S - shift],
                                               scalar=cw[:, q, t, KW - 1 - shift:KW - shift],
                                               in1=conv[:, ci % 4, shift:S], op0=ALU.mult, op1=ALU.add).then_inc(tap, 1)

                def state_step(c):
                    bb, m = state
                    sbank = misc_of("s", n)
                    if c == 0:
                        after(dve, s_ready, SLOTS, bb, m)
                        after(dve, hbd_done, 2 * SLOTS, bb, 2 * (m - 2) + 1)
                        V.tensor_copy(hpk[:, m % 2, 0, :], sbank[:, 0:NS]).then_inc(hstep, 1)
                    else:
                        after(dve, hstep, 3 * SLOTS, bb, 3 * m + c - 1)
                        V.scalar_tensor_tensor(out=hpk[:, m % 2, c, :], in0=hpk[:, m % 2, c - 1, :],
                                               scalar=pend[:, m % R, c:c + 1], in1=sbank[:, NS * c:NS * c + NS],
                                               op0=ALU.mult, op1=ALU.add).then_inc(hstep, 1)

                def chunk_products():
                    bb, m = ssd
                    after(dve, bc_ready, 3 * SLOTS, bb, 3 * m + 2)
                    V.tensor_copy(pend[:, m % R, :].unsqueeze(2),
                                  bc_bank[(3 * m + 2) % 2][:, :].rearrange("p (c i) -> p c i", c=CH)[:, :, P - 1:P]).then_inc(pend_done, 1)

                def decay_c():
                    bb, m = ssd
                    if m % R == 0:
                        after(dve, silu_done, NCONV, bb, CONV_ORDER.index((m // R, 1)))
                    V.tensor_tensor(cdec[:, m % R, :], bc_bank[(3 * m + 2) % 2][:, :], chan[:, chan_of(m // R, 1), :],
                                    ALU.mult).then_inc(cdec_done, 1)

                def skip():
                    bb, m = yy
                    v, mr = divmod(m, R)
                    after(dve, y_ready, SLOTS, bb, m)
                    after(dve, out_step, SLOTS, bb, m - 8)
                    V.scalar_tensor_tensor(out=gated[:, v % 2, mr, :], in0=chan[:, chan_of(v, 2 + mr), :],
                                           scalar=dskip[:, m:m + 1], in1=y_bank[:, :],
                                           op0=ALU.mult, op1=ALU.add).then_inc(skipped, 1)

                def times_gate():
                    bb, m = yy
                    v, mr = divmod(m, R)
                    after(dve, gate_done, SLOTS, bb, m)
                    after(dve, skipped, SLOTS, bb, m)
                    V.tensor_tensor(gated[:, v % 2, mr, :], gated[:, v % 2, mr, :], gate[:, mr, :],
                                    ALU.mult).then_inc(gated_done, 1)

                one_tile = len(PLAN[r]) == 1
                if ssd is not None:
                    scans()
                    if not one_tile:
                        x_times_dt()
                if real:
                    taps(1)
                if ssd is not None and one_tile:
                    x_times_dt()
                if state is not None and not one_tile:
                    state_step(0)
                if real:
                    taps(2)
                if state is not None:
                    state_step(0 if one_tile else 1)
                if real:
                    taps(3)
                if state is not None:
                    state_step(1 if one_tile else 2)
                if ssd is not None:
                    chunk_products()
                if state is not None and one_tile:
                    state_step(2)
                if ssd is not None:
                    decay_c()
                if yy is not None:
                    skip()
                if n == XN_SLOT and following(b) is not None:
                    after(dve, hi_done, 1, b, 1)
                    V.tensor_tensor(xn_of(xn_lo, following(b)), misc_of("xn", n), xn_of(xn_hi, following(b)).bitcast(F32),
                                    ALU.subtract).then_inc(lo_done, 1)
                if yy is not None:
                    times_gate()
                if n == XO_SLOT and back(b, n, SLOTS) is not None:
                    bb, _ = back(b, n, SLOTS)
                    after(dve, xo_ready, 1, bb, 0)
                    dve.wait_ge(res_loaded, bb * 16 + 16)
                    xs = r_stage[:, :, :]
                    V.tensor_tensor(xs, misc_of("xo", n).rearrange("p (c d) -> p c d", d=DM), xs, ALU.add).then_inc(x1_done, 1)

            for n in range(SLOTS):
                slot(0, n)
            with dve.Fori(1, NB - 1) as b:
                for n in range(SLOTS):
                    slot(b, n)
            def quantise():
                qn = 0

                def qchain(ins):
                    nonlocal qn
                    qn += 1
                    ins.then_inc(q_step, 1)
                    dve.wait_ge(q_step, qn)

                V.memset(ones, 1.0).then_inc(q_ones, 1)
                dve.wait_ge(q_tot, 1)
                mean, scale, inv = qs[:, 4:6], qs[:, 8:10], qs[:, 12:14]
                qchain(V.tensor_scalar(mean, bank[0][:, 0:2], 1.0 / (HID * DM), EPS, ALU.mult, ALU.max))
                qchain(V.reciprocal(scale, mean))
                qchain(V.reciprocal(inv, scale))
                for k in range(2):
                    w, t = qw[:, k, :], qt[:, k, :]
                    qchain(V.tensor_scalar(t, w, scale[:, k:k + 1], 2.0, ALU.mult, ALU.min))
                    qchain(V.tensor_scalar(t, t, -2.0, MAGIC, ALU.max, ALU.add))
                    qchain(V.tensor_scalar(t, t, MAGIC, None, ALU.subtract))
                    qchain(V.tensor_scalar(t, t, 1.0, -1.0, ALU.min, ALU.max))
                    qchain(V.scalar_tensor_tensor(out=t, in0=t, scalar=inv[:, k:k + 1], in1=w, op0=ALU.mult, op1=ALU.subtract))
                    qchain(V.tensor_tensor(w, w, t, ALU.add))

            for b in (NB - 1, NB):
                for n in range(SLOTS):
                    slot(b, n)
                    if (b, n) == (NB, QUANT_SLOT):
                        quantise()

            dve.wait_ge(xo_ready, NB)

            def step(i, par, k):
                def last_aggr(mv, bn, s):
                    V.bn_aggr(mv[:, CH - 1, :], bn[:, CH - 1, :]).then_inc(s, 1)

                if there(i, 1):
                    for c in range(CH):
                        if c == 0:
                            reach(dve, f_loaded[1 - par], k + par, 16, 16)
                            reach(dve, f_xn, i, CH, CH)
                        else:
                            reach(dve, f_xstats, i, CH, CH + c)
                        V.bn_stats(bn_x[:, c, :], fx[:, 1 - par, c, :]).then_inc(f_xstats, 1)
                        if c > 0:
                            V.bn_aggr(mv_x[:, c - 1, :], bn_x[:, c - 1, :]).then_inc(f_xaggr, 1)
                    reach(dve, f_xstats, i, CH, 2 * CH)
                    if not there(i, 0):
                        last_aggr(mv_x, bn_x, f_xaggr)
                if there(i, 0):
                    for c in range(CH):
                        reach(dve, f_mm1, i, CH, c + 1)
                        reach(dve, f_gelu, i, CH, c + 1 - CH)
                        if isinstance(i, int) and i == 0:
                            dve.wait_ge(b_load, 16)
                        V.tensor_tensor(fh[:, c, :], h_bank[c][:, :], bias1[:, :], ALU.add).then_inc(f_h, 1)
                        if c == 0 and there(i, 1):
                            last_aggr(mv_x, bn_x, f_xaggr)
                if there(i, -1):
                    for c in range(CH):
                        reach(dve, f_gelu, i, CH, c + 1 - CH)
                        reach(dve, f_hstats, i, CH, c - CH)
                        if c == 0:
                            reach(dve, f_nrm, i, CH, -CH)
                        V.bn_stats(bn_h[:, c, :], fge[:, 1 - par, c, :]).then_inc(f_hstats, 1)
                        if c > 0:
                            V.bn_aggr(mv_h[:, c - 1, :], bn_h[:, c - 1, :]).then_inc(f_haggr, 1)
                    reach(dve, f_hstats, i, CH)
                if there(i, 1):
                    reach(dve, f_xr, i, 1, 2)
                    reach(dve, f_t, i, 1, 1)
                    for c in range(CH):
                        V.tensor_scalar(fxn[:, c, :], fx[:, 1 - par, c, :], mv_x[:, c, 0:1], r_x[:, c:c + 1],
                                        ALU.subtract, ALU.mult).then_inc(f_xn, 1)
                        if c == 0 and there(i, -1):
                            last_aggr(mv_h, bn_h, f_haggr)
                elif there(i, -1):
                    last_aggr(mv_h, bn_h, f_haggr)
                if there(i, -2):
                    reach(dve, f_mm2, i, 1, -1)
                    dve.wait_ge(f_xb, 1)
                    place = fres[:, bass.ds((i - 2) * CH, CH), :]
                    V.tensor_tensor(place, bank[5][:, :].rearrange("p (c d) -> p c d", d=DM), place, ALU.add).then_inc(f_out, 1)
                if there(i, -1):
                    reach(dve, f_hr, i, 1)
                    for c in range(CH):
                        V.tensor_scalar(fge[:, 1 - par, c, :], fge[:, 1 - par, c, :], mv_h[:, c, 0:1], r_h[:, c:c + 1],
                                        ALU.subtract, ALU.mult).then_inc(f_nrm, 1)

            ffn_steps(step, dve.Fori)

        @block.tensor
        def _(pe):
            MM, TR = nc.tensor.matmul, nc.tensor.transpose
            pe.wait_ge(consts, 26)
            pe.wait_ge(w_split_dt, 2)

            def dt_products(b):
                pe.wait_ge(xnlo, b + 1)
                for c in range(CH):
                    dst = bank[2 + b // 4][:, H * (CH * (b % 4) + c):H * (CH * (b % 4) + c + 1)]
                    tok = slice(P * c, P * c + P)
                    MM(dst, xn_hi[:, b % 2, tok], wdt_hi[:, :], start=True, stop=False)
                    MM(dst, xn_lo[:, b % 2, tok], wdt_hi[:, :], start=False, stop=False)
                    last = MM(dst, xn_hi[:, b % 2, tok], wdt_lo[:, :], start=False, stop=True)
                last.then_inc(dt_mm, 1)

            for b in range(NB):
                pe.wait_ge(xn_done, b // 2 + 1)
                if b >= 2:
                    pe.wait_ge(xnlo, b - 1)
                for c in range(CH):
                    last = TR(bank[b % 2][:, P * c:P * c + P], xc[b // 2][:, CH * (b % 2) + c, :], ident)
                last.then_inc(xn_t, 1)
                if b >= 1:
                    dt_products(b - 1)
            dt_products(NB - 1)
            pe.wait_ge(dtstep_a, 3)
            pe.wait_ge(dt_raw, 2)
            for i in range(NB):
                if i >= 2:
                    pe.wait_ge(pr_scan, CH * (i - 1))
                for c in range(CH):
                    at = (CH * i + c) * H
                    last = TR(bank[2 + i % 2][0:H, P * c:P * c + P], wk[4][:, at:at + H], ident)
                last.then_inc(pr_t, 1)
            pe.wait_ge(da_split_done, 1)
            for i in range(NB):
                if i >= 2:
                    pe.wait_ge(da_copied, i - 1)
                for c in range(CH):
                    at = (CH * i + c) * 3 * H
                    last = TR(bank[i % 2][0:96, 0:S // 2].bitcast(BF16)[:, P * c:P * c + P], da_split[:, at:at + 3 * H], ident_b[:, :])
                last.then_inc(da_t, 1)
            pe.wait_ge(da_copied, NB + 1)
            pe.wait_ge(pr_split, 5)
            pe.wait_ge(wlo, 4 * UNITS)
            pe.wait_ge(wo_scaled, SLOTS)

            def misc_free(b, n, kind, k=0):
                at = misc_position(kind, n, k)
                bb = b
                while True:
                    at -= 2
                    if at < 0:
                        at, bb = at + len(MISC), bb - 1
                        if isinstance(bb, int) and bb < 0:
                            return
                    pn, pkind, lag, pk = MISC[at]
                    who = back(bb, pn, lag) if pkind != "xn" else following(bb)
                    if who is not None:
                        break
                if pkind == "xn":
                    after(pe, lo_done, 1, who, 0)
                    return
                wb, wm = who
                if pkind == "cb":
                    after(pe, cb_copied, 2 * UNITS, wb, 2 * (wm // R) + pk)
                elif pkind == "bt":
                    after(pe, bt_copied, UNITS, wb, wm // R)
                elif pkind == "xt":
                    after(pe, xdt_done, SLOTS, wb, wm)
                elif pkind == "s":
                    after(pe, hstep, 3 * SLOTS, wb, 3 * wm + 2)
                elif pkind == "var":
                    after(pe, var_copied, UNITS, wb, wm // R)
                elif pkind == "rbc":
                    after(pe, rbc_copied, UNITS, wb, wm // R)
                elif pkind == "xo":
                    after(pe, x1_done, 1, wb, 0)

            def proj_free(b, i):
                bb = b
                while True:
                    i -= 2
                    if i < 0:
                        i, bb = i + len(PROJ), bb - 1
                        if isinstance(bb, int) and bb < 0:
                            return
                    pn, pt = PROJ[i]
                    who = back(bb, pn, LAG_SSD if pt == "z" else 0)
                    if who is not None:
                        break
                if pt == "z":
                    after(pe, gate_done, SLOTS, *who)
                else:
                    after(pe, tap, NTAP, bb, TAP[pn // R, pt, KW - 1])

            def transpose_xn(src, dst):
                for c in range(CH):
                    last = TR(dst[:, P * c:P * c + P], src[:, c, :], ident)
                last.then_inc(xnt_ready, 1)

            transpose_xn(xc[0], bank[6])

            def project(b, n, t, who):
                q = n // R
                i = proj_position(n, t)
                proj_free(b, i)
                bb, m = who
                out_b = proj_bank[i % 2][:, :]
                tile = (m // R, CONVS + m % R) if t == "z" else (q, t)
                wh, wl = w_hi[:, tile[0], tile[1], :], w_lo[:, tile[0], tile[1], :]
                if (q, t) == CONV_ORDER[0]:
                    after(pe, lo_done, 1, b, 0)
                hi, lo = xn_of(xn_hi, bb), xn_of(xn_lo, bb)
                MM(out_b, wh, hi, start=True, stop=False)
                MM(out_b, wh, lo, start=False, stop=False)
                MM(out_b, wl, hi, start=False, stop=True).then_inc(z_ready if t == "z" else proj_ready, 1)

            def spread(bb, m, k):
                i = 3 * m + k
                pm, pk = divmod(i - 2, 3)
                if pk < 2:
                    after(pe, scanned, 2 * SLOTS, bb, 2 * pm + pk)
                else:
                    after(pe, cdec_done, SLOTS, bb, pm)
                first = (0, P, HP)[k]
                MM(bc_bank[i % 2][:, :], sel[:, m, first:first + P], (pr_parts if k == 2 else da_parts)[:, bass.ds(bb * S, S)],
                   start=True, stop=True).then_inc(bc_ready, 1)

            def slot(b, n):
                q, r = divmod(n, R)
                real = not (isinstance(b, int) and b == NB)
                ssd = back(b, n, LAG_SSD)
                if ssd is not None:
                    bb, m = ssd
                    mq, mr = divmod(m, R)
                    after(pe, silu_done, NCONV, bb, CONV_ORDER.index((mq, 2 + mr)))
                    misc_free(b, n, "xt")
                    for c in range(CH):
                        last = TR(misc_of("xt", n)[:, P * c:P * c + P], chan[:, chan_of(mq, 2 + mr), P * c:P * c + P], ident)
                    last.then_inc(xt_ready, 1)
                if real:
                    for t in PLAN[r]:
                        project(b, n, t, (b, n))
                st = back(b, n, LAG_STATE)
                if st is not None:
                    bb, m = st
                    after(pe, xw_done, 2 * SLOTS, bb, 2 * m + 1)
                    after(pe, bt_copied, UNITS, bb, m // R)
                    misc_free(b, n, "s")
                    for a in range(2):
                        half = slice(HP * a, HP * a + HP)
                        for c in range(CH - 1):
                            last = MM(misc_of("s", n)[half, NS * c:NS * c + NS], bt[:, c, half], xw[:, m % 2, c, half],
                                      start=True, stop=True)
                    last.then_inc(s_ready, 1)
                if back(b, n, LAG_OUT) is not None:
                    bb, m = back(b, n, LAG_OUT)
                    after(pe, normed, SLOTS, bb, m)
                    if m == 0:
                        after(pe, out_copied, 1, bb, -1)
                    last = MM(out_bank[:, :], w_out[:, m, :], gated[:, (m // R) % 2, m % R, :], start=(m == 0), stop=(m == SLOTS - 1))
                    last.then_inc(out_step, 1)
                if ssd is not None:
                    spread(*ssd, 2)
                yy = back(b, n, LAG_Y)
                if yy is not None:
                    bb, m = yy
                    mr = m % R
                    after(pe, m_done, SLOTS, bb, m)
                    after(pe, hbd_done, 2 * SLOTS, bb, 2 * m + 1)
                    after(pe, cdec_done, SLOTS, bb, m)
                    after(pe, skipped, SLOTS, bb, m - 1)
                    for c in range(CH):
                        tok = slice(P * c, P * c + P)
                        if c > 0:
                            MM(y_bank[:, tok], hbd[:, m % 2, c - 1, :], cdec[:, mr, tok], start=True, stop=False)
                        for a in range(2):
                            half = slice(HP * a, HP * a + HP)
                            last = MM(y_bank[half, tok], xdt[:, mr, P * c + HP * a:P * c + HP * a + HP], lm[:, mr, a, tok],
                                      start=(c == 0), stop=True)
                    last.then_inc(y_ready, 1)
                if r == 0 and back(b, n, LAG_VAR) is not None:
                    bb, m = back(b, n, LAG_VAR)
                    v = m // R
                    after(pe, ssum_step, 3 * UNITS, bb, 3 * v + 2)
                    misc_free(b, n, "var")
                    for c in range(CH):
                        last = MM(misc_of("var", n)[:, 2 * c:2 * c + 2], ssum[:, v % 2, P * c:P * c + P], blockones[:, :], start=True, stop=True)
                    last.then_inc(var_ready, 1)
                if r == 1 and back(b, n, LAG_M) is not None:
                    bb, m = back(b, n, LAG_M)
                    v = m // R
                    misc_free(b, n, "bt")
                    for c in range(CH):
                        last = TR(misc_of("bt", n)[:, P * c:P * c + P], chan[:, 0, P * c:P * c + P], ident)
                    last.then_inc(bt_ready, 1)
                if ssd is not None:
                    project(b, n, "z", ssd)
                if r == 0 and ssd is not None:
                    bb, m = ssd
                    v = m // R
                    after(pe, silu_done, NCONV, bb, CONV_ORDER.index((v, 1)))
                    for a in range(2):
                        half = slice(HP * a, HP * a + HP)
                        misc_free(b, n, "cb", a)
                        for c in range(CH):
                            tok = slice(P * c, P * c + P)
                            last = MM(misc_of("cb", n, a)[:, tok], chan[half, 0, tok], chan[half, chan_of(v, 1), tok],
                                      start=True, stop=True)
                        last.then_inc(cb_ready, 1)
                if r == 1 and back(b, n, LAG_FACTOR) is not None:
                    bb, m = back(b, n, LAG_FACTOR)
                    v = m // R
                    after(pe, rexp_done, UNITS, bb, v)
                    misc_free(b, n, "rbc")
                    for c in range(CH):
                        last = TR(misc_of("rbc", n)[:, P * c:P * c + P], rexp[:, 2 * c:2 * c + 2, :].rearrange("p a d -> p (a d)"), ident)
                    last.then_inc(rbc_ready, 1)
                if n == XN_SLOT and following(b) is not None:
                    pe.wait_ge(staged, b * 16 + 16)
                    misc_free(b, n, "xn")
                    transpose_xn(xn_stage, misc_of("xn", n))
                if n == XO_SLOT and back(b, n, SLOTS) is not None:
                    bb, _ = back(b, n, SLOTS)
                    after(pe, out_copied, 1, bb, 0)
                    misc_free(b, n, "xo")
                    for c in range(CH):
                        last = TR(misc_of("xo", n)[:, P * c:P * c + P], ocm[:, P * c:P * c + P], ident)
                    last.then_inc(xo_ready, 1)
                if back(b, n + 1, LAG_SSD) is not None:
                    for k in range(2):
                        spread(*back(b, n + 1, LAG_SSD), k)

            for n in range(SLOTS):
                slot(0, n)
            with pe.Fori(1, NB - 1) as b:
                for n in range(SLOTS):
                    slot(b, n)
            for b in (NB - 1, NB):
                for n in range(SLOTS):
                    slot(b, n)
                    if (b, n) == (NB, QUANT_SLOT):
                        pe.wait_ge(q_abs, 2)
                        pe.wait_ge(q_ones, 1)
                        MM(bank[0][:, 0:2], ones, qs[:, 0:2], start=True, stop=True).then_inc(q_tot, 1)

            for k in range(2):
                pe.wait_ge(q_step, 9 + 6 * k)
                for t in range(HT):
                    last = TR(bank[k][:, P * t:P * t + P], qw[:, k, P * t:P * t + P], ident)
                last.then_inc(q_t, 1)
            pe.wait_ge(q_copied, 2)

            def step(i, par, k):
                if there(i, -2):
                    reach(pe, f_ntcopy, i, HT, -HT)
                    reach(pe, f_out, i, 1, -2)
                    for c in range(CH):
                        for t in range(HT):
                            last = MM(bank[5][:, P * c:P * c + P], fnt[:, t, P * c:P * c + P], w2t[:, P * t:P * t + P],
                                      start=(t == 0), stop=(t == HT - 1))
                    last.then_inc(f_mm2, 1)
                if there(i, 1):
                    reach(pe, f_xn, i, CH, 2 * CH)
                    reach(pe, f_tcopy, i, 1, 1)
                    for c in range(CH):
                        last = TR(bank[0][:, P * c:P * c + P], fxn[:, c, :], ident)
                    last.then_inc(f_t, 1)
                    reach(pe, f_tcopy, i, 1, 2)
                    for c in range(CH):
                        reach(pe, f_h, i, CH, c + 1)
                        MM(h_bank[c][:, :], fxt[:, P * c:P * c + P], w1t[:, :], start=True, stop=True).then_inc(f_mm1, 1)
                if there(i, -1):
                    for t in range(HT):
                        reach(pe, f_nrm, i, CH)
                        reach(pe, f_ntcopy, i, HT, t - 1 - HT)
                        for c in range(CH):
                            last = TR(bank[3 + t % 2][:, P * c:P * c + P], fge[:, 1 - par, c, P * t:P * t + P], ident)
                        last.then_inc(f_nt, 1)

            ffn_steps(step, pe.Fori)


_INS = ["L0_attn_hidden_states", "L0_attn_norm_w", "L0_attn_in_proj_w", "L0_attn_conv_w", "L0_attn_conv_b",
        "L0_attn_dt_bias", "L0_attn_A_log", "L0_attn_D", "L0_attn_gate_norm_w", "L0_attn_out_proj_w",
        "L0_ffn_ln1_g", "L0_ffn_ln1_b", "L0_ffn_w1", "L0_ffn_b1", "L0_ffn_ln2_g", "L0_ffn_ln2_b", "L0_ffn_w2",
        "L0_ffn_b2"]


def kernel(**inputs):
    import numpy as _np
    import concourse.bacc as _bacc
    from concourse.bass_utils import run_bass_kernel_spmd as _run

    nc = _bacc.Bacc("TRN2", target_bir_lowering=False, num_devices=1)
    arrays, args = {}, []
    for name in _INS:
        a = _np.ascontiguousarray(inputs[name])
        arrays[f"in_{name}"] = a
        args.append(nc.dram_tensor(f"in_{name}", a.shape, mybir.dt.from_np(a.dtype), kind="ExternalInput").ap())
    out = nc.dram_tensor("out_tokens", (NB, S, DM), F32, kind="ExternalOutput").ap()
    build(nc, *args, out)
    r = _run(nc, [arrays], core_ids=[0])
    return r.results[0]["out_tokens"]
```

```python
from contextlib import ExitStack

import numpy as np

import concourse.bass as bass
from concourse import mybir

F32 = mybir.dt.float32
F32R = mybir.dt.float32r
BF16 = mybir.dt.bfloat16
ALU = mybir.AluOpType
ACT = mybir.ActivationFunctionType
AX_X = mybir.AxisListType.X

P = 128
NB, S, DM = 8, 512, 128
H, HP, G, NS, KW = 32, 64, 8, 64, 4
DI = H * HP
CH = S // P
NCH = NB * CH
UNITS, R = G // 2, 4
SLOTS = UNITS * R
TILES = 10
CONVS = 6
HID = 512
HT = HID // P
EPS = 1e-5
MAGIC = 1.5 * 2.0 ** 23
Z0, X0, B0, C0, DT0 = 0, DI, 2 * DI, 2 * DI + G * NS, 2 * DI + 2 * G * NS
DPROJ = DT0 + H

PLAN = [[2], [3, 4], [0, 1], [5]]
CONV_ORDER = [(q, t) for q in range(UNITS) for r in range(R) for t in PLAN[r]]
NCONV = len(CONV_ORDER)


def tap_numbers():
    found, n = {}, 0
    for q in range(UNITS):
        for r in range(R):
            for shift in range(1, KW):
                for t in PLAN[r]:
                    found[q, t, shift] = n
                    n += 1
    return found


TAP = tap_numbers()
NTAP = len(TAP)

LAG_SSD, LAG_M, LAG_STATE, LAG_Y, LAG_SUM, LAG_VAR, LAG_FACTOR, LAG_NORM, LAG_OUT = 4, 5, 6, 7, 8, 12, 13, 14, 15
SUM_SLOTS, QUANT_SLOTS, QUANT_END = (5, 6), (6, 7), 12
EARLY_STEPS = {12: -2, 13: -1, 14: 0}
XN_SLOT = 7
XO_SLOT = LAG_OUT


XDT_ACT = (2,3)


def back(b, n, lag):
    m = n - lag
    while m < 0:
        b, m = b - 1, m + SLOTS
    if isinstance(b, int) and not 0 <= b < NB:
        return None
    return b, m


def following(b):
    return None if isinstance(b, int) and b + 1 >= NB else b + 1


def misc_plan():
    plan = []
    for q in range(UNITS):
        for r in range(R):
            n = 4 * q + r
            plan.append((n, "xt", LAG_SSD, 0))
            plan.append((n, "s", LAG_STATE, 0))
            if r == 0:
                plan.append((n, "var", LAG_VAR, 0))
                plan += [(n, "cb", LAG_SSD, 0), (n, "cb", LAG_SSD, 1)]
            if r == 1:
                plan.append((n, "bt", LAG_M, 0))
                plan.append((n, "rbc", LAG_FACTOR, 0))
            if n == XO_SLOT:
                plan.append((n, "xo", SLOTS, 0))
            if n == XN_SLOT:
                plan.append((n, "xn", 0, 0))
    return plan


MISC = misc_plan()
PR_ORDER = [(0, 0), (0, 1), (1, 0), (0, 2), (1, 1), (0, 3), (1, 2), (1, 3)]
PIECE = NB * S // 4
ROOT_STEPS = (2, 10)
DT_STEPS = 16


def pr_rest_of(part, piece):
    return PR_ORDER.index((part, piece)) + 1


PROJ = [(4 * q + r, t) for q in range(UNITS) for r in range(R) for t in PLAN[r] + ["z"]]
assert len(PROJ) % 2 == 0
FIRST_BANKS = (0, 4, 1, 5, 6, 7)


def proj_position(n, t):
    return PROJ.index((n, t))
assert len(MISC) % 2 == 0


def log1p_series(degree=9):
    fit = np.polynomial.chebyshev.Chebyshev.interpolate(lambda x: np.log1p(0.5 + 0.5 * x) / (0.5 + 0.5 * x), degree)
    return [float(c) * 2.0 ** k for k, c in enumerate(np.polynomial.chebyshev.cheb2poly(fit.coef))]


def build(nc, hid_in, norm_w, in_w, conv_w, conv_b, dt_bias, a_log, d_skip, gnorm_w, out_w,
          ln1_g, ln1_b, w1, b1, ln2_g, ln2_b, w2, b2, out):
    ctx = ExitStack()
    with ctx:
        def sb(name, shape, dt=F32):
            return ctx.enter_context(nc.sbuf_tensor(name, shape, dt))

        def pb(name, shape, dt=F32):
            return ctx.enter_context(nc.psum_tensor(name, shape, dt))

        def sem(name):
            return ctx.enter_context(nc.semaphore(name))

        ident4 = sb("ident4", [P, S])
        ident = ident4[:, 0:P]
        ident_b = sb("ident_b", [P, P], BF16)
        sel = sb("sel", [96, SLOTS, 2 * P], BF16)
        blockones = sb("blockones", [P, 2])
        neghalf = sb("neghalf", [P, 8])
        eps_c = sb("eps_c", [P, 8])
        w_hi = sb("w_hi", [P, UNITS, TILES, P], F32R)
        w_lo = sb("w_lo", [P, UNITS, TILES, P], F32R)
        w_out = sb("w_out", [P, SLOTS, DM])
        nw = sb("nw", [P, 1])
        cw = sb("cw", [P, UNITS, CONVS, KW])
        cb_bias = sb("cb_bias", [P, UNITS, CONVS])
        dskip = sb("dskip", [P, SLOTS])
        gnw = sb("gnw", [P, SLOTS])
        dtb = sb("dtb", [P, H])
        alog = sb("alog", [P, H])
        aexp = sb("aexp", [P, 2, H])
        w1t = sb("w1t", [P, HID])
        w2t = sb("w2t", [P, HID])
        fg1 = sb("fg1", [P, 1])
        fb1 = sb("fb1", [P, 1])
        fg2 = sb("fg2", [P, HT])
        fb2 = sb("fb2", [P, HT])
        dt_all = sb("dt_all", [P, NCH, H])
        da_parts = sb("da_parts", [96, NB * S], BF16)
        pr_parts = sb("pr_parts", [96, NB * S], BF16)
        xn_dram = nc.dram_tensor("xn_scratch", (P, NCH, DM), F32, kind="Internal").ap()
        res_dram = nc.dram_tensor("residual_scratch", (P, NCH, DM), F32, kind="Internal").ap()
        x1_dram = nc.dram_tensor("x1_scratch", (P, NCH, DM), F32, kind="Internal").ap()
        xn_hi = sb("xn_hi", [P, 2, S], F32R)
        xn_lo = sb("xn_lo", [P, 2, S], F32R)
        xn_stage = sb("xn_stage", [P, CH, DM])
        r_stage = sb("r_stage", [P, CH, DM])
        conv = sb("conv", [P, 4, S])
        bt = sb("bt", [P, CH, P])
        chan = sb("chan", [P, 2 * CONVS - 1, S])
        gate = sb("gate", [P, R, S])
        cbs = sb("cbs", [P, 2, S])
        lm = sb("lm", [P, 4, 2, S])
        xdt = sb("xdt", [P, 4, S])
        cdec = sb("cdec", [P, 4, S])
        pend = sb("pend", [P, 4, CH])
        xw = sb("xw", [P, 2, CH - 1, P])
        hpk = sb("hpk", [P, 2, CH - 1, NS])
        hbd = sb("hbd", [P, 2, CH - 1, P])
        gated = sb("gated", [P, 2, R, S])
        sq = sb("sq", [P, S])
        ssum = sb("ssum", [P, 2, S])
        rbs = sb("rbs", [P, S])
        vtok = sb("vtok", [P, 2 * CH])
        rtok = sb("rtok", [P, 2 * CH])
        rexp = sb("rexp", [P, 2 * CH, HP])
        ocm = rexp[:, :, :].rearrange("p c d -> p (c d)")

        def xn_of(ring, b):
            return ring[:, bass.ds(b % 2, 1), :].rearrange("p a s -> p (a s)")

        def chan_of(q, t):
            return 0 if t == 0 else 1 + (CONVS - 1) * (q % 2) + t - 1

        bank = [pb(f"bank{i}", [P, S]) for i in range(8)]
        proj_bank, bc_bank, misc_bank, y_bank, out_bank = bank[0:2], bank[2:4], bank[4:6], bank[6], bank[7]

        def tile_bank(b, n, t):
            if isinstance(b, int) and b == 0 and n < R:
                return bank[FIRST_BANKS[CONV_ORDER.index((0, t))]]
            return proj_bank[proj_position(n, t) % 2]

        raw_w = lm[:, :, :, :].rearrange("p a b s -> p (a b s)")
        raw_w2 = gated[:, :, :, :].rearrange("p a b s -> p (a b s)")[:, 2048:2048 + DPROJ - 4096]
        work = chan[:, :, :].rearrange("p a s -> p (a s)")
        flat = [t.rearrange("p a s -> p (a s)") for t in (gate[:, :, :], cdec[:, :, :], conv[:, :, :])]
        gflat = gated[:, :, :, :].rearrange("p a b s -> p (a b s)")
        halves = [t[:, at:at + 1024] for t, at in ((gflat, 0), (gflat, 1024), (work, 4096), (flat[2], 1024),
                                                   (flat[0], 0), (flat[0], 1024), (flat[1], 0), (flat[1], 1024))]
        by_chunk = [t.rearrange("p (c d) -> p c d", d=DM) for t in halves]
        xg, xc = by_chunk[0:4], by_chunk[4:8]
        wk = [t.rearrange("p a s -> p (a s)") for t in (xdt[:, 0:2, :], xdt[:, 2:4, :], ssum[:, :, :], cbs[:, :, :])] + [halves[7]]
        stat = conv[:, :, :].rearrange("p a s -> p (a s)")
        var, var_eps, root, newton, r1, r2, r12 = (stat[:, 96 + 32 * i:128 + 32 * i] for i in range(7))
        da_split = work[:, 0:1536].bitcast(BF16)
        prod_rest = work[0:H, 1536:1536 + NB * S]
        xn_cm = (sq, rbs)
        w_dt = raw_w2[:, DT0 - 4096:DT0 - 4096 + H]
        prod = raw_w[0:H, :]
        zeros = bt[0:H, 0, :]

        w_loaded = sem("w_loaded")
        w2_loaded = sem("w2_loaded")
        wo_loaded = sem("wo_loaded")
        small_loaded = sem("small_loaded")
        x_loaded = [sem(f"x_loaded_{i}") for i in range(4)]
        consts = sem("consts")
        mean_sum = sem("mean_sum")
        cent = sem("cent")
        sqd = sem("sqd")
        sq_sum = sem("sq_sum")
        rstep_v = sem("rstep_v")
        rstep_a = sem("rstep_a")
        t_done = sem("t_done")
        xn_done = sem("xn_done")
        xn_t = sem("xn_t")
        xn_copied = sem("xn_copied")
        resid = sem("resid")
        w_norm = sem("w_norm")
        whi = sem("whi")
        wlo = sem("wlo")
        raw_parts = sem("raw_parts")
        raw_parts_v = sem("raw_parts_v")
        da_part = sem("da_part")
        da_rest = sem("da_rest")
        pr_high = sem("pr_high")
        pr_mid = sem("pr_mid")
        pr_back = sem("pr_back")
        pr_rest = sem("pr_rest")
        dt_mm = sem("dt_mm")
        dt_raw = sem("dt_raw")
        dtstep_v = sem("dtstep_v")
        dtstep_a = sem("dtstep_a")
        da_split_done = sem("da_split_done")
        da_t = sem("da_t")
        da_copied = sem("da_copied")
        pr_t = sem("pr_t")
        wo_scaled = sem("wo_scaled")
        proj_ready = sem("proj_ready")
        z_ready = sem("z_ready")
        xnt_ready = sem("xnt_ready")
        staged = sem("staged")
        res_stored = sem("res_stored")
        xn_stored = sem("xn_stored")
        res_loaded = sem("res_loaded")
        x1_stored = sem("x1_stored")
        hi_done = sem("hi_done")
        lo_done = sem("lo_done")
        acc_init = sem("acc_init")
        tap = sem("tap")
        silu_done = sem("silu_done")
        gate_done = sem("gate_done")
        cb_ready = sem("cb_ready")
        cb_copied = sem("cb_copied")
        bt_ready = sem("bt_ready")
        bt_copied = sem("bt_copied")
        xt_ready = sem("xt_ready")
        xdt_done = sem("xdt_done")
        xdt_act = sem("xdt_act")
        xw_done = sem("xw_done")
        bc_ready = sem("bc_ready")
        scanned = sem("scanned")
        cdec_done = sem("cdec_done")
        pend_done = sem("pend_done")
        m_done = sem("m_done")
        s_ready = sem("s_ready")
        hstep = sem("hstep")
        hbd_done = sem("hbd_done")
        y_ready = sem("y_ready")
        skipped = sem("skipped")
        gated_done = sem("gated_done")
        sq_done = sem("sq_done")
        ssum_step = sem("ssum_step")
        var_ready = sem("var_ready")
        var_copied = sem("var_copied")
        rstd_done = sem("rstd_done")
        rexp_done = sem("rexp_done")
        rbc_ready = sem("rbc_ready")
        rbc_copied = sem("rbc_copied")
        normed = sem("normed")
        out_copied = sem("out_copied")
        xo_ready = sem("xo_ready")
        x1_done = sem("x1_done")
        pr_scan = sem("pr_scan")
        dt_aux = sem("dt_aux")
        out_step = sem("out_step")
        f_loaded = [sem("f_loaded_even"), sem("f_loaded_odd")]
        f_xstats = sem("f_xstats")
        f_xaggr = sem("f_xaggr")
        f_xeps = sem("f_xeps")
        f_xr = sem("f_xr")
        f_xn = sem("f_xn")
        f_xb = sem("f_xb")
        f_t = sem("f_t")
        f_tcopy = sem("f_tcopy")
        f_mm1 = sem("f_mm1")
        f_h = sem("f_h")
        f_gelu = sem("f_gelu")
        f_hstats = sem("f_hstats")
        f_haggr = sem("f_haggr")
        f_heps = sem("f_heps")
        f_hr = sem("f_hr")
        f_nrm = sem("f_nrm")
        f_nt = sem("f_nt")
        f_ntcopy = sem("f_ntcopy")
        f_mm2 = sem("f_mm2")
        f_out = sem("f_out")
        f_stored = sem("f_stored")
        b1_load = sem("b1_load")
        b_load = sem("b_load")
        q_load = sem("q_load")
        q_ones = sem("q_ones")
        q_abs = sem("q_abs")
        q_tot = sem("q_tot")
        q_step = sem("q_step")
        q_t = sem("q_t")
        q_copied = sem("q_copied")

        def after(eng, s, per, b, i):
            if isinstance(b, int) and b * per + i + 1 <= 0:
                return
            eng.wait_ge(s, b * per + (i + 1))

        def xdt_there(eng, b, m):
            u, r = divmod(m, R)
            if r in XDT_ACT:
                after(eng, xdt_act, 2 * CH * UNITS * len(XDT_ACT), b, 2 * CH * (u * len(XDT_ACT) + XDT_ACT.index(r) + 1) - 1)
            else:
                mine = [k for k in range(R) if k not in XDT_ACT]
                after(eng, xdt_done, UNITS * len(mine), b, u * len(mine) + mine.index(r))

        def raw_t(i):
            return work[:, 1024 * i:1024 * i + 1024].rearrange("p (c d) -> p c d", d=DM)

        qw, qt = conv[:, 0:2, :], conv[:, 2:4, :]
        ones = xn_stage[:, 0, :]
        qs = xn_stage[:, 1, :]
        fx = cbs[:, :, :].rearrange("p a (c d) -> p a c d", d=DM)
        fres = gflat.rearrange("p (c d) -> p c d", d=DM)
        fxn = xdt[:, 0, :].rearrange("p (c d) -> p c d", d=DM)
        fxt = xdt[:, 1, :]
        bias1 = xdt[:, 2, :]
        bias2 = xdt[:, 3, 0:DM]
        fh = gate[:, :, :]
        fge = lm[:, :, :, :].rearrange("p (k a) b s -> p k (a b) s", k=2)
        fnt = cdec[:, :, :]
        fst = xn_stage[:, 2:4, :].rearrange("p c d -> p (c d)")
        bn_x = fst[:, 0:6 * CH].rearrange("p (c k) -> p c k", k=6)
        mv_x = fst[:, 32:32 + 2 * CH].rearrange("p (c k) -> p c k", k=2)
        ve_x, r_x = fst[:, 48:48 + CH], fst[:, 64:64 + CH]
        bn_h = fst[:, 128:128 + 6 * CH].rearrange("p (c k) -> p c k", k=6)
        mv_h = fst[:, 160:160 + 2 * CH].rearrange("p (c k) -> p c k", k=2)
        ve_h, r_h = fst[:, 176:176 + CH], fst[:, 192:192 + CH]
        h_bank, nt_bank = (bank[1], bank[2], bank[6], bank[3]), (bank[4], bank[7])

        def ffn_steps(step, loop):
            step(1, 1, 0)
            with loop(1, NB // 2 - 1) as k:
                step(k * 2, 0, k)
                step(k * 2 + 1, 1, k)
            for i in range(NB - 2, NB + 2):
                step(i, i % 2, i // 2)

        def early(step, b, n):
            if b == NB and n in EARLY_STEPS:
                i = EARLY_STEPS[n]
                step(i, i % 2, i // 2)

        def there(i, shift):
            return not isinstance(i, int) or 0 <= i + shift < NB

        def reach(eng, s, value, per, more=0):
            if isinstance(value, int) and value * per + more <= 0:
                return
            eng.wait_ge(s, value * per + more)

        def tile_sources(q):
            found = []
            bsrc = raw_w2[:, P * q:P * q + P]
            csrc = raw_w2[:, G * NS + P * q:G * NS + P * q + P]
            found.append((0, (bsrc, lambda w: w[:, q, 0, :])))
            found.append((1, (csrc, lambda w: w[:, q, 1, :])))
            for t0, at in ((2, X0), (CONVS, Z0)):
                src = raw_w[:, at + 512 * q:at + 512 * q + 512].rearrange("p (a r d) -> p r a d", a=2, r=R)
                found.append((t0, (src, lambda w, t0=t0: w[:, q, t0:t0 + R, :].rearrange("p r (a d) -> p r a d", a=2))))
            return found

        NSMALL = 2 + 2 * UNITS * 4 + 4 + 4

        def misc_position(kind, n, k=0):
            return [j for j, x in enumerate(MISC) if x[0] == n and x[1] == kind][k]

        def misc_of(kind, n, k=0):
            return misc_bank[misc_position(kind, n, k) % 2][:, :]

        block = ctx.enter_context(nc.Block())

        @block.sync
        def _(sp):
            x_v = hid_in.rearrange("b (c p) d -> p (b c) d", p=P)
            for i in range(4):
                sp.dma_start(xg[i], x_v[:, 8 * i:8 * i + 8, :]).then_inc(x_loaded[i], 16)
            with nc.allow_non_contiguous_dma(reason="small parameters"):
                sp.dma_start(nw[:, :], norm_w.rearrange("(p o) -> p o", o=1)).then_inc(w2_loaded, 16)
            sp.dma_start(raw_w2, in_w[:, 4096:DPROJ]).then_inc(w2_loaded, 16)
            sp.dma_start(raw_w, in_w[:, 0:4096]).then_inc(w_loaded, 16)
            with nc.allow_non_contiguous_dma(reason="small parameters"):
                sp.dma_start(dtb[:, :], dt_bias.rearrange("(o h) -> o h", o=1).broadcast_to([P, H])).then_inc(small_loaded, 16)
                sp.dma_start(alog[:, :], a_log.rearrange("(o h) -> o h", o=1).broadcast_to([P, H])).then_inc(small_loaded, 16)
                for a in range(2):
                    half = slice(HP * a, HP * a + HP)
                    for q in range(UNITS):
                        sp.dma_start(cw[half, q, 2:CONVS, :],
                                     conv_w[0:DI].rearrange("(q a r p) k -> q a p r k", q=UNITS, a=2, r=R)[q, a]).then_inc(small_loaded, 16)
                        sp.dma_start(cb_bias[half, q, 2:CONVS],
                                     conv_b[0:DI].rearrange("(q a r p) -> q a p r", q=UNITS, a=2, r=R)[q, a]).then_inc(small_loaded, 16)
                        sp.dma_start(gnw[half, R * q:R * q + R],
                                     gnorm_w.rearrange("(q a r p) -> q a p r", q=UNITS, a=2, r=R)[q, a]).then_inc(small_loaded, 16)
                        sp.dma_start(dskip[half, R * q:R * q + R],
                                     d_skip.rearrange("(q a r) -> q a r", q=UNITS, a=2)[q, a:a + 1].broadcast_to([HP, R])).then_inc(small_loaded, 16)
                for t, at in ((0, DI), (1, DI + G * NS)):
                    sp.dma_start(cw[:, :, t, :], conv_w[at:at + G * NS].rearrange("(q p) k -> p q k", p=P)).then_inc(small_loaded, 16)
                    sp.dma_start(cb_bias[:, :, t], conv_b[at:at + G * NS].rearrange("(q p) -> p q", p=P)).then_inc(small_loaded, 16)
                sp.dma_start(fg1[:, :], ln1_g.rearrange("(p o) -> p o", o=1)).then_inc(small_loaded, 16)
                sp.dma_start(fb1[:, :], ln1_b.rearrange("(p o) -> p o", o=1)).then_inc(small_loaded, 16)
                sp.dma_start(fg2[:, :], ln2_g.rearrange("(t p) -> p t", p=P)).then_inc(small_loaded, 16)
                sp.dma_start(fb2[:, :], ln2_b.rearrange("(t p) -> p t", p=P)).then_inc(small_loaded, 16)
            for a in range(2):
                src = out_w.rearrange("(q a r p) d -> a p q r d", q=UNITS, a=2, r=R)[a]
                for q in range(UNITS):
                    sp.dma_start(w_out[HP * a:HP * a + HP, R * q:R * q + R, :], src[:, q]).then_inc(wo_loaded, 16)
            for i in range(4):
                sp.wait_ge(xn_done, i + 1)
                sp.dma_start(xn_dram[:, 8 * i:8 * i + 8, :], raw_t(i)).then_inc(xn_stored, 16)
            for i in range(4):
                sp.wait_ge(resid, i + 1)
                sp.dma_start(res_dram[:, 8 * i:8 * i + 8, :], xg[i]).then_inc(res_stored, 16)
            sp.wait_ge(res_stored, 64)
            sp.wait_ge(xn_stored, 64)

            def batch(b):
                if following(b) is not None:
                    sp.wait_ge(xnt_ready, b + 1)
                    sp.dma_start(xn_stage[:, :, :], xn_dram[:, bass.ds((b + 1) * CH, CH), :]).then_inc(staged, 16)
                if not (isinstance(b, int) and b == 0):
                    sp.wait_ge(x1_done, b)
                    sp.dma_start(x1_dram[:, bass.ds((b - 1) * CH, CH), :], r_stage[:, :, :]).then_inc(x1_stored, 16)
                    sp.wait_ge(x1_stored, b * 16)
                if not (isinstance(b, int) and b == NB):
                    sp.dma_start(r_stage[:, :, :], res_dram[:, bass.ds(b * CH, CH), :]).then_inc(res_loaded, 16)

            batch(0)
            with sp.Fori(1, NB - 1) as b:
                batch(b)
            batch(NB - 1)
            sp.wait_ge(silu_done, NB * NCONV)
            sp.dma_start(qw[:, 0, :].rearrange("p (t d) -> p t d", d=DM), w1.rearrange("(t p) d -> p t d", p=P)).then_inc(q_load, 16)
            sp.dma_start(qw[:, 1, :], w2).then_inc(q_load, 16)
            def load(i, par):
                reach(sp, f_xn, i, CH, CH)
                sp.dma_start(fx[:, par, :, :], x1_dram[:, bass.ds((i + 2) * CH, CH), :]).then_inc(f_loaded[par], 16)

            def step(i, par, k):
                if there(i, 2) and not (isinstance(i, int) and i <= 1):
                    load(i, par)

            sp.wait_ge(m_done, NB * SLOTS)
            sp.wait_ge(y_ready, NB * SLOTS)
            for i in range(-2, 0):
                load(i, i % 2)
            sp.dma_start(bias1[:, :], b1.rearrange("(o h) -> o h", o=1).broadcast_to([P, HID])).then_inc(b1_load, 16)
            sp.dma_start(bias2[:, :], b2.rearrange("(o h) -> o h", o=1).broadcast_to([P, DM])).then_inc(b_load, 16)
            for i in range(0, 2):
                load(i, i % 2)
            batch(NB)
            sp.wait_ge(x1_stored, 16 * NB)
            sp.dma_start(fres, x1_dram).then_inc(b_load, 16)
            ffn_steps(step, sp.Fori)
            sp.wait_ge(f_stored, 16 * NB)

        @block.gpsimd
        def _(gp):
            gp.memset(ident4[:, :], 0.0).then_inc(consts, 1)
            gp.memset(ident_b[:, :], 0.0).then_inc(consts, 1)
            gp.memset(sel[:, :, :], 0.0).then_inc(consts, 1)
            gp.memset(neghalf[:, :], -0.5).then_inc(consts, 1)
            gp.memset(eps_c[:, :], EPS).then_inc(consts, 1)
            gp.memset(zeros, 0.0).then_inc(consts, 1)
            gp.memset(blockones[:, :], 0.0).then_inc(consts, 1)
            gp.memset(hbd[:, :, :, :], 0.0).then_inc(consts, 1)
            gp.wait_ge(consts, 8)
            gp.affine_select(out=ident_b[:, :], in_=ident_b[:, :], compare_op=ALU.not_equal, fill=1.0, base=0,
                             pattern=[[-1, P]], channel_multiplier=1).then_inc(consts, 1)
            i4 = ident4[:, :].rearrange("p (c i) -> p c i", c=CH)
            gp.affine_select(out=i4, in_=i4, compare_op=ALU.not_equal, fill=1.0, base=0,
                             pattern=[[0, CH], [-1, P]], channel_multiplier=1).then_inc(consts, 1)
            for k in range(3):
                gp.wait_ge(consts, 10 + UNITS * k)
                part = sel[32 * k:32 * k + 32, :, :]
                part = part.rearrange("k (q r) (a c) -> k q r a c", r=R, a=2)
                for q in range(UNITS):
                    gp.affine_select(out=part[:, q], in_=part[:, q], compare_op=ALU.not_equal, fill=1.0, base=-8 * q,
                                     pattern=[[-1, R], [-4, 2], [0, P]], channel_multiplier=1).then_inc(consts, 1)
            for a in range(2):
                gp.wait_ge(consts, 10 + 3 * UNITS + a)
                gp.memset(blockones[HP * a:HP * a + HP, a:a + 1], 1.0).then_inc(consts, 1)
            gp.wait_ge(consts, 24)

            for i in range(4):
                gp.wait_ge(t_done, i + 1)
                gp.tensor_tensor(xg[i], xg[i], xc[i], ALU.add).then_inc(resid, 1)
            n_hi = 0
            for q in range(UNITS):
                for t0, src in tile_sources(q):
                    n_hi += 1
                    gp.wait_ge(whi, n_hi)
                    gp.tensor_tensor(src[1](w_lo), src[0], src[1](w_hi).bitcast(F32), ALU.subtract).then_inc(wlo, 1)
            gp.wait_ge(da_part, 3)
            gp.wait_ge(da_rest, 2)
            gp.memset(da_split[0:1, :], 0.0).then_inc(da_split_done, 1)
            gp.wait_ge(pr_rest, len(PR_ORDER))

            def slot(b, n):
                q, r = divmod(n, R)
                if back(b, n, LAG_NORM) is not None:
                    bb, m = back(b, n, LAG_NORM)
                    v = m // R
                    after(gp, rbc_copied, UNITS, bb, v)
                    after(gp, sq_done, SLOTS, bb, m)
                    gp.tensor_tensor(gated[:, v % 2, m % R, :], gated[:, v % 2, m % R, :], rbs[:, :], ALU.mult).then_inc(normed, 1)
                ssd = back(b, n, LAG_M)
                if ssd is not None:
                    bb, m = ssd
                    mq, mr = divmod(m, R)
                    xdt_there(gp, bb, m)
                    after(gp, scanned, 2 * SLOTS, bb, 2 * m + 1)
                    after(gp, s_ready, SLOTS, bb, m - 2)
                    for a in range(2):
                        ldec = (lm[:, mr, a, :].rearrange("p (c i) -> p c i", c=CH)[:, 0:CH - 1, P - 1:P]
                                .broadcast_to([P, CH - 1, HP]))
                        gp.tensor_tensor(xw[:, mr % 2, :, HP * a:HP * a + HP],
                                         xdt[:, mr, :].rearrange("p (c d) -> p c d", c=CH)[:, 0:CH - 1, HP * a:HP * a + HP],
                                         ldec, ALU.mult).then_inc(xw_done, 1)
                    after(gp, cb_copied, 2 * UNITS, bb, 2 * mq + 1)
                    after(gp, xw_done, 2 * SLOTS, bb, 2 * m + 1)
                    gp.tensor_tensor(lm[:, mr, :, :], lm[:, mr, :, :], cbs[:, :, :], ALU.mult).then_inc(m_done, 1)
                yy = back(b, n, LAG_SUM)
                if yy is not None and yy[1] % R > 0:
                    bb, m = yy
                    after(gp, sq_done, SLOTS, bb, m)
                    after(gp, ssum_step, 3 * UNITS, bb, 3 * (m // R) + m % R - 2)
                    gp.tensor_tensor(ssum[:, m // R % 2, :], ssum[:, m // R % 2, :], sq[:, :], ALU.add).then_inc(ssum_step, 1)
                if r == 0 and back(b, n, LAG_VAR) is not None:
                    bb, m = back(b, n, LAG_VAR)
                    v = m // R
                    after(gp, var_copied, UNITS, bb, v)
                    after(gp, rexp_done, UNITS, bb, v - 1)
                    gp.tensor_tensor(rtok[:, :], vtok[:, :], neghalf[:, 0:2 * CH], ALU.pow).then_inc(rstd_done, 1)

            def step(i, par, k):
                if there(i, 2):
                    reach(gp, f_xaggr, i, CH, 3 * CH)
                    gp.tensor_tensor(ve_x, mv_x[:, :, 1], eps_c[:, 0:CH], ALU.add).then_inc(f_xeps, 1)
                    reach(gp, f_xeps, i, 1, 3)
                    reach(gp, f_xn, i, CH, 2 * CH)
                    gp.tensor_tensor(r_x, ve_x, neghalf[:, 0:CH], ALU.pow).then_inc(f_xr, 1)
                if there(i, -1):
                    reach(gp, f_haggr, i, CH)
                    gp.tensor_tensor(ve_h, mv_h[:, :, 1], eps_c[:, 0:CH], ALU.add).then_inc(f_heps, 1)
                    reach(gp, f_heps, i, 1)
                    reach(gp, f_nrm, i, CH, -CH)
                    gp.tensor_tensor(r_h, ve_h, neghalf[:, 0:CH], ALU.pow).then_inc(f_hr, 1)
                if there(i, -1):
                    if isinstance(i, int) and i == 1:
                        gp.wait_ge(b_load, 32)
                    rest = fres[:, bass.ds((i - 1) * CH, CH), :]
                    gp.tensor_tensor(rest, rest, bias2[:, :].unsqueeze(1).broadcast_to([P, CH, DM]), ALU.add).then_inc(f_xb, 1)

            for n in range(SLOTS):
                slot(0, n)
            with gp.Fori(1, NB - 1) as b:
                for n in range(SLOTS):
                    slot(b, n)
            for b in (NB - 1, NB):
                for n in range(SLOTS):
                    slot(b, n)
                    early(step, b, n)

            gp.wait_ge(xo_ready, NB)

            ffn_steps(step, gp.Fori)

        @block.scalar
        def _(act):
            for i in range(4):
                act.wait_ge(cent, i + 1)
                act.activation(raw_t(i), xc[i], ACT.Square).then_inc(sqd, 1)
            for k in range(2):
                act.wait_ge(rstep_v, ROOT_STEPS[k])
                act.activation(root, var_eps, ACT.Sqrt).then_inc(rstep_a, 1)
            for b in range(NB):
                if b == 1:
                    act.wait_ge(w2_loaded, 32)
                    act.activation(raw_w2, raw_w2, ACT.Copy, scale=nw[:, :]).then_inc(w_norm, 1)
                act.wait_ge(xn_t, b + 1)
                if b >= 2:
                    act.wait_ge(dt_mm, b - 1)
                act.activation(xn_cm[b % 2][:, :], bank[b % 2][:, :], ACT.Copy).then_inc(xn_copied, 1)
            act.wait_ge(xnt_ready, 1)
            act.activation(xn_hi[:, 0, :], bank[6][:, :], ACT.Copy).then_inc(hi_done, 1)
            act.wait_ge(dt_raw, 2)
            act.activation(wk[1], wk[0], ACT.Abs).then_inc(raw_parts, 1)
            act.wait_ge(raw_parts, 1)
            act.activation(wk[1], wk[1], ACT.Exp, scale=-1.0).then_inc(dtstep_a, 1)
            act.wait_ge(dt_aux, 2)
            act.activation(aexp[:, :, :], aexp[:, :, :], ACT.Exp).then_inc(dtstep_a, 1)
            act.wait_ge(w_loaded, 16)
            act.activation(raw_w, raw_w, ACT.Copy, scale=nw[:, :]).then_inc(w_norm, 1)
            act.wait_ge(w_norm, 2)
            for q in range(UNITS):
                for t0, src in tile_sources(q):
                    act.activation(src[1](w_hi), src[0], ACT.Copy).then_inc(whi, 1)
            act.wait_ge(wo_loaded, 16 * 2 * UNITS)
            act.wait_ge(small_loaded, NSMALL * 16)
            for k in range(SLOTS):
                act.activation(w_out[:, k, :], w_out[:, k, :], ACT.Copy, scale=gnw[:, k:k + 1]).then_inc(wo_scaled, 1)
            act.wait_ge(dtstep_v, DT_STEPS)
            act.activation(wk[4], wk[4], ACT.Exp, scale=-1.0).then_inc(dtstep_a, 1)
            act.wait_ge(dtstep_a, 3)
            act.wait_ge(xn_stored, 64)
            parts = da_split.rearrange("p (c k h) -> p c k h", k=3, h=H)

            def da_copy(k):
                act.wait_ge(da_rest, k)
                act.activation(parts[:, :, k, :], (wk[4], wk[2], wk[3])[k].rearrange("p (c h) -> p c h", h=H), ACT.Copy).then_inc(da_part, 1)

            def pr_copies(high, mid):
                if high is not None:
                    act.wait_ge(pr_scan, (high + 1) * 2 * CH)
                    act.activation(pr_parts[0:H, PIECE * high:PIECE * (high + 1)], prod[:, PIECE * high:PIECE * (high + 1)], ACT.Copy).then_inc(pr_high, 1)
                if mid is not None:
                    act.wait_ge(pr_rest, pr_rest_of(0, mid))
                    tok = slice(PIECE * mid, PIECE * (mid + 1))
                    act.activation(pr_parts[H:2 * H, tok], prod_rest[:, tok], ACT.Copy).then_inc(pr_mid, 1)
                    act.wait_ge(pr_mid, mid + 1)
                    act.activation(prod[:, tok], pr_parts[H:2 * H, tok], ACT.Copy).then_inc(pr_back, 1)

            def da_rows(i):
                act.wait_ge(da_t, i + 1)
                act.activation(da_parts[:, S * i:S * i + S], bank[6 + i % 2][0:96, 0:S // 2].bitcast(BF16), ACT.Copy).then_inc(da_copied, 1)

            da_copy(0)
            pr_copies(0, None)
            da_copy(1)
            pr_copies(1, 0)
            da_copy(2)
            pr_copies(2, 1)
            pr_copies(3, 2)
            act.wait_ge(res_stored, 64)

            def slot(b, n):
                q, r = divmod(n, R)
                real = not (isinstance(b, int) and b == NB)
                st = back(b, n, LAG_STATE + 1)
                if st is not None:
                    bb, m = st
                    after(act, hstep, 3 * SLOTS, bb, 3 * m + 2)
                    after(act, y_ready, SLOTS, bb, m - 2)
                    for a in range(2):
                        half = slice(HP * a, HP * a + HP)
                        act.activation(hbd[half, m % 2, :, half], hpk[half, m % 2, :, :], ACT.Copy).then_inc(hbd_done, 1)
                if real:
                    for t in PLAN[r]:
                        ci = CONV_ORDER.index((q, t))
                        after(act, proj_ready, NCONV, b, ci)
                        after(act, silu_done, NCONV, b, ci - 4)
                        act.activation(conv[:, ci % 4, :], tile_bank(b, n, t)[:, :], ACT.Identity,
                                       scale=cw[:, q, t, KW - 1:KW], bias=cb_bias[:, q, t:t + 1]).then_inc(acc_init, 1)
                prev = back(b, n, 1)
                if prev is not None:
                    bb, m = prev
                    pq, prr = divmod(m, R)
                    for t in PLAN[prr]:
                        i = CONV_ORDER.index((pq, t))
                        after(act, tap, NTAP, bb, TAP[pq, t, KW - 1])
                        if t == 0:
                            after(act, bt_ready, UNITS, bb, pq - 1)
                            after(act, cb_ready, 2 * UNITS, bb, 2 * (pq - 1) + 1)
                        elif t == 1:
                            after(act, cdec_done, SLOTS, bb, 4 * (pq - 2) + 3)
                        else:
                            after(act, skipped, SLOTS, bb, 4 * (pq - 2) + t - 2)
                        act.activation(chan[:, chan_of(pq, t), :], conv[:, i % 4, :], ACT.Silu).then_inc(silu_done, 1)
                ssd = back(b, n, LAG_SSD)
                if ssd is not None and r in XDT_ACT:
                    bb, m = ssd
                    after(act, xt_ready, SLOTS, bb, m)
                    after(act, y_ready, SLOTS, bb, m - 4)
                    for c in range(CH):
                        for a in range(2):
                            at = P * c + HP * a
                            head = 8 * (m // R) + 4 * a + r
                            dt_h = dt_all[:, bass.ds(bb * CH + c, 1), head:head + 1].rearrange("p c h -> p (c h)")
                            act.activation(xdt[:, r, at:at + HP], misc_of("xt", n)[:, at:at + HP], ACT.Copy, scale=dt_h).then_inc(xdt_act, 1)

                yy = back(b, n, LAG_SUM)
                if yy is not None:
                    bb, m = yy
                    after(act, gated_done, SLOTS, bb, m)
                    v = m // R
                    if m % R == 0:
                        after(act, var_ready, UNITS, bb, v - 2)
                        after(act, ssum_step, 3 * UNITS, bb, 3 * v - 1)
                        dst = ssum[:, v % 2, :]
                    else:
                        after(act, ssum_step, 3 * UNITS, bb, 3 * v + m % R - 2)
                        dst = sq[:, :]
                    act.activation(dst, gated[:, v % 2, m % R, :], ACT.Square).then_inc(sq_done, 1)
                if r == 1 and back(b, n, LAG_FACTOR) is not None:
                    bb, m = back(b, n, LAG_FACTOR)
                    v = m // R
                    after(act, rstd_done, UNITS, bb, v)
                    after(act, rbc_ready, UNITS, bb, v - 1)
                    act.activation(rexp[:, :, :], rtok[:, :].unsqueeze(2).broadcast_to([P, 2 * CH, HP]), ACT.Copy).then_inc(rexp_done, 1)
                if n == XN_SLOT and following(b) is not None:
                    after(act, xnt_ready, 1, b, 1)
                    act.activation(xn_of(xn_hi, following(b)), misc_of("xn", n), ACT.Copy).then_inc(hi_done, 1)
                if n == XO_SLOT - 1 and back(b, n, SLOTS) is not None:
                    bb, _ = back(b, n, SLOTS)
                    after(act, out_step, SLOTS, bb, SLOTS - 1)
                    after(act, xo_ready, 1, bb, -1)
                    act.activation(ocm[:, :], out_bank[:, :], ACT.Copy).then_inc(out_copied, 1)
                if r == 0 and back(b, n, LAG_VAR) is not None:
                    bb, m = back(b, n, LAG_VAR)
                    v = m // R
                    after(act, var_ready, UNITS, bb, v)
                    after(act, rstd_done, UNITS, bb, v - 1)
                    act.activation(vtok[:, :], misc_of("var", n)[:, 0:2 * CH], ACT.Identity, scale=1.0 / (DI // G),
                                   bias=eps_c[:, 0:1]).then_inc(var_copied, 1)
                if r == 1 and back(b, n, LAG_M) is not None:
                    bb, m = back(b, n, LAG_M)
                    v = m // R
                    after(act, bt_ready, UNITS, bb, v)
                    after(act, s_ready, SLOTS, bb, m - 1)
                    act.activation(bt[:, :, :], misc_of("bt", n).rearrange("p (c d) -> p c d", c=CH), ACT.Copy).then_inc(bt_copied, 1)
                if ssd is not None:
                    bb, m = ssd
                    after(act, z_ready, SLOTS, bb, m)
                    after(act, gated_done, SLOTS, bb, m - 4)
                    act.activation(gate[:, m % R, :], proj_bank[proj_position(n, "z") % 2][:, :], ACT.Silu).then_inc(gate_done, 1)
                if r == 0 and ssd is not None:
                    bb, m = ssd
                    v = m // R
                    for a in range(2):
                        after(act, cb_ready, 2 * UNITS, bb, 2 * v + a)
                        after(act, m_done, SLOTS, bb, m - 1)
                        act.activation(cbs[:, a, :], misc_of("cb", n, a), ACT.Copy).then_inc(cb_copied, 1)
                if r == 1 and back(b, n, LAG_FACTOR) is not None:
                    bb, m = back(b, n, LAG_FACTOR)
                    v = m // R
                    after(act, rbc_ready, UNITS, bb, v)
                    after(act, normed, SLOTS, bb, 4 * v - 1)
                    act.activation(rbs[:, :], misc_of("rbc", n), ACT.Copy).then_inc(rbc_copied, 1)

            def step(i, par, k):
                if there(i, 0):
                    for c in range(CH):
                        reach(act, f_h, i, CH, c + 1)
                        reach(act, f_nt, i, HT, -HT)
                        act.activation(fge[:, par, c, :], fh[:, c, :], ACT.Gelu).then_inc(f_gelu, 1)
                if there(i, -1):
                    for t in range(HT):
                        reach(act, f_nt, i, HT, t + 1 - HT)
                        reach(act, f_mm2, i, 1, -1)
                        act.activation(fnt[:, t, :], nt_bank[t % 2][:, :], ACT.Identity, scale=fg2[:, t:t + 1],
                                       bias=fb2[:, t:t + 1]).then_inc(f_ntcopy, 1)
                if there(i, 2):
                    reach(act, f_t, i, 1, 3)
                    reach(act, f_mm1, i, CH, 2 * CH)
                    act.activation(fxt, bank[0][:, :], ACT.Identity, scale=fg1[:, :], bias=fb1[:, :]).then_inc(f_tcopy, 1)
                if there(i, -2):
                    reach(act, f_out, i, 1, -1)
                    act.dma_start(out_v[bass.ds(i - 2, 1)].rearrange("b p c d -> p (b c) d"),
                                  fres[:, bass.ds((i - 2) * CH, CH), :]).then_inc(f_stored, 16)

            slot(0, 0)
            for i in range(NB):
                da_rows(i)
                if i == 0:
                    pr_copies(None, 3)
            act.wait_ge(pr_rest, len(PR_ORDER))
            for n in range(1, SLOTS):
                slot(0, n)
            with act.Fori(1, NB - 1) as b:
                for n in range(SLOTS):
                    slot(b, n)
            for b in (NB - 1, NB):
                for n in range(SLOTS):
                    slot(b, n)
                    if (b, n) == (NB, SUM_SLOTS[0]):
                        act.wait_ge(q_load, 32)
                        for k in range(2):
                            act.activation(qt[:, k, :], qw[:, k, :], ACT.Abs, accum_out=qs[:, k:k + 1]).then_inc(q_abs, 1)
                    if (b, n) == (NB, QUANT_END):
                        for k in range(2):
                            act.wait_ge(q_t, k + 1)
                            act.activation((w1t, w2t)[k][:, :], bank[2 + k][:, :], ACT.Copy).then_inc(q_copied, 1)
                    early(step, b, n)

            act.wait_ge(xo_ready, NB)
            out_v = out.rearrange("b (c p) d -> b p c d", p=P)
            ffn_steps(step, act.Fori)

        @block.vector
        def _(dve):
            V = nc.vector
            for i in range(4):
                dve.wait_ge(x_loaded[i], 16)
                V.tensor_reduce(stat[:, 8 * i:8 * i + 8], xg[i], AX_X, ALU.add).then_inc(mean_sum, 1)
                dve.wait_ge(mean_sum, 2 * i + 1)
                V.tensor_scalar(stat[:, 32 + 8 * i:40 + 8 * i], stat[:, 8 * i:8 * i + 8], 1.0 / DM, None, ALU.mult).then_inc(mean_sum, 1)
                dve.wait_ge(mean_sum, 2 * i + 2)
                V.tensor_tensor(xc[i], xg[i],
                                stat[:, 32 + 8 * i:40 + 8 * i].unsqueeze(2).broadcast_to([P, 8, DM]),
                                ALU.subtract).then_inc(cent, 1)
            for i in range(4):
                dve.wait_ge(sqd, i + 1)
                V.tensor_reduce(stat[:, 64 + 8 * i:72 + 8 * i], raw_t(i), AX_X, ALU.add).then_inc(sq_sum, 1)
            dve.wait_ge(sq_sum, 4)
            step = 0

            def rchain(ins):
                nonlocal step
                step += 1
                ins.then_inc(rstep_v, 1)
                dve.wait_ge(rstep_v, step)

            rchain(V.tensor_scalar(var, stat[:, 64:96], 1.0 / DM, None, ALU.mult))
            for k, r in enumerate((r1, r2)):
                if k == 0:
                    rchain(V.tensor_scalar(var_eps, var, EPS, None, ALU.add))
                else:
                    rchain(V.tensor_tensor(newton, r1, r1, ALU.mult))
                    rchain(V.tensor_tensor(newton, newton, var, ALU.mult))
                    rchain(V.tensor_scalar(var_eps, newton, EPS, None, ALU.add))
                assert step == ROOT_STEPS[k]
                dve.wait_ge(rstep_a, k + 1)
                rchain(V.reciprocal(r, root))
                rchain(V.tensor_tensor(newton, r, r, ALU.mult))
                rchain(V.tensor_tensor(newton, newton, var_eps, ALU.mult))
                rchain(V.tensor_scalar(newton, newton, -0.5, 1.5, ALU.mult, ALU.add))
                rchain(V.tensor_tensor(r, r, newton, ALU.mult))
            rchain(V.tensor_tensor(r12, r1, r2, ALU.mult))

            def scaled(out, i, factor):
                return V.tensor_tensor(out, xc[i], factor[:, 8 * i:8 * i + 8].unsqueeze(2).broadcast_to([P, 8, DM]), ALU.mult)

            for i in range(4):
                scaled(raw_t(i), i, r12).then_inc(xn_done, 1)
            for i in range(4):
                scaled(xc[i], i, r1).then_inc(t_done, 1)
            dve.wait_ge(small_loaded, NSMALL * 16)
            V.tensor_scalar(aexp[:, 0, :], alog[:, :], 80.0, None, ALU.min).then_inc(dt_aux, 1)
            V.tensor_scalar(aexp[:, 1, :], alog[:, :], 80.0, 0.0, ALU.subtract, ALU.max).then_inc(raw_parts_v, 1)
            dve.wait_ge(raw_parts_v, 1)
            V.tensor_scalar(aexp[:, 1, :], aexp[:, 1, :], 80.0, None, ALU.min).then_inc(dt_aux, 1)
            step = 0

            def chain(ins):
                nonlocal step
                step += 1
                ins.then_inc(dtstep_v, 1)
                dve.wait_ge(dtstep_v, step)

            dve.wait_ge(dt_mm, NB)
            raw3 = wk[0].rearrange("p (c h) -> p c h", h=H)
            for k in range(2):
                V.tensor_tensor(raw3[:, 16 * k:16 * k + 16, :], bank[2 + k][:, :].rearrange("p (c h) -> p c h", h=H),
                                dtb[:, :].unsqueeze(1).broadcast_to([P, 16, H]), ALU.add).then_inc(dt_raw, 1)
            dve.wait_ge(hi_done, 1)
            V.tensor_tensor(xn_lo[:, 0, :], bank[6][:, :], xn_hi[:, 0, :].bitcast(F32), ALU.subtract).then_inc(lo_done, 1)
            dve.wait_ge(raw_parts, 1)
            chain(V.tensor_scalar(wk[0], wk[0], 0.0, None, ALU.max))
            series = log1p_series()
            dve.wait_ge(dtstep_a, 1)
            chain(V.tensor_scalar(wk[2], wk[1], -0.5, None, ALU.add))
            chain(V.tensor_scalar(wk[3], wk[2], series[-1], None, ALU.mult))
            for c in series[-2:0:-1]:
                chain(V.scalar_tensor_tensor(out=wk[3], in0=wk[3], scalar=c, in1=wk[2], op0=ALU.add, op1=ALU.mult))
            chain(V.scalar_tensor_tensor(out=wk[3], in0=wk[3], scalar=series[0], in1=wk[1], op0=ALU.add, op1=ALU.mult))
            chain(V.tensor_tensor(dt_all[:, :, :].rearrange("p c h -> p (c h)"), wk[3], wk[0], ALU.add))
            dve.wait_ge(dtstep_a, 2)
            dve.wait_ge(resid, 4)
            w4 = wk[4].rearrange("p (c h) -> p c h", h=H)
            chain(V.tensor_tensor(w4, dt_all[:, :, :], aexp[:, 0:1, :].broadcast_to([P, NCH, H]), ALU.mult))
            chain(V.tensor_scalar(wk[4], wk[4], 200.0, None, ALU.min))
            chain(V.tensor_tensor(w4, w4, aexp[:, 1:2, :].broadcast_to([P, NCH, H]), ALU.mult))
            assert step == DT_STEPS, step
            parts = da_split.rearrange("p (c k h) -> p c k h", k=3, h=H)

            def da_left(k):
                dve.wait_ge(da_part, k + 1)
                V.tensor_tensor(wk[2 + k].rearrange("p (c h) -> p c h", h=H), wk[(4, 2)[k]].rearrange("p (c h) -> p c h", h=H),
                                parts[:, :, k, :], ALU.subtract).then_inc(da_rest, 1)

            def products(piece):
                for i in (2 * piece, 2 * piece + 1):
                    dve.wait_ge(pr_t, i + 1)
                    for c in range(CH):
                        at = S * i + P * c
                        V.tensor_tensor_scan(prod[:, at:at + P], bank[2 + i % 2][0:H, P * c:P * c + P], zeros[:, :], 1.0,
                                             ALU.mult, ALU.add).then_inc(pr_scan, 1)

            def left(k, piece):
                tok = slice(PIECE * piece, PIECE * (piece + 1))
                if k == 0:
                    dve.wait_ge(pr_high, piece + 1)
                    V.tensor_tensor(prod_rest[:, tok], prod[:, tok], pr_parts[0:H, tok], ALU.subtract).then_inc(pr_rest, 1)
                else:
                    dve.wait_ge(pr_back, piece + 1)
                    V.tensor_tensor(pr_parts[2 * H:3 * H, tok], prod_rest[:, tok], prod[:, tok], ALU.subtract).then_inc(pr_rest, 1)

            dve.wait_ge(wlo, 4 * UNITS)
            products(0)
            da_left(0)
            products(1)
            dve.wait_ge(res_stored, 64)
            dve.wait_ge(xn_stored, 64)
            left(0, 0)
            da_left(1)
            products(2)
            left(0, 1)
            left(1, 0)
            products(3)
            left(0, 2)
            left(1, 1)
            left(0, 3)
            left(1, 2)

            def slot(b, n):
                q, r = divmod(n, R)
                real = not (isinstance(b, int) and b == NB)
                ssd, state, yy = back(b, n, LAG_SSD), back(b, n, LAG_STATE), back(b, n, LAG_Y)

                def scans():
                    bb, m = ssd
                    after(dve, y_ready, SLOTS, bb, m - 4)
                    for a in range(2):
                        after(dve, bc_ready, 3 * SLOTS, bb, 3 * m + a)
                        V.tensor_tensor_scan(lm[:, m % R, a, :], bc_bank[(3 * m + a) % 2][:, :], ident4[:, :], 0.0,
                                             ALU.mult, ALU.add).then_inc(scanned, 1)

                def x_times_dt():
                    bb, m = ssd
                    mq, mr = divmod(m, R)
                    if mr in XDT_ACT:
                        return
                    after(dve, xt_ready, SLOTS, bb, m)
                    dt_b = (dt_all[:, bass.ds(bb * CH, CH), 8 * mq + mr:8 * mq + mr + 5:4]
                            .unsqueeze(3).broadcast_to([P, CH, 2, HP]))
                    V.tensor_tensor(xdt[:, mr, :].rearrange("p (c a d) -> p c a d", c=CH, a=2),
                                    misc_of("xt", n).rearrange("p (c a d) -> p c a d", c=CH, a=2),
                                    dt_b, ALU.mult).then_inc(xdt_done, 1)

                def taps(shift):
                    for t in PLAN[r]:
                        ci = CONV_ORDER.index((q, t))
                        if shift == 1:
                            after(dve, acc_init, NCONV, b, ci)
                        else:
                            after(dve, tap, NTAP, b, TAP[q, t, shift - 1])
                        V.scalar_tensor_tensor(out=conv[:, ci % 4, shift:S], in0=tile_bank(b, n, t)[:, 0:S - shift],
                                               scalar=cw[:, q, t, KW - 1 - shift:KW - shift],
                                               in1=conv[:, ci % 4, shift:S], op0=ALU.mult, op1=ALU.add).then_inc(tap, 1)

                def state_step(c):
                    bb, m = state
                    sbank = misc_of("s", n)
                    if c == 0:
                        after(dve, s_ready, SLOTS, bb, m)
                        after(dve, hbd_done, 2 * SLOTS, bb, 2 * (m - 2) + 1)
                        V.tensor_copy(hpk[:, m % 2, 0, :], sbank[:, 0:NS]).then_inc(hstep, 1)
                    else:
                        after(dve, hstep, 3 * SLOTS, bb, 3 * m + c - 1)
                        V.scalar_tensor_tensor(out=hpk[:, m % 2, c, :], in0=hpk[:, m % 2, c - 1, :],
                                               scalar=pend[:, m % R, c:c + 1], in1=sbank[:, NS * c:NS * c + NS],
                                               op0=ALU.mult, op1=ALU.add).then_inc(hstep, 1)

                def chunk_products():
                    bb, m = ssd
                    after(dve, bc_ready, 3 * SLOTS, bb, 3 * m + 2)
                    V.tensor_copy(pend[:, m % R, :].unsqueeze(2),
                                  bc_bank[(3 * m + 2) % 2][:, :].rearrange("p (c i) -> p c i", c=CH)[:, :, P - 1:P]).then_inc(pend_done, 1)

                def decay_c():
                    bb, m = ssd
                    if m % R == 0:
                        after(dve, silu_done, NCONV, bb, CONV_ORDER.index((m // R, 1)))
                    V.tensor_tensor(cdec[:, m % R, :], bc_bank[(3 * m + 2) % 2][:, :], chan[:, chan_of(m // R, 1), :],
                                    ALU.mult).then_inc(cdec_done, 1)

                def skip():
                    bb, m = yy
                    v, mr = divmod(m, R)
                    after(dve, y_ready, SLOTS, bb, m)
                    after(dve, out_step, SLOTS, bb, m - 8)
                    V.scalar_tensor_tensor(out=gated[:, v % 2, mr, :], in0=chan[:, chan_of(v, 2 + mr), :],
                                           scalar=dskip[:, m:m + 1], in1=y_bank[:, :],
                                           op0=ALU.mult, op1=ALU.add).then_inc(skipped, 1)

                def times_gate():
                    bb, m = yy
                    v, mr = divmod(m, R)
                    after(dve, gate_done, SLOTS, bb, m)
                    after(dve, skipped, SLOTS, bb, m)
                    V.tensor_tensor(gated[:, v % 2, mr, :], gated[:, v % 2, mr, :], gate[:, mr, :],
                                    ALU.mult).then_inc(gated_done, 1)

                one_tile = len(PLAN[r]) == 1
                if ssd is not None:
                    scans()
                    if not one_tile:
                        x_times_dt()
                if real:
                    taps(1)
                if ssd is not None and one_tile:
                    x_times_dt()
                if state is not None and not one_tile:
                    state_step(0)
                if real:
                    taps(2)
                if state is not None:
                    state_step(0 if one_tile else 1)
                if real:
                    taps(3)
                if state is not None:
                    state_step(1 if one_tile else 2)
                if ssd is not None:
                    chunk_products()
                if state is not None and one_tile:
                    state_step(2)
                if ssd is not None:
                    decay_c()
                if yy is not None:
                    skip()
                if n == XN_SLOT and following(b) is not None:
                    after(dve, hi_done, 1, b, 1)
                    V.tensor_tensor(xn_of(xn_lo, following(b)), misc_of("xn", n), xn_of(xn_hi, following(b)).bitcast(F32),
                                    ALU.subtract).then_inc(lo_done, 1)
                if yy is not None:
                    times_gate()
                if n == XO_SLOT and back(b, n, SLOTS) is not None:
                    bb, _ = back(b, n, SLOTS)
                    after(dve, xo_ready, 1, bb, 0)
                    dve.wait_ge(res_loaded, bb * 16 + 16)
                    xs = r_stage[:, :, :]
                    V.tensor_tensor(xs, misc_of("xo", n).rearrange("p (c d) -> p c d", d=DM), xs, ALU.add).then_inc(x1_done, 1)

            def step(i, par, k):
                def last_aggr(mv, bn, s):
                    V.bn_aggr(mv[:, CH - 1, :], bn[:, CH - 1, :]).then_inc(s, 1)

                if there(i, 2):
                    for c in range(CH):
                        if c == 0:
                            reach(dve, f_loaded[par], k, 16, 32)
                            reach(dve, f_xn, i, CH, 2 * CH)
                        else:
                            reach(dve, f_xstats, i, CH, 2 * CH + c)
                        V.bn_stats(bn_x[:, c, :], fx[:, par, c, :]).then_inc(f_xstats, 1)
                        if c > 0:
                            V.bn_aggr(mv_x[:, c - 1, :], bn_x[:, c - 1, :]).then_inc(f_xaggr, 1)
                    reach(dve, f_xstats, i, CH, 3 * CH)
                    if not there(i, 0):
                        last_aggr(mv_x, bn_x, f_xaggr)
                if there(i, 0):
                    for c in range(CH):
                        reach(dve, f_mm1, i, CH, c + 1)
                        reach(dve, f_gelu, i, CH, c + 1 - CH)
                        if isinstance(i, int) and i == 0:
                            dve.wait_ge(b1_load, 16)
                        V.tensor_tensor(fh[:, c, :], h_bank[c][:, :], bias1[:, :], ALU.add).then_inc(f_h, 1)
                        if c == 0 and there(i, 2):
                            last_aggr(mv_x, bn_x, f_xaggr)
                if there(i, -1):
                    for c in range(CH):
                        reach(dve, f_gelu, i, CH, c + 1 - CH)
                        reach(dve, f_hstats, i, CH, c - CH)
                        if c == 0:
                            reach(dve, f_nrm, i, CH, -CH)
                        V.bn_stats(bn_h[:, c, :], fge[:, 1 - par, c, :]).then_inc(f_hstats, 1)
                        if c > 0:
                            V.bn_aggr(mv_h[:, c - 1, :], bn_h[:, c - 1, :]).then_inc(f_haggr, 1)
                    reach(dve, f_hstats, i, CH)
                if there(i, 2):
                    reach(dve, f_xr, i, 1, 3)
                    reach(dve, f_t, i, 1, 2)
                    for c in range(CH):
                        V.tensor_scalar(fxn[:, c, :], fx[:, par, c, :], mv_x[:, c, 0:1], r_x[:, c:c + 1],
                                        ALU.subtract, ALU.mult).then_inc(f_xn, 1)
                        if c == 0 and there(i, -1):
                            last_aggr(mv_h, bn_h, f_haggr)
                elif there(i, -1):
                    last_aggr(mv_h, bn_h, f_haggr)
                def result():
                    if there(i, -2):
                        reach(dve, f_mm2, i, 1, -1)
                        reach(dve, f_xb, i, 1, -1)
                        place = fres[:, bass.ds((i - 2) * CH, CH), :]
                        V.tensor_tensor(place, bank[5][:, :].rearrange("p (c d) -> p c d", d=DM), place, ALU.add).then_inc(f_out, 1)

                def normalise_hidden():
                    if there(i, -1):
                        reach(dve, f_hr, i, 1)
                        for c in range(CH):
                            V.tensor_scalar(fge[:, 1 - par, c, :], fge[:, 1 - par, c, :], mv_h[:, c, 0:1], r_h[:, c:c + 1],
                                            ALU.subtract, ALU.mult).then_inc(f_nrm, 1)

                if there(i, 1):
                    result()
                    normalise_hidden()
                else:
                    normalise_hidden()
                    result()

            slot(0, 0)
            left(1, 3)
            for n in range(1, SLOTS):
                slot(0, n)
            with dve.Fori(1, NB - 1) as b:
                for n in range(SLOTS):
                    slot(b, n)
            qn = 0

            def quantise(k):

                def qchain(ins):
                    nonlocal qn
                    qn += 1
                    ins.then_inc(q_step, 1)
                    dve.wait_ge(q_step, qn)

                mean, scale, inv = qs[:, 4:6], qs[:, 8:10], qs[:, 12:14]
                if k == 0:
                    dve.wait_ge(q_tot, 1)
                    qchain(V.tensor_scalar(mean, bank[1][:, 0:2], 1.0 / (HID * DM), EPS, ALU.mult, ALU.max))
                    qchain(V.reciprocal(scale, mean))
                    qchain(V.reciprocal(inv, scale))
                w, t = qw[:, k, :], qt[:, k, :]
                qchain(V.tensor_scalar(t, w, scale[:, k:k + 1], 2.0, ALU.mult, ALU.min))
                qchain(V.tensor_scalar(t, t, -2.0, MAGIC, ALU.max, ALU.add))
                qchain(V.tensor_scalar(t, t, MAGIC, None, ALU.subtract))
                qchain(V.tensor_scalar(t, t, 1.0, -1.0, ALU.min, ALU.max))
                qchain(V.scalar_tensor_tensor(out=t, in0=t, scalar=inv[:, k:k + 1], in1=w, op0=ALU.mult, op1=ALU.subtract))
                qchain(V.tensor_tensor(w, w, t, ALU.add))

            for b in (NB - 1, NB):
                for n in range(SLOTS):
                    slot(b, n)
                    if (b, n) == (NB, SUM_SLOTS[0]):
                        V.memset(ones, 1.0).then_inc(q_ones, 1)
                    if b == NB and n in QUANT_SLOTS:
                        quantise(QUANT_SLOTS.index(n))
                    early(step, b, n)

            dve.wait_ge(xo_ready, NB)

            ffn_steps(step, dve.Fori)

        @block.tensor
        def _(pe):
            MM, TR = nc.tensor.matmul, nc.tensor.transpose
            pe.wait_ge(consts, 24)
            def transpose_xn(src, dst):
                for c in range(CH):
                    last = TR(dst[:, P * c:P * c + P], src[:, c, :], ident)
                last.then_inc(xnt_ready, 1)

            def dt_products(b):
                pe.wait_ge(xn_copied, b + 1)
                pe.wait_ge(w_norm, 1)
                for c in range(CH):
                    at = H * (CH * (b % 4) + c)
                    last = MM(bank[2 + b // 4][:, at:at + H], xn_cm[b % 2][:, P * c:P * c + P], w_dt, start=True, stop=True)
                last.then_inc(dt_mm, 1)

            for b in range(NB):
                pe.wait_ge(xn_done, b // 2 + 1)
                if b >= 2:
                    pe.wait_ge(xn_copied, b - 1)
                for c in range(CH):
                    last = TR(bank[b % 2][:, P * c:P * c + P], raw_t(b // 2)[:, CH * (b % 2) + c, :], ident)
                last.then_inc(xn_t, 1)
                if b >= 1:
                    dt_products(b - 1)
            dt_products(NB - 1)
            transpose_xn(raw_t(0), bank[6])
            pe.wait_ge(dtstep_a, 3)
            pe.wait_ge(dt_raw, 2)
            for i in range(NB):
                if i >= 2:
                    pe.wait_ge(pr_scan, CH * (i - 1))
                for c in range(CH):
                    at = (CH * i + c) * H
                    last = TR(bank[2 + i % 2][0:H, P * c:P * c + P], wk[4][:, at:at + H], ident)
                last.then_inc(pr_t, 1)
            pe.wait_ge(wlo, 4 * UNITS)
            pe.wait_ge(wo_scaled, SLOTS)

            def misc_free(b, n, kind, k=0):
                at = misc_position(kind, n, k)
                bb = b
                while True:
                    at -= 2
                    if at < 0:
                        at, bb = at + len(MISC), bb - 1
                        if isinstance(bb, int) and bb < 0:
                            return
                    pn, pkind, lag, pk = MISC[at]
                    who = back(bb, pn, lag) if pkind != "xn" else following(bb)
                    if who is not None:
                        break
                if pkind == "xn":
                    after(pe, lo_done, 1, who, 0)
                    return
                wb, wm = who
                if pkind == "cb":
                    after(pe, cb_copied, 2 * UNITS, wb, 2 * (wm // R) + pk)
                elif pkind == "bt":
                    after(pe, bt_copied, UNITS, wb, wm // R)
                elif pkind == "xt":
                    xdt_there(pe, wb, wm)
                elif pkind == "s":
                    after(pe, hstep, 3 * SLOTS, wb, 3 * wm + 2)
                elif pkind == "var":
                    after(pe, var_copied, UNITS, wb, wm // R)
                elif pkind == "rbc":
                    after(pe, rbc_copied, UNITS, wb, wm // R)
                elif pkind == "xo":
                    xdt_there(pe, bb, pn - LAG_SSD)
                    after(pe, x1_done, 1, wb, 0)

            def proj_free(b, i):
                bb = b
                while True:
                    i -= 2
                    if i < 0:
                        i, bb = i + len(PROJ), bb - 1
                        if isinstance(bb, int) and bb < 0:
                            return
                    pn, pt = PROJ[i]
                    who = back(bb, pn, LAG_SSD if pt == "z" else 0)
                    if who is not None:
                        break
                if pt == "z":
                    after(pe, gate_done, SLOTS, *who)
                else:
                    after(pe, tap, NTAP, bb, TAP[pn // R, pt, KW - 1])

            def project(b, n, t, who):
                q = n // R
                bb, m = who
                if isinstance(b, int) and b == 0 and n < R:
                    out_b = tile_bank(b, n, t)[:, :]
                else:
                    proj_free(b, proj_position(n, t))
                    out_b = proj_bank[proj_position(n, t) % 2][:, :]
                tile = (m // R, CONVS + m % R) if t == "z" else (q, t)
                wh, wl = w_hi[:, tile[0], tile[1], :], w_lo[:, tile[0], tile[1], :]
                if (q, t) == CONV_ORDER[0]:
                    after(pe, lo_done, 1, b, 0)
                hi, lo = xn_of(xn_hi, bb), xn_of(xn_lo, bb)
                MM(out_b, wh, hi, start=True, stop=False)
                MM(out_b, wh, lo, start=False, stop=False)
                MM(out_b, wl, hi, start=False, stop=True).then_inc(z_ready if t == "z" else proj_ready, 1)

            def spread(bb, m, k):
                i = 3 * m + k
                pm, pk = divmod(i - 2, 3)
                if pk < 2:
                    after(pe, scanned, 2 * SLOTS, bb, 2 * pm + pk)
                else:
                    after(pe, cdec_done, SLOTS, bb, pm)
                if isinstance(bb, int) and (bb, m, k) == (0, 0, 0):
                    pe.wait_ge(pr_rest, len(PR_ORDER))
                first = (0, P, HP)[k]
                MM(bc_bank[i % 2][:, :], sel[:, m, first:first + P], (pr_parts if k == 2 else da_parts)[:, bass.ds(bb * S, S)],
                   start=True, stop=True).then_inc(bc_ready, 1)

            def slot(b, n):
                q, r = divmod(n, R)
                real = not (isinstance(b, int) and b == NB)
                ssd = back(b, n, LAG_SSD)
                if isinstance(b, int) and (b, n) == (0, R):
                    pe.wait_ge(tap, NTAP // UNITS)
                if ssd is not None:
                    bb, m = ssd
                    mq, mr = divmod(m, R)
                    after(pe, silu_done, NCONV, bb, CONV_ORDER.index((mq, 2 + mr)))
                    misc_free(b, n, "xt")
                    for c in range(CH):
                        last = TR(misc_of("xt", n)[:, P * c:P * c + P], chan[:, chan_of(mq, 2 + mr), P * c:P * c + P], ident)
                    last.then_inc(xt_ready, 1)
                if real:
                    for t in PLAN[r]:
                        project(b, n, t, (b, n))
                st = back(b, n, LAG_STATE)
                if st is not None:
                    bb, m = st
                    after(pe, xw_done, 2 * SLOTS, bb, 2 * m + 1)
                    after(pe, bt_copied, UNITS, bb, m // R)
                    misc_free(b, n, "s")
                    for a in range(2):
                        half = slice(HP * a, HP * a + HP)
                        for c in range(CH - 1):
                            last = MM(misc_of("s", n)[half, NS * c:NS * c + NS], bt[:, c, half], xw[:, m % 2, c, half],
                                      start=True, stop=True)
                    last.then_inc(s_ready, 1)
                if back(b, n, LAG_OUT) is not None:
                    bb, m = back(b, n, LAG_OUT)
                    after(pe, normed, SLOTS, bb, m)
                    if m == 0:
                        after(pe, out_copied, 1, bb, -1)
                    last = MM(out_bank[:, :], w_out[:, m, :], gated[:, (m // R) % 2, m % R, :], start=(m == 0), stop=(m == SLOTS - 1))
                    last.then_inc(out_step, 1)
                if ssd is not None:
                    spread(*ssd, 2)
                yy = back(b, n, LAG_Y)
                if yy is not None:
                    bb, m = yy
                    mr = m % R
                    after(pe, m_done, SLOTS, bb, m)
                    after(pe, hbd_done, 2 * SLOTS, bb, 2 * m + 1)
                    after(pe, cdec_done, SLOTS, bb, m)
                    after(pe, skipped, SLOTS, bb, m - 1)
                    for c in range(CH):
                        tok = slice(P * c, P * c + P)
                        if c > 0:
                            MM(y_bank[:, tok], hbd[:, m % 2, c - 1, :], cdec[:, mr, tok], start=True, stop=False)
                        for a in range(2):
                            half = slice(HP * a, HP * a + HP)
                            last = MM(y_bank[half, tok], xdt[:, mr, P * c + HP * a:P * c + HP * a + HP], lm[:, mr, a, tok],
                                      start=(c == 0), stop=True)
                    last.then_inc(y_ready, 1)
                if r == 0 and back(b, n, LAG_VAR) is not None:
                    bb, m = back(b, n, LAG_VAR)
                    v = m // R
                    after(pe, ssum_step, 3 * UNITS, bb, 3 * v + 2)
                    misc_free(b, n, "var")
                    for c in range(CH):
                        last = MM(misc_of("var", n)[:, 2 * c:2 * c + 2], ssum[:, v % 2, P * c:P * c + P], blockones[:, :], start=True, stop=True)
                    last.then_inc(var_ready, 1)
                if r == 1 and back(b, n, LAG_M) is not None:
                    bb, m = back(b, n, LAG_M)
                    v = m // R
                    misc_free(b, n, "bt")
                    for c in range(CH):
                        last = TR(misc_of("bt", n)[:, P * c:P * c + P], chan[:, 0, P * c:P * c + P], ident)
                    last.then_inc(bt_ready, 1)
                if ssd is not None:
                    project(b, n, "z", ssd)
                if r == 0 and ssd is not None:
                    bb, m = ssd
                    v = m // R
                    after(pe, silu_done, NCONV, bb, CONV_ORDER.index((v, 1)))
                    for a in range(2):
                        half = slice(HP * a, HP * a + HP)
                        misc_free(b, n, "cb", a)
                        for c in range(CH):
                            tok = slice(P * c, P * c + P)
                            last = MM(misc_of("cb", n, a)[:, tok], chan[half, 0, tok], chan[half, chan_of(v, 1), tok],
                                      start=True, stop=True)
                        last.then_inc(cb_ready, 1)
                if r == 1 and back(b, n, LAG_FACTOR) is not None:
                    bb, m = back(b, n, LAG_FACTOR)
                    v = m // R
                    after(pe, rexp_done, UNITS, bb, v)
                    misc_free(b, n, "rbc")
                    for c in range(CH):
                        last = TR(misc_of("rbc", n)[:, P * c:P * c + P], rexp[:, 2 * c:2 * c + 2, :].rearrange("p a d -> p (a d)"), ident)
                    last.then_inc(rbc_ready, 1)
                if n == XN_SLOT and following(b) is not None:
                    pe.wait_ge(staged, b * 16 + 16)
                    misc_free(b, n, "xn")
                    transpose_xn(xn_stage, misc_of("xn", n))
                if n == XO_SLOT and back(b, n, SLOTS) is not None:
                    bb, _ = back(b, n, SLOTS)
                    after(pe, out_copied, 1, bb, 0)
                    misc_free(b, n, "xo")
                    for c in range(CH):
                        last = TR(misc_of("xo", n)[:, P * c:P * c + P], ocm[:, P * c:P * c + P], ident)
                    last.then_inc(xo_ready, 1)
                if back(b, n + 1, LAG_SSD) is not None:
                    for k in range(2):
                        spread(*back(b, n + 1, LAG_SSD), k)

            def step(i, par, k):
                if there(i, -2):
                    reach(pe, f_ntcopy, i, HT, -HT)
                    reach(pe, f_out, i, 1, -2)
                    for c in range(CH):
                        for t in range(HT):
                            last = MM(bank[5][:, P * c:P * c + P], fnt[:, t, P * c:P * c + P], w2t[:, P * t:P * t + P],
                                      start=(t == 0), stop=(t == HT - 1))
                    last.then_inc(f_mm2, 1)
                if there(i, 1):
                    reach(pe, f_tcopy, i, 1, 2)
                    for c in range(CH):
                        reach(pe, f_h, i, CH, c + 1)
                        MM(h_bank[c][:, :], fxt[:, P * c:P * c + P], w1t[:, :], start=True, stop=True).then_inc(f_mm1, 1)
                if there(i, -1):
                    for t in range(HT):
                        reach(pe, f_nrm, i, CH)
                        reach(pe, f_ntcopy, i, HT, t - 1 - HT)
                        for c in range(CH):
                            last = TR(nt_bank[t % 2][:, P * c:P * c + P], fge[:, 1 - par, c, P * t:P * t + P], ident)
                        last.then_inc(f_nt, 1)
                if there(i, 2):
                    reach(pe, f_xn, i, CH, 3 * CH)
                    reach(pe, f_tcopy, i, 1, 2)
                    for c in range(CH):
                        last = TR(bank[0][:, P * c:P * c + P], fxn[:, c, :], ident)
                    last.then_inc(f_t, 1)

            slot(0, 0)
            pe.wait_ge(da_split_done, 1)
            for i in range(NB):
                if i >= 2:
                    pe.wait_ge(da_copied, i - 1)
                for c in range(CH):
                    at = (CH * i + c) * 3 * H
                    last = TR(bank[6 + i % 2][0:96, 0:S // 2].bitcast(BF16)[:, P * c:P * c + P], da_split[:, at:at + 3 * H], ident_b[:, :])
                last.then_inc(da_t, 1)
            slot(0, 1)
            pe.wait_ge(da_copied, NB)
            for n in range(2, SLOTS):
                slot(0, n)
            with pe.Fori(1, NB - 1) as b:
                for n in range(SLOTS):
                    slot(b, n)
            for b in (NB - 1, NB):
                for n in range(SLOTS):
                    slot(b, n)
                    if (b, n) == (NB, SUM_SLOTS[1]):
                        pe.wait_ge(q_abs, 2)
                        pe.wait_ge(q_ones, 1)
                        MM(bank[1][:, 0:2], ones, qs[:, 0:2], start=True, stop=True).then_inc(q_tot, 1)
                    if (b, n) == (NB, QUANT_END):
                        for k in range(2):
                            pe.wait_ge(q_step, 9 + 6 * k)
                            for t in range(HT):
                                last = TR(bank[2 + k][:, P * t:P * t + P], qw[:, k, P * t:P * t + P], ident)
                            last.then_inc(q_t, 1)
                        pe.wait_ge(q_copied, 2)
                    early(step, b, n)

            ffn_steps(step, pe.Fori)


_INS = ["L0_attn_hidden_states", "L0_attn_norm_w", "L0_attn_in_proj_w", "L0_attn_conv_w", "L0_attn_conv_b",
        "L0_attn_dt_bias", "L0_attn_A_log", "L0_attn_D", "L0_attn_gate_norm_w", "L0_attn_out_proj_w",
        "L0_ffn_ln1_g", "L0_ffn_ln1_b", "L0_ffn_w1", "L0_ffn_b1", "L0_ffn_ln2_g", "L0_ffn_ln2_b", "L0_ffn_w2",
        "L0_ffn_b2"]


def kernel(**inputs):
    import concourse.bacc as _bacc
    from concourse.bass_utils import run_bass_kernel_spmd as _run

    nc = _bacc.Bacc("TRN2", target_bir_lowering=False, num_devices=1)
    arrays, args = {}, []
    for name in _INS:
        a = np.ascontiguousarray(inputs[name])
        arrays[f"in_{name}"] = a
        args.append(nc.dram_tensor(f"in_{name}", a.shape, mybir.dt.from_np(a.dtype), kind="ExternalInput").ap())
    out = nc.dram_tensor("out_tokens", (NB, S, DM), F32, kind="ExternalOutput").ap()
    build(nc, *args, out)
    r = _run(nc, [arrays], core_ids=[0])
    return r.results[0]["out_tokens"]
```
